# Optimizing a Trainium2 kernel written in Bass

```python
import numpy as np
import jax
import jax.numpy as jnp

def _softmax(x, axis=-1):
    return jax.nn.softmax(x, axis=axis)

def _gelu(x):
    return jax.nn.gelu(x, approximate=True)

def _silu(x):
    return jax.nn.silu(x)

def _sigmoid(x):
    return jax.nn.sigmoid(x)

def _layernorm(x, axis=-1, eps=1e-05):
    m = jnp.mean(x, axis=axis, keepdims=True)
    v = jnp.var(x, axis=axis, keepdims=True)
    return (x - m) / jnp.sqrt(v + eps)

def _scatter_add(tgt, idx, src, axis=0):
    return tgt.at[idx].add(src)

def _segment_sum(src, seg, n):
    return jax.ops.segment_sum(src, seg, n)
kernel_name = 'mk_seq_postln_d1_jaxref_r4_91a93c'

def setup_inputs(seed: int=0):
    np.random.seed(seed)
    _w = jnp.asarray

    def _L0_attn_setup():
        import jax, jax.numpy as jnp
        import numpy as np
        DIM = 256
        HEADS = 16
        HEAD_DIM = DIM // HEADS
        THRESH = 0.29514
        SHARP = 15.0
        LN_EPS = 1e-05
        NORM_EPS = 1e-12

        def _l2norm(t):
            n = jnp.sqrt(jnp.sum(t * t, axis=-1, keepdims=True))
            return t / jnp.maximum(n, NORM_EPS)
        key = jax.random.key(seed)
        ks = jax.random.split(key, 8)
        s = 1.0 / np.sqrt(DIM)
        sg = 1.0 / np.sqrt(HEAD_DIM)
        return {'x': jax.random.normal(ks[0], (2, 512, DIM), dtype=jnp.float32), 'Wq': jax.random.uniform(ks[1], (DIM, DIM), jnp.float32, -s, s), 'Wk': jax.random.uniform(ks[2], (DIM, DIM), jnp.float32, -s, s), 'Wv': jax.random.uniform(ks[3], (DIM, DIM), jnp.float32, -s, s), 'gq': jax.random.uniform(ks[4], (HEAD_DIM,), jnp.float32, -sg, sg), 'gk': jax.random.uniform(ks[5], (HEAD_DIM,), jnp.float32, -sg, sg), 'Wo': jax.random.uniform(ks[6], (DIM, DIM), jnp.float32, -s, s), 'bo': jax.random.uniform(ks[7], (DIM,), jnp.float32, -s, s), 'ln_w': jnp.ones((DIM,), jnp.float32), 'ln_b': jnp.zeros((DIM,), jnp.float32)}
    _L0_attn_in = _L0_attn_setup()

    def _L0_ffn_setup():
        import jax, jax.numpy as jnp
        import numpy as np
        LN_EPS = 1e-05
        NORM_EPS = 1e-12

        def _layernorm(x, gamma, beta):
            mu = x.mean(axis=-1, keepdims=True)
            var = ((x - mu) ** 2).mean(axis=-1, keepdims=True)
            return (x - mu) * jax.lax.rsqrt(var + LN_EPS) * gamma + beta

        def _l2norm(x, axis):
            n = jnp.sqrt((x ** 2).sum(axis=axis, keepdims=True))
            return x / jnp.maximum(n, NORM_EPS)
        key = jax.random.key(seed)
        ks = jax.random.split(key, 4)
        B, N, D, E, S, H = (64, 64, 256, 16, 16, 64)
        x = jax.random.normal(ks[0], (B, N, D), dtype=jnp.float32)
        mu = jax.random.normal(ks[1], (D, E, S), dtype=jnp.float32) / np.sqrt(D)
        w1 = jax.random.normal(ks[2], (E, D, H), dtype=jnp.float32) * np.sqrt(2.0 / D)
        w2 = jax.random.normal(ks[3], (E, H, D), dtype=jnp.float32) * np.sqrt(2.0 / (H + D))
        return {'x': x, 'ln_gamma': jnp.ones((D,), jnp.float32), 'ln_beta': jnp.zeros((D,), jnp.float32), 'mu': mu, 'scale': jnp.ones((1,), jnp.float32), 'w1': w1, 'b1': jnp.zeros((E, H), jnp.float32), 'w2': w2, 'b2': jnp.zeros((E, D), jnp.float32)}
    _L0_ffn_in = _L0_ffn_setup()
    _d = {'L0_attn_x': _L0_attn_in['x'], 'L0_attn_Wq': _L0_attn_in['Wq'], 'L0_attn_Wk': _L0_attn_in['Wk'], 'L0_attn_Wv': _L0_attn_in['Wv'], 'L0_attn_gq': _L0_attn_in['gq'], 'L0_attn_gk': _L0_attn_in['gk'], 'L0_attn_Wo': _L0_attn_in['Wo'], 'L0_attn_bo': _L0_attn_in['bo'], 'L0_attn_ln_w': _L0_attn_in['ln_w'], 'L0_attn_ln_b': _L0_attn_in['ln_b'], 'L0_ffn_ln_gamma': _L0_ffn_in['ln_gamma'], 'L0_ffn_ln_beta': _L0_ffn_in['ln_beta'], 'L0_ffn_mu': _L0_ffn_in['mu'], 'L0_ffn_scale': _L0_ffn_in['scale'], 'L0_ffn_w1': _L0_ffn_in['w1'], 'L0_ffn_b1': _L0_ffn_in['b1'], 'L0_ffn_w2': _L0_ffn_in['w2'], 'L0_ffn_b2': _L0_ffn_in['b2']}
    _x0 = _d['L0_attn_x']
    _d['L0_attn_x'] = jax.random.normal(jax.random.fold_in(jax.random.key(seed), 1), (16, 512, 256), dtype=_x0.dtype)
    del _x0
    return _d

def reference(L0_attn_x, L0_attn_Wq, L0_attn_Wk, L0_attn_Wv, L0_attn_gq, L0_attn_gk, L0_attn_Wo, L0_attn_bo, L0_attn_ln_w, L0_attn_ln_b, L0_ffn_ln_gamma, L0_ffn_ln_beta, L0_ffn_mu, L0_ffn_scale, L0_ffn_w1, L0_ffn_b1, L0_ffn_w2, L0_ffn_b2):

    def _L0_attn_ref(x, Wq, Wk, Wv, gq, gk, Wo, bo, ln_w, ln_b):
        import jax, jax.numpy as jnp
        import numpy as np
        DIM = 256
        HEADS = 16
        HEAD_DIM = DIM // HEADS
        THRESH = 0.29514
        SHARP = 15.0
        LN_EPS = 1e-05
        NORM_EPS = 1e-12

        def _l2norm(t):
            n = jnp.sqrt(jnp.sum(t * t, axis=-1, keepdims=True))
            return t / jnp.maximum(n, NORM_EPS)
        B, T, D = x.shape
        mu = jnp.mean(x, axis=-1, keepdims=True)
        var = jnp.mean((x - mu) ** 2, axis=-1, keepdims=True)
        x_norm = (x - mu) / jnp.sqrt(var + LN_EPS) * ln_w + ln_b

        def split_heads(t):
            return t.reshape(B, T, HEADS, HEAD_DIM).transpose(0, 2, 1, 3)
        q = _l2norm(split_heads(x_norm @ Wq))
        k = _l2norm(split_heads(x_norm @ Wk))
        v = split_heads(x @ Wv)
        align = jnp.einsum('bhtd,bhsd->bhts', q, k)
        resonance = jax.nn.sigmoid((align - THRESH) * SHARP)
        gate_q = jnp.einsum('bhtd,d->bht', q, gq)
        gate_k = jnp.einsum('bhsd,d->bhs', k, gk)
        modulation = resonance * gate_q[..., :, None] * gate_k[..., None, :]
        collapse = jnp.einsum('bhts,bhsd->bhtd', modulation, v)
        collapse = collapse.transpose(0, 2, 1, 3).reshape(B, T, D)
        return collapse @ Wo + bo

    def _L0_ffn_ref(x, ln_gamma, ln_beta, mu, scale, w1, b1, w2, b2):
        import jax, jax.numpy as jnp
        import numpy as np
        LN_EPS = 1e-05
        NORM_EPS = 1e-12

        def _layernorm(x, gamma, beta):
            mu = x.mean(axis=-1, keepdims=True)
            var = ((x - mu) ** 2).mean(axis=-1, keepdims=True)
            return (x - mu) * jax.lax.rsqrt(var + LN_EPS) * gamma + beta

        def _l2norm(x, axis):
            n = jnp.sqrt((x ** 2).sum(axis=axis, keepdims=True))
            return x / jnp.maximum(n, NORM_EPS)
        B, N, D = x.shape
        _, E, S = mu.shape
        xn = _layernorm(x, ln_gamma, ln_beta)
        x_unit = _l2norm(xn, axis=-1)
        mu_unit = _l2norm(mu, axis=0)
        logits = jnp.einsum('bnd,des->bnes', x_unit * scale, mu_unit)
        dispatch = jax.nn.softmax(logits, axis=1)
        combine = jax.nn.softmax(logits.reshape(B, N, E * S), axis=-1).reshape(B, N, E, S)
        slot_in = jnp.einsum('bnd,bnes->besd', xn, dispatch)
        h = jax.nn.gelu(jnp.einsum('besd,edh->besh', slot_in, w1) + b1[None, :, None, :], approximate=False)
        slot_out = jnp.einsum('besh,ehd->besd', h, w2) + b2[None, :, None, :]
        out = jnp.einsum('besd,bnes->bnd', slot_out, combine)
        return out
    x = L0_attn_x
    x = _layernorm(x + _L0_attn_ref(x, L0_attn_Wq, L0_attn_Wk, L0_attn_Wv, L0_attn_gq, L0_attn_gk, L0_attn_Wo, L0_attn_bo, L0_attn_ln_w, L0_attn_ln_b), axis=-1)
    x = _layernorm(x + _L0_ffn_ref(x, L0_ffn_ln_gamma, L0_ffn_ln_beta, L0_ffn_mu, L0_ffn_scale, L0_ffn_w1, L0_ffn_b1, L0_ffn_w2, L0_ffn_b2), axis=-1)
    return x

_drawn_inputs = setup_inputs


def setup_inputs(seed=0):
    import zlib

    import numpy as np

    out = dict(_drawn_inputs(seed))
    spreads = {'L0_attn_ln_w': (1.0, 0.589),
     'L0_attn_ln_b': (0.0, 0.53),
     'L0_ffn_ln_gamma': (1.0, 0.6),
     'L0_ffn_ln_beta': (0.0, 0.717),
     'L0_ffn_b1': (0.0, 0.8),
     'L0_ffn_b2': (0.0, 0.318)}
    factors = {'L0_ffn_mu': 8.0, 'L0_ffn_w1': 4.144, 'L0_ffn_w2': 3.558}
    for name, (base, spread) in spreads.items():
        noise = np.random.default_rng([zlib.crc32(name.encode()), seed]).standard_normal(out[name].shape)
        drawn = base * np.exp(spread * noise) if base else spread * noise
        out[name] = jnp.asarray(drawn.astype(out[name].dtype))
    for name, factor in factors.items():
        out[name] = (out[name] * factor).astype(out[name].dtype)
    return out
```

```python
from contextlib import ExitStack

import concourse.bass as bass
from concourse import mybir

F32 = mybir.dt.float32
F16 = mybir.dt.float16
ALU = mybir.AluOpType
ACT = mybir.ActivationFunctionType
AX_X = mybir.AxisListType.X

P = 128
THRESH = 0.29514
SHARP = 15.0
LN_EPS = 1e-5
NORM_EPS = 1e-12
GATE_SCALE = 16.0

LOOP_FROM, LOOP_SLOTS, LOOP_TIMES = 16, 8, 4


def seq_block_kernel(nc, x, Wq, Wk, Wv, gq, gk, Wo, bo, ln_w, ln_b, gamma, beta, mu, scale,
                     w1, b1, w2, b2, consts, out):
    B, T, D = x.shape
    HD = gq.shape[0]
    H = D // HD
    E, S = mu.shape[1], mu.shape[2]
    ES = E * S
    HF = w1.shape[2]
    KC = D // P
    TC = T // P
    NCH = B * TC
    PAIRS = H // 2
    GROUPS = 4
    QUADS = 4
    assert (D, HD, E, S, HF, TC) == (256, 16, 16, 16, 64, 4)

    x_rows = x.rearrange("b t d -> (b t) d")
    out_rows = out.rearrange("b t d -> (b t) d")
    x1_dram = nc.dram_tensor("x1_scratch", (B * T, D), F32, kind="Internal").ap()
    comb_dram = nc.dram_tensor("combine_scratch", (B, P, KC, T), F32, kind="Internal").ap()
    slot_dram = nc.dram_tensor("slot_out_scratch", (B, ES, D), F32, kind="Internal").ap()

    with ExitStack() as ctx:
        def sb(name, shape, dt=F32):
            return ctx.enter_context(nc.sbuf_tensor(name, shape, dt))

        def ps(name, shape, dt=F32):
            return ctx.enter_context(nc.psum_tensor(name, shape, dt))

        def sem(name):
            return ctx.enter_context(nc.semaphore(name))

        ident = sb("ident", [P, P])
        ident16 = sb("ident16", [P, P], F16)
        masks = sb("masks", [P, 2 + 2 * HD])
        minus_half = sb("minus_half", [P, 2 * H])
        wqk = sb("wqk", [P, KC, 2 * D])
        wv = sb("wv", [P, KC, D])
        wo = sb("wo", [P, KC, D])
        mu_unit = sb("mu_unit", [P, KC, ES])
        qk_bias = sb("qk_bias", [P, 2 * D])
        gk_all = sb("gk_all", [P, D])
        bo_all = sb("bo_all", [P, D])
        gamma_all = sb("gamma_all", [P, D])
        beta_all = sb("beta_all", [P, D])
        lnw_col = sb("lnw_col", [P, KC])
        lnb_col = sb("lnb_col", [P, KC])
        scale_col = sb("scale_col", [P, 1])
        gq_col = sb("gq_col", [P, 4])
        gq_hi16 = sb("gq_hi16", [P, 1], F16)
        gate_w = sb("gate_w", [P, 2 * HD], F16)
        wait_holder = sb("wait_holder", [P, 1])
        mu_norm = sb("mu_norm", [P, 2 * KC])

        xs = sb("xs", [P, 4, D])
        bn = sb("bn", [P, 2, 6])
        mv = sb("mv", [P, 4, 2])
        var_eps = sb("var_eps", [P, 4])
        rstd = sb("rstd", [P, 4])
        z = sb("z", [P, 2, D])
        xzT = sb("xzT", [P, 2, 4, P])
        qk = sb("qk", [P, 4, 2 * D])
        v_raw = sb("v_raw", [P, 4, D])
        sqg = sb("sqg", [P, 3 * D])
        sums = sb("sums", [P, 2, 3 * H])
        rn = sb("rn", [P, 2, 2 * H])
        qn = sb("qn", [P, 2 * D])
        hl = sb("hl", [P, 2, 2 * H, 4, HD], F16)
        gate_k = sb("gate_k", [P, 2, H])
        stack = sb("stack", [P, 2, 2, PAIRS, T], F16)
        vpad = sb("vpad", [P, 2, TC, PAIRS, 3 * HD])
        res = sb("res", [P, 4, QUADS, T])
        ones = res[:, 0, 0, 0:P]
        gate_q = sb("gate_q", [P, 2, T])
        coll = sb("coll", [P, 2, 2, T])
        xr = sb("xr", [P, 4, D])
        y = sb("y", [P, 2, D])
        ybn = sb("ybn", [P, 2, 6])
        ymv = sb("ymv", [P, 2, 2])
        yvar = sb("yvar", [P, 2])
        yrstd = sb("yrstd", [P, 2])
        v1 = sb("v1", [P, 2, 2])
        r1 = sb("r1", [P, 2])
        x1 = sb("x1", [P, 2, D])
        xg = sb("xg", [P, D])
        xn = sb("xn", [P, 2, TC, D])
        xss = sb("xss", [P, 2, 2])
        xrn = sb("xrn", [P, 2])
        xnT = sb("xnT", [P, 2, KC, P])
        logit = sb("logit", [P, 2, TC, ES])
        rmax = sb("rmax", [P, 2, TC, 2])
        csum = sb("csum", [P, 2, TC])
        logitT = sb("logitT", [P, 2, KC, T])
        cmax = sb("cmax", [P, KC])
        esum = sb("esum", [P, 2, KC])
        disp = sb("disp", [P, TC, ES])
        combT = sb("combT", [P, 2, 2 * ES])
        slotT = sb("slotT", [P, KC, E, B, S])
        crec = sb("crec", [P, NCH])

        score_ps = [ps(f"score{t}", [P, 2, T]) for t in range(2)]
        coll_ps = ps("coll_ps", [P, T])
        f0 = ps("f0", [P, 512])
        f1 = ps("f1", [P, 512])
        b0 = ps("b0", [P, 512])
        f0h, f1h = f0[:, :].bitcast(F16), f1[:, :].bitcast(F16)

        const_loaded, weight_loaded = sem("const_loaded"), sem("weight_loaded")
        setup_v, setup_p, setup_t = sem("setup_v"), sem("setup_p"), sem("setup_t")
        x_loaded = [sem(f"x_loaded{k}") for k in range(4)]
        xr_loaded = [sem(f"xr_loaded{k}") for k in range(4)]
        x1_stored = [sem(f"x1_stored{k}") for k in range(2)]
        comb_stored = [sem(f"comb_stored{k}") for k in range(2)]
        stats, z_ready, rstd_ready = sem("stats"), sem("z_ready"), sem("rstd_ready")
        xzT_ready, xzT_copied = sem("xzT_ready"), sem("xzT_copied")
        qk_ready, qk_copied = sem("qk_ready"), sem("qk_copied")
        v_ready, v_copied = sem("v_ready"), sem("v_copied")
        sqg_ready, sums_ready, rn_ready = sem("sqg_ready"), sem("sums_ready"), sem("rn_ready")
        norm_step, hl_ready, v_gated = sem("norm_step"), sem("hl_ready"), sem("v_gated")
        stk_ready, stk_copied = sem("stk_ready"), sem("stk_copied")
        sc_ready, sig_done, pv_done = sem("sc_ready"), sem("sig_done"), sem("pv_done")
        gate_ready, gate_copied, coll_done = sem("gate_ready"), sem("gate_copied"), sem("coll_done")
        wo_ready, xb_ready = sem("wo_ready"), sem("xb_ready")
        y_step, yrstd_ready = sem("y_step"), sem("yrstd_ready")
        x1_ready, r1_ready = sem("x1_ready"), sem("r1_ready")
        xn_step, xrn_ready = sem("xn_step"), sem("xrn_ready")
        xnT_ready, xnT_copied = sem("xnT_ready"), sem("xnT_copied")
        log_ready, log_step = sem("log_ready"), sem("log_step")
        logT_ready, logT_copied = sem("logT_ready"), sem("logT_copied")
        soft_max, soft_exp, soft_post = sem("soft_max"), sem("soft_exp"), sem("soft_post")
        disp_ready, disp_copied = sem("disp_ready"), sem("disp_copied")
        slot_ready, slot_copied = sem("slot_ready"), sem("slot_copied")
        combT_ready, combT_copied = sem("combT_ready"), sem("combT_copied")

        gate_setup, mu_ready, hi_ready = sem("gate_setup"), sem("mu_ready"), sem("hi_ready")

        def times(i, base, per_body):
            return base if i is None else i * per_body + base

        def per_slot(i, base, n=1):
            return times(i, base, n * LOOP_SLOTS)

        def per_batch(i, base, n=1):
            return times(i, base, n * LOOP_SLOTS // TC)

        def slots(eng, slot, first, last):
            loop_end = LOOP_FROM + LOOP_SLOTS * LOOP_TIMES
            for s in range(first, LOOP_FROM):
                slot(None, s)
            with eng.Fori(0, LOOP_TIMES) as i:
                for s in range(LOOP_FROM, LOOP_FROM + LOOP_SLOTS):
                    slot(i, s)
            for s in range(loop_end, last + 1):
                slot(None, s)

        def chunk_ok(c):
            return 0 <= c < NCH

        def batch_ok(b):
            return 0 <= b < B

        FIRST, LAST = -10, NCH + 10

        def hold_wait():
            nc.vector.memset(wait_holder[:], 0.0)

        def heads(ap):
            return ap.rearrange("p (h d) -> p h d", d=HD)

        def over(ap, n):
            return ap.unsqueeze(len(ap.shape)).broadcast_to(list(ap.shape) + [n])

        WEIGHTS = 12 + P // HD
        with nc.Block() as block:

            @block.sync
            def _(sp):
                c_eye, c_masks = consts[:, 0:P], consts[:, P:P + 2 + 2 * HD]
                sp.dma_start(ident[:], c_eye).then_inc(const_loaded, 16)
                sp.dma_start(masks[:], c_masks).then_inc(const_loaded, 16)

                def load_x(i, c):
                    k = c % 4
                    if c >= 4:
                        sp.wait_ge(xzT_ready, per_slot(i, c - 3))
                    sp.dma_start(xs[:, k, :], x_rows[bass.ds(per_slot(i, c * P, P), P), :]).then_inc(x_loaded[k], 16)

                for c in range(4):
                    load_x(None, c)

                def weight(dst, src):
                    sp.dma_start(dst, src, allow_slow_non_contiguous=True).then_inc(weight_loaded, 16)

                weight(wqk[:, :, 0:D], Wq.rearrange("(k p) n -> p k n", p=P))
                weight(wqk[:, :, D:2 * D], Wk.rearrange("(k p) n -> p k n", p=P))
                weight(lnw_col[:], ln_w.rearrange("(k p) -> p k", p=P))
                weight(lnb_col[:], ln_b.rearrange("(k p) -> p k", p=P))
                weight(wv[:], Wv.rearrange("(k p) n -> p k n", p=P))
                weight(gk_all[:, :].rearrange("p (h d) -> p h d", d=HD),
                       gk.unsqueeze(0).unsqueeze(0).broadcast_to([P, H, HD]))
                for n in range(P // HD):
                    weight(gq_col[n * HD:(n + 1) * HD, 0:1], gq.unsqueeze(1))
                weight(wo[:], Wo.rearrange("(k p) n -> p k n", p=P))
                weight(bo_all[:], bo.unsqueeze(0).broadcast_to([P, D]))
                weight(gamma_all[:], gamma.unsqueeze(0).broadcast_to([P, D]))
                weight(beta_all[:], beta.unsqueeze(0).broadcast_to([P, D]))
                weight(scale_col[:], scale.unsqueeze(0).broadcast_to([P, 1]))
                weight(mu_unit[:], mu.rearrange("(k p) e s -> p k (e s)", p=P))

                def slot(i, s):
                    j = s % TC
                    if chunk_ok(s + 10) and s + 10 >= 4:
                        load_x(i, s + 10)
                    c = s - 2
                    if chunk_ok(c):
                        if c >= 4:
                            sp.wait_ge(y_step, per_slot(i, 4 * (c - 4) + 1, 4))
                        sp.dma_start(xr[:, c % 4, :], x_rows[bass.ds(per_slot(i, c * P, P), P), :])\
                            .then_inc(xr_loaded[c % 4], 16)
                    c = s - 6
                    if chunk_ok(c):
                        sp.wait_ge(x1_ready, per_slot(i, 3 * c + 1, 3))
                        sp.dma_start(x1_dram[bass.ds(per_slot(i, c * P, P), P), :], x1[:, c % 2, :])\
                            .then_inc(x1_stored[c % 2], 16)
                    half, b = j - 1, s // TC - 3
                    if j in (1, 2) and batch_ok(b):
                        sp.wait_ge(combT_copied, per_batch(i, 2 * b + half + 1, 2))
                        dst = comb_dram[bass.ds(per_batch(i, b), 1), :, :, half * 2 * P:(half + 1) * 2 * P]
                        sp.dma_start(dst.rearrange("b p k n -> (b p) k n"),
                                     combT[:, half, :].rearrange("p (k n) -> p k n", k=KC))\
                            .then_inc(comb_stored[half], 16)

                slots(sp, slot, FIRST, LAST)
                for k in range(2):
                    sp.wait_ge(x1_stored[k], 16 * NCH // 2)
                for k in range(2):
                    sp.wait_ge(comb_stored[k], 16 * B)

            @block.gpsimd
            def _(pool):
                nc.gpsimd.memset(minus_half[:], -0.5).then_inc(setup_p, 1)
                nc.gpsimd.memset(vpad[:], 0.0).then_inc(setup_p, 1)
                pool.wait_ge(setup_p, 2)

                def power(dst, src, n):
                    return nc.gpsimd.tensor_tensor(dst, src, minus_half[:, 0:n], ALU.pow)

                def slot(i, s):
                    c = s - 5
                    if chunk_ok(c):
                        pool.wait_ge(y_step, per_slot(i, 4 * c + 4, 4))
                        power(yrstd[:, c % 2:c % 2 + 1], yvar[:, c % 2:c % 2 + 1], 1).then_inc(yrstd_ready, 1)
                    c = s + 8
                    if chunk_ok(c):
                        pool.wait_ge(stats, per_slot(i, 3 * c + 3, 3))
                        power(rstd[:, c % 4:c % 4 + 1], var_eps[:, c % 4:c % 4 + 1], 1).then_inc(rstd_ready, 1)
                    if s == -5:
                        pool.wait_ge(setup_v, 8)
                        power(mu_norm[:, KC:2 * KC], mu_norm[:, 0:KC], KC).then_inc(setup_p, 1)
                    c = s + 6
                    if chunk_ok(c):
                        pool.wait_ge(qk_copied, per_slot(i, c + 1))
                        if c == 0:
                            pool.wait_ge(weight_loaded, 16 * WEIGHTS)
                        if c >= 1:
                            pool.wait_ge(sums_ready, per_slot(i, 2 * (c - 1) + 1, 2))
                        nc.gpsimd.tensor_tensor(sqg[:, 0:2 * D], qk[:, c % 4, :], qk[:, c % 4, :], ALU.mult)\
                            .then_inc(sqg_ready, 1)
                        nc.gpsimd.tensor_tensor(sqg[:, 2 * D:3 * D], qk[:, c % 4, D:2 * D], gk_all[:], ALU.mult)\
                            .then_inc(sqg_ready, 1)
                    c = s - 5
                    if chunk_ok(c):
                        pool.wait_ge(x1_ready, per_slot(i, 3 * c + 3, 3))
                        power(r1[:, c % 2:c % 2 + 1], v1[:, c % 2, 1:2], 1).then_inc(r1_ready, 1)
                    c = s + 6
                    if chunk_ok(c):
                        pool.wait_ge(sums_ready, per_slot(i, 2 * c + 2, 2))
                        if c >= 2:
                            pool.wait_ge(norm_step, per_slot(i, 2 * (c - 2) + 2, 2))
                        power(rn[:, c % 2, :], sums[:, c % 2, 0:2 * H], 2 * H).then_inc(rn_ready, 1)
                    c = s - 3
                    if chunk_ok(c):
                        pool.wait_ge(xr_loaded[c % 4], per_batch(i, 16 * (c // 4 + 1), 16))
                        nc.gpsimd.tensor_tensor(xr[:, c % 4, :], xr[:, c % 4, :], bo_all[:], ALU.add)\
                            .then_inc(xb_ready, 1)
                    c = s - 5
                    if chunk_ok(c):
                        pool.wait_ge(xn_step, per_slot(i, 4 * c + 4, 4))
                        if c >= 2:
                            pool.wait_ge(log_step, per_slot(i, 3 * (c - 2) + 3, 3))
                        power(xrn[:, c % 2:c % 2 + 1], xss[:, c % 2, 1:2], 1).then_inc(xrn_ready, 1)

                slots(pool, slot, FIRST, LAST)

            @block.scalar
            def _(act):
                def sigmoid(i, s, k):
                    u = 4 * s + k
                    for t in range(2):
                        act.wait_ge(sc_ready, per_slot(i, 2 * u + t + 1, 8))
                        if t == 0 and u >= 4:
                            act.wait_ge(pv_done, per_slot(i, u - 3, 4))
                        nc.scalar.activation(res[:, k, 2 * t:2 * t + 2, :], score_ps[t][:, :, :], ACT.Sigmoid,
                                             bias=-THRESH * SHARP, scale=SHARP).then_inc(sig_done, 1)

                def slot(i, s):
                    j = s % TC
                    attn = chunk_ok(s)
                    if attn:
                        sigmoid(i, s, 0)
                    b = s // TC - 3
                    if j in (1, 2) and batch_ok(b):
                        half = j - 1
                        act.wait_ge(combT_ready, per_batch(i, 2 * b + half + 1, 2))
                        if b >= 1:
                            act.wait_ge(comb_stored[half], per_batch(i, 16 * b, 16))
                        nc.scalar.activation(combT[:, half, :], b0[:, :], ACT.Copy).then_inc(combT_copied, 1)
                    if j == 0 and batch_ok(b):
                        act.wait_ge(disp_ready, per_batch(i, 2 * b + 2, 2))
                        nc.scalar.activation(disp[:, 2:4, :], b0[:, :].rearrange("p (t n) -> p t n", t=2), ACT.Copy)\
                            .then_inc(disp_copied, 1)
                    if attn:
                        sigmoid(i, s, 1)
                    c = s + 7
                    if chunk_ok(c):
                        act.wait_ge(xzT_ready, per_slot(i, c + 1))
                        if c >= 2:
                            act.wait_ge(v_ready, per_slot(i, c - 1))
                        nc.scalar.activation(xzT[:, c % 2, :, :], f0[:, :].rearrange("p (k n) -> p k n", n=P), ACT.Copy)\
                            .then_inc(xzT_copied, 1)
                    b = s // TC
                    if attn and j in (0, 2):
                        half = j // 2
                        act.wait_ge(gate_ready, per_batch(i, 2 * b + half + 1, 2))
                        if b >= 1:
                            act.wait_ge(coll_done, per_batch(i, 2 * (b - 1) + half + 1, 2))
                        nc.scalar.activation(gate_q[:, half, :], f1[:, :], ACT.Copy, scale=1.0 / GATE_SCALE)\
                            .then_inc(gate_copied, 1)
                    b = s // TC - 3
                    if batch_ok(b) and j == 1:
                        act.wait_ge(slot_ready, per_batch(i, b + 1))
                        nc.scalar.activation(slotT[:, :, :, bass.ds(per_batch(i, b), 1), :].rearrange("p k e b s -> p k e (b s)"),
                                             f1[:, :].rearrange("p (k e s) -> p k e s", k=KC, s=S), ACT.Copy)\
                            .then_inc(slot_copied, 1)
                    b = s // TC - 2
                    if batch_ok(b) and j == 3:
                        act.wait_ge(disp_ready, per_batch(i, 2 * b + 1, 2))
                        if b >= 1:
                            act.wait_ge(slot_ready, per_batch(i, b))
                        nc.scalar.activation(disp[:, 0:2, :], f1[:, :].rearrange("p (t n) -> p t n", t=2), ACT.Copy)\
                            .then_inc(disp_copied, 1)
                    c = s - 6
                    if chunk_ok(c):
                        act.wait_ge(xnT_ready, per_slot(i, c + 1))
                        if c >= 1:
                            act.wait_ge(logT_ready, per_slot(i, c))
                        if c >= 2:
                            act.wait_ge(log_ready, per_slot(i, c - 1))
                        nc.scalar.activation(xnT[:, c % 2, :, :], b0[:, 0:KC * P].rearrange("p (k n) -> p k n", n=P), ACT.Copy)\
                            .then_inc(xnT_copied, 1)
                    c = s - 7
                    if chunk_ok(c):
                        b, t = c // TC, c % TC
                        act.wait_ge(logT_ready, per_slot(i, c + 1))
                        if b >= 2 and t == 0:
                            act.wait_ge(disp_ready, per_batch(i, 2 * (b - 1), 2))
                        nc.scalar.activation(logitT[:, b % 2, :, t * P:(t + 1) * P],
                                             b0[:, KC * P:2 * KC * P].rearrange("p (k n) -> p k n", n=P), ACT.Copy)\
                            .then_inc(logT_copied, 1)
                    if attn:
                        sigmoid(i, s, 2)
                        sigmoid(i, s, 3)
                    b = s // TC - 2
                    if batch_ok(b) and j == 2:
                        act.wait_ge(log_step, per_batch(i, 3 * TC * (b + 1), 3 * TC))
                        if b >= 2:
                            act.wait_ge(soft_post, per_batch(i, 4 * (b - 1), 4))
                        for t in range(TC):
                            nc.scalar.activation(logit[:, b % 2, t, :], logit[:, b % 2, t, :], ACT.Exp,
                                                 bias=rmax[:, b % 2, t, 1:2], accum_out=csum[:, b % 2, t:t + 1]).then_inc(soft_exp, 1)
                        act.wait_ge(soft_max, per_batch(i, 2 * b + 2, 2))
                        for k in range(KC):
                            nc.scalar.activation(logitT[:, b % 2, k, :], logitT[:, b % 2, k, :], ACT.Exp,
                                                 bias=cmax[:, k:k + 1], accum_out=esum[:, b % 2, k:k + 1]).then_inc(soft_exp, 1)
                    c = s + 7
                    if chunk_ok(c):
                        act.wait_ge(v_ready, per_slot(i, c + 1))
                        if c >= 4:
                            act.wait_ge(v_gated, per_slot(i, c - 3))
                        nc.scalar.activation(v_raw[:, c % 4, :], f0[:, 0:D], ACT.Copy).then_inc(v_copied, 1)

                slots(act, slot, FIRST, LAST)

            @block.tensor
            def _(pe):
                def setup():
                    pe.wait_ge(setup_v, 3)
                    for k in range(KC):
                        last = nc.tensor.matmul(f1[:, :], xzT[:, 0, k, :], wqk[:, k, :], start=(k == 0), stop=(k == KC - 1))
                    last.then_inc(setup_t, 1)

                def setup_mu():
                    pe.wait_ge(setup_v, 7)
                    for m in range(KC):
                        for k in range(KC):
                            last = nc.tensor.matmul(b0[:, m:m + 1], logit[:, 0, k, m * P:(m + 1) * P], ones[:, 0:1],
                                                    start=(k == 0), stop=(k == KC - 1))
                    last.then_inc(setup_t, 1)

                def setup_mu_rows():
                    pe.wait_ge(setup_v, 10)
                    for m in range(KC):
                        last = nc.tensor.matmul(b0[:, m * P:(m + 1) * P], ones, disp[:, m, 0:P], start=True, stop=True)
                    last.then_inc(setup_t, 1)

                def scores(i, s, k):
                    u = 4 * s + k
                    b, j = s // TC, s % TC
                    half, odd = j // 2, j % 2
                    rows = slice(64 * odd, 64 * odd + 64)
                    if j == 0 and k == 0:
                        pe.wait_ge(stk_copied, per_slot(i, 2 * TC * (b + 1), 2))
                    for t in range(2):
                        if 2 * u + t >= 2:
                            pe.wait_ge(sig_done, per_slot(i, 2 * u + t - 1, 8))
                        for q in (2 * t, 2 * t + 1):
                            pair = 4 * half + q
                            last = nc.tensor.matmul(score_ps[t][:, q % 2, :], stack[rows, b % 2, 1, pair, k * P:(k + 1) * P],
                                                    stack[rows, b % 2, 0, pair, :], start=True, stop=True,
                                                    tile_position=(64 * odd, 0))
                        last.then_inc(sc_ready, 1)

                def weighted_sum(i, s, k):
                    u = 4 * s + k
                    b, j = s // TC, s % TC
                    half, odd = j // 2, j % 2
                    if j == 0 and k == 0:
                        pe.wait_ge(v_gated, per_slot(i, TC * (b + 1)))
                    if odd == 0 and k == 0 and 2 * b + half >= 1:
                        pe.wait_ge(coll_done, per_batch(i, 2 * b + half, 2))
                    pe.wait_ge(sig_done, per_slot(i, 2 * u + 2, 8))
                    for q in range(QUADS):
                        pair = 4 * half + q
                        last = nc.tensor.matmul(coll_ps[32 * q:32 * q + 32, :],
                                                vpad[:, b % 2, k, pair, HD * odd:HD * odd + 2 * HD], res[:, k, q, :],
                                                start=(odd == 0 and k == 0), stop=(odd == 1 and k == TC - 1),
                                                tile_position=(0, 32 * q))
                    last.then_inc(pv_done, 1)

                def stacks(i, c):
                    pe.wait_ge(hl_ready, per_slot(i, 3 * c + 3, 3))
                    for side, bank in ((0, f0h), (1, f1h)):
                        if side == 0 and c + 2 < NCH:
                            pe.wait_ge(v_copied, per_slot(i, c + 3))
                        if side == 1 and c + 2 < NCH:
                            pe.wait_ge(qk_copied, per_slot(i, c + 3))
                        for pair in range(PAIRS):
                            parts = hl[:, c % 2, side * H + 2 * pair:side * H + 2 * pair + 2, :, :].rearrange("p h a d -> p (h a d)")
                            last = nc.tensor.transpose(bank[:, pair * P:(pair + 1) * P], parts, ident16[:])
                        last.then_inc(stk_ready, 1)

                def transposes(i, c):
                    pe.wait_ge(z_ready, per_slot(i, c + 1))
                    if c == 0:
                        pe.wait_ge(const_loaded, 32)
                    if chunk_ok(c - 3):
                        pe.wait_ge(stk_copied, per_slot(i, 2 * (c - 3) + 1, 2))
                    elif c >= 1:
                        pe.wait_ge(v_copied, per_slot(i, c))
                    for n, src in enumerate((z[:, c % 2, 0:P], z[:, c % 2, P:2 * P], xs[:, c % 4, 0:P], xs[:, c % 4, P:2 * P])):
                        last = nc.tensor.transpose(f0[:, n * P:(n + 1) * P], src, ident[:])
                    last.then_inc(xzT_ready, 1)

                def project_qk(i, s, c):
                    pe.wait_ge(xzT_copied, per_slot(i, c + 1))
                    b, j = s // TC, s % TC
                    if c == 0:
                        pe.wait_ge(setup_v, 6)
                    if chunk_ok(s + 4):
                        pe.wait_ge(stk_copied, per_slot(i, 2 * (s + 4) + 2, 2))
                    elif c >= 1:
                        pe.wait_ge(qk_copied, per_slot(i, c))
                    if chunk_ok(s) and j in (0, 2):
                        pe.wait_ge(gate_copied, per_batch(i, 2 * b + j // 2 + 1, 2))
                    if j == 1 and batch_ok(b - 3):
                        pe.wait_ge(slot_copied, per_batch(i, b - 3 + 1))
                    if j == 3 and batch_ok(b - 2):
                        pe.wait_ge(disp_copied, per_batch(i, 2 * (b - 2) + 1, 2))
                    for k in range(KC):
                        last = nc.tensor.matmul(f1[:, :], xzT[:, c % 2, k, :], wqk[:, k, :], start=(k == 0), stop=(k == KC - 1))
                    last.then_inc(qk_ready, 1)

                def project_v(i, c):
                    for k in range(KC):
                        last = nc.tensor.matmul(f0[:, 0:D], xzT[:, c % 2, KC + k, :], wv[:, k, :], start=(k == 0), stop=(k == KC - 1))
                    last.then_inc(v_ready, 1)

                def gates(i, s):
                    b, half = s // TC, s % TC // 2
                    if half == 0:
                        pe.wait_ge(stk_copied, per_slot(i, 2 * TC * (b + 1), 2))
                    if chunk_ok(s + 4):
                        pe.wait_ge(stk_copied, per_slot(i, 2 * (s + 4) + 2, 2))
                    elif half == 1:
                        pe.wait_ge(gate_copied, per_batch(i, 2 * b + 1, 2))
                    for q in range(QUADS):
                        last = nc.tensor.matmul(f1[32 * q:32 * q + 32, :], gate_w[:], stack[:, b % 2, 0, 4 * half + q, :],
                                                start=True, stop=True, tile_position=(0, 32 * q))
                    last.then_inc(gate_ready, 1)

                def output_projection(i, c):
                    b, j = c // TC, c % TC
                    if j == 0:
                        pe.wait_ge(coll_done, per_batch(i, 2 * b + 2, 2))
                    if chunk_ok(c - 2):
                        pe.wait_ge(log_step, per_slot(i, 3 * (c - 2) + 3, 3))
                    elif c == 0:
                        pe.wait_ge(mu_ready, KC)
                    elif c == 1:
                        pe.wait_ge(y_step, 1)
                    for k in range(KC):
                        last = nc.tensor.matmul(b0[:, 0:D], coll[:, b % 2, k, j * P:(j + 1) * P], wo[:, k, :],
                                                start=(k == 0), stop=(k == KC - 1))
                    last.then_inc(wo_ready, 1)

                def b0_emptied(i, s):
                    b, j = s // TC - 3, s % TC
                    if chunk_ok(s - 5):
                        pe.wait_ge(y_step, per_slot(i, 4 * (s - 5) + 1, 4))
                    elif chunk_ok(s - 7):
                        pe.wait_ge(log_step, per_slot(i, 3 * (s - 7) + 3, 3))
                    elif chunk_ok(s - 8):
                        pe.wait_ge(logT_copied, per_slot(i, s - 7))
                    if j in (1, 2) and batch_ok(b):
                        pe.wait_ge(combT_copied, per_batch(i, 2 * b + j, 2))
                    if j == 0 and batch_ok(b):
                        pe.wait_ge(disp_copied, per_batch(i, 2 * b + 2, 2))

                def transpose_xn_and_logits(i, s):
                    b0_emptied(i, s)
                    c = s - 6
                    if chunk_ok(c):
                        pe.wait_ge(xn_step, per_slot(i, 4 * c + 2, 4))
                        for k in range(KC):
                            last = nc.tensor.transpose(b0[:, k * P:(k + 1) * P], xn[:, c // TC % 2, c % TC, k * P:(k + 1) * P], ident[:])
                        last.then_inc(xnT_ready, 1)
                    c = s - 7
                    if chunk_ok(c):
                        pe.wait_ge(log_step, per_slot(i, 3 * c + 3, 3))
                        for k in range(KC):
                            last = nc.tensor.transpose(b0[:, (KC + k) * P:(KC + k + 1) * P],
                                                       logit[:, c // TC % 2, c % TC, k * P:(k + 1) * P], ident[:])
                        last.then_inc(logT_ready, 1)

                def logits(i, c):
                    pe.wait_ge(xnT_copied, per_slot(i, c + 1))
                    if c >= 1:
                        pe.wait_ge(logT_copied, per_slot(i, c))
                    for k in range(KC):
                        last = nc.tensor.matmul(b0[:, 0:ES], xnT[:, c % 2, k, :], mu_unit[:, k, :], start=(k == 0), stop=(k == KC - 1))
                    last.then_inc(log_ready, 1)

                def b0_emptied_first(i, s):
                    if chunk_ok(s - 5):
                        pe.wait_ge(y_step, per_slot(i, 4 * (s - 5) + 1, 4))
                    elif chunk_ok(s - 7):
                        pe.wait_ge(log_step, per_slot(i, 3 * (s - 7) + 3, 3))
                    elif chunk_ok(s - 8):
                        pe.wait_ge(logT_copied, per_slot(i, s - 7))
                    elif s % TC == 1:
                        pe.wait_ge(disp_copied, 2 * (s // TC - 3) + 2)
                    elif s % TC == 2:
                        pe.wait_ge(combT_copied, 2 * (s // TC - 3) + 1)

                def transpose_combine(i, s, b, half):
                    pe.wait_ge(soft_exp, per_batch(i, 6 * b + TC, 6))
                    b0_emptied_first(i, s)
                    for k in range(KC):
                        for t in range(2):
                            last = nc.tensor.transpose(b0[:, (2 * k + t) * P:(2 * k + t + 1) * P],
                                                       logit[:, b % 2, 2 * half + t, k * P:(k + 1) * P], ident[:])
                    last.then_inc(combT_ready, 1)

                def transpose_dispatch(i, s, b, half):
                    pe.wait_ge(soft_post, per_batch(i, 4 * b + 3, 4))
                    if half == 1:
                        bank = b0
                        b0_emptied_first(i, s)
                    else:
                        bank = f1
                        if chunk_ok(s + 4):
                            pe.wait_ge(stk_copied, per_slot(i, 2 * (s + 4) + 2, 2))
                    for t in range(2):
                        for k in range(KC):
                            n = 2 * half + t
                            last = nc.tensor.transpose(bank[:, (t * KC + k) * P:(t * KC + k + 1) * P],
                                                       logitT[:, b % 2, k, n * P:(n + 1) * P], ident[:])
                    last.then_inc(disp_ready, 1)

                def slot_inputs(i, s, b):
                    pe.wait_ge(disp_copied, per_batch(i, 2 * b + 2, 2))
                    if chunk_ok(s + 4):
                        pe.wait_ge(stk_copied, per_slot(i, 2 * (s + 4) + 2, 2))
                    for k in range(KC):
                        for t in range(TC):
                            last = nc.tensor.matmul(f1[:, k * ES:(k + 1) * ES], xn[:, b % 2, t, k * P:(k + 1) * P], disp[:, t, :],
                                                    start=(t == 0), stop=(t == TC - 1))
                    last.then_inc(slot_ready, 1)

                def slot(i, s):
                    b, j = s // TC, s % TC
                    attn = chunk_ok(s)
                    if s == -8:
                        setup()
                    if s == -6:
                        setup_mu()
                    if s == -4:
                        setup_mu_rows()
                    if attn:
                        scores(i, s, 0)
                    if chunk_ok(s + 4):
                        stacks(i, s + 4)
                    if j in (1, 2) and batch_ok(b - 3):
                        transpose_combine(i, s, b - 3, j - 1)
                    if j == 0 and batch_ok(b - 3):
                        transpose_dispatch(i, s, b - 3, 1)
                    if chunk_ok(s - 1):
                        weighted_sum(i, s - 1, 2)
                    if attn:
                        scores(i, s, 1)
                    if chunk_ok(s + 7):
                        transposes(i, s + 7)
                    if attn and j in (0, 2):
                        gates(i, s)
                    if j == 1 and batch_ok(b - 3):
                        slot_inputs(i, s, b - 3)
                    if j == 3 and batch_ok(b - 2):
                        transpose_dispatch(i, s, b - 2, 0)
                    if chunk_ok(s - 1):
                        weighted_sum(i, s - 1, 3)
                    if chunk_ok(s - 6) or chunk_ok(s - 7):
                        transpose_xn_and_logits(i, s)
                    if attn:
                        scores(i, s, 2)
                    if chunk_ok(s + 7):
                        project_qk(i, s, s + 7)
                    if attn:
                        weighted_sum(i, s, 0)
                    if chunk_ok(s - 6):
                        logits(i, s - 6)
                    if attn:
                        scores(i, s, 3)
                    if chunk_ok(s + 7):
                        project_v(i, s + 7)
                    if attn:
                        weighted_sum(i, s, 1)
                    if chunk_ok(s - 4):
                        output_projection(i, s - 4)

                slots(pe, slot, FIRST, LAST)

            @block.vector
            def _(dve):
                def setup():
                    nc.vector.memset(ones, 1.0).then_inc(setup_v, 1)
                    dve.wait_ge(const_loaded, 32)
                    nc.vector.tensor_copy(ident16[:], ident[:]).then_inc(setup_v, 1)
                    dve.wait_ge(weight_loaded, 16 * WEIGHTS)
                    dve.wait_ge(setup_v, 2)
                    nc.vector.tensor_copy(xzT[:, 0, 0:KC, :], over(lnb_col[:, :], P)).then_inc(setup_v, 1)
                    dve.wait_ge(setup_t, 1)
                    nc.vector.tensor_copy(qk_bias[:], f1[:, :]).then_inc(setup_v, 1)
                    for k in range(KC):
                        nc.vector.tensor_scalar(wqk[:, k, :], wqk[:, k, :], lnw_col[:, k:k + 1], None, ALU.mult)\
                            .then_inc(setup_v, 1)
                    nc.vector.tensor_tensor(logit[:, 0, 0:KC, :], mu_unit[:, :, :], mu_unit[:, :, :], ALU.mult)\
                        .then_inc(setup_v, 1)
                    nc.vector.tensor_scalar(gq_col[:, 1:2], gq_col[:, 0:1], GATE_SCALE, None, ALU.mult).then_inc(gate_setup, 1)
                    dve.wait_ge(gate_setup, 1)
                    nc.vector.tensor_copy(gq_hi16[:], gq_col[:, 1:2]).then_inc(gate_setup, 1)
                    dve.wait_ge(gate_setup, 2)
                    nc.vector.tensor_tensor(gq_col[:, 2:3], gq_col[:, 1:2], gq_hi16[:], ALU.subtract).then_inc(gate_setup, 1)
                    nc.vector.tensor_tensor(gq_col[:, 3:4], gq_hi16[:], masks[:, 0:1], ALU.mult).then_inc(gate_setup, 1)
                    dve.wait_ge(gate_setup, 4)
                    nc.vector.scalar_tensor_tensor(out=gq_col[:, 0:1], in0=gq_col[:, 2:3], scalar=masks[:, 1:2],
                                                   in1=gq_col[:, 3:4], op0=ALU.mult, op1=ALU.add).then_inc(gate_setup, 1)
                    dve.wait_ge(gate_setup, 5)
                    nc.vector.tensor_scalar(gate_w[:], masks[:, 2:2 + 2 * HD], gq_col[:, 0:1], None, ALU.mult)\
                        .then_inc(gate_setup, 1)

                def setup_mu():
                    dve.wait_ge(setup_t, 2)
                    nc.vector.tensor_scalar(mu_norm[:, 0:KC], b0[:, 0:KC], NORM_EPS * NORM_EPS, None, ALU.max)\
                        .then_inc(setup_v, 1)

                def setup_mu_diag():
                    dve.wait_ge(setup_p, 3)
                    for k in range(KC):
                        nc.vector.tensor_scalar(disp[:, k, 0:P], ident[:], mu_norm[:, KC + k:KC + k + 1], None, ALU.mult)\
                            .then_inc(setup_v, 1)
                    dve.wait_ge(setup_t, 3)
                    for k in range(KC):
                        nc.vector.scalar_tensor_tensor(out=mu_unit[:, k, :], in0=mu_unit[:, k, :], scalar=scale_col[:, 0:1],
                                                       in1=b0[:, 0:ES], op0=ALU.mult, op1=ALU.mult).then_inc(mu_ready, 1)

                def row_stats(i, c):
                    dve.wait_ge(x_loaded[c % 4], times(i, 16 * (c // 4 + 1), 32))
                    nc.vector.bn_stats(bn[:, c % 2, :], xs[:, c % 4, :]).then_inc(stats, 1)
                    dve.wait_ge(stats, per_slot(i, 3 * c + 1, 3))
                    hold_wait()
                    nc.vector.bn_aggr(mv[:, c % 4, :], bn[:, c % 2, :]).then_inc(stats, 1)
                    dve.wait_ge(stats, per_slot(i, 3 * c + 2, 3))
                    nc.vector.tensor_scalar(var_eps[:, c % 4:c % 4 + 1], mv[:, c % 4, 1:2], LN_EPS, None, ALU.add)\
                        .then_inc(stats, 1)

                def normalise(i, c):
                    dve.wait_ge(rstd_ready, per_slot(i, c + 1))
                    if c >= 2:
                        dve.wait_ge(xzT_ready, per_slot(i, c - 1))
                    nc.vector.tensor_scalar(z[:, c % 2, :], xs[:, c % 4, :], mv[:, c % 4, 0:1], rstd[:, c % 4:c % 4 + 1],
                                            ALU.subtract, ALU.mult).then_inc(z_ready, 1)

                def copy_stacks(i, c):
                    b, j = c // TC, c % TC
                    if b >= 2 and j == 0:
                        dve.wait_ge(sc_ready, per_slot(i, 8 * TC * (b - 1), 8))
                        dve.wait_ge(gate_ready, per_batch(i, 2 * (b - 1), 2))
                    for side, bank in ((0, f0h), (1, f1h)):
                        dve.wait_ge(stk_ready, per_slot(i, 2 * c + side + 1, 2))
                        nc.vector.tensor_copy(stack[:, b % 2, side, :, j * P:(j + 1) * P],
                                              bank.rearrange("p (a n) -> p a n", n=P)).then_inc(stk_copied, 1)

                def add_qk_bias(i, c):
                    dve.wait_ge(qk_ready, per_slot(i, c + 1))
                    if c >= 4:
                        dve.wait_ge(sqg_ready, per_slot(i, 2 * (c - 4) + 2, 2))
                    nc.vector.tensor_tensor(qk[:, c % 4, :], f1[:, :], qk_bias[:], ALU.add).then_inc(qk_copied, 1)

                def sum_squares(i, c):
                    dve.wait_ge(sqg_ready, per_slot(i, 2 * c + 2, 2))
                    if c >= 2:
                        dve.wait_ge(rn_ready, per_slot(i, c - 1))
                    nc.vector.tensor_reduce(sums[:, c % 2, :], heads(sqg[:, :]), AX_X, ALU.add).then_inc(sums_ready, 1)
                    dve.wait_ge(sums_ready, per_slot(i, 2 * c + 1, 2))
                    nc.vector.tensor_scalar(sums[:, c % 2, 0:2 * H], sums[:, c % 2, 0:2 * H], NORM_EPS * NORM_EPS, None, ALU.max)\
                        .then_inc(sums_ready, 1)

                def split_qk(i, c):
                    dve.wait_ge(rn_ready, per_slot(i, c + 1))
                    nc.vector.tensor_tensor(heads(qn[:, :]), heads(qk[:, c % 4, :]), over(rn[:, c % 2, :], HD), ALU.mult)\
                        .then_inc(norm_step, 1)
                    if c >= 2:
                        dve.wait_ge(v_gated, per_slot(i, c - 1))
                    nc.vector.tensor_tensor(gate_k[:, c % 2, :], sums[:, c % 2, 2 * H:3 * H], rn[:, c % 2, H:2 * H], ALU.mult)\
                        .then_inc(norm_step, 1)
                    if c >= 2:
                        dve.wait_ge(stk_ready, per_slot(i, 2 * (c - 2) + 2, 2))
                    dve.wait_ge(norm_step, per_slot(i, 2 * c + 2, 2))
                    nc.vector.tensor_copy(hl[:, c % 2, :, 0, :], heads(qn[:, :])).then_inc(hi_ready, 1)
                    dve.wait_ge(hi_ready, per_slot(i, 2 * c + 1, 2))
                    nc.vector.tensor_tensor(hl[:, c % 2, :, 3, :], heads(qn[:, :]), hl[:, c % 2, :, 0, :], ALU.subtract)\
                        .then_inc(hi_ready, 1)
                    dve.wait_ge(hi_ready, per_slot(i, 2 * c + 2, 2))
                    nc.vector.tensor_copy(hl[:, c % 2, 0:H, 1:3, :], hl[:, c % 2, 0:H, 0:4:3, :]).then_inc(hl_ready, 1)
                    nc.vector.tensor_copy(hl[:, c % 2, H:2 * H, 1, :], hl[:, c % 2, H:2 * H, 3, :]).then_inc(hl_ready, 1)
                    nc.vector.tensor_copy(hl[:, c % 2, H:2 * H, 2, :], hl[:, c % 2, H:2 * H, 0, :]).then_inc(hl_ready, 1)

                def gate_values(i, c):
                    b, j = c // TC, c % TC
                    dve.wait_ge(norm_step, per_slot(i, 2 * c + 2, 2))
                    dve.wait_ge(v_copied, per_slot(i, c + 1))
                    if c == 0:
                        dve.wait_ge(setup_p, 2)
                    if b >= 2 and j == 0:
                        dve.wait_ge(pv_done, per_slot(i, 4 * TC * (b - 1), 4))
                    nc.vector.tensor_tensor(vpad[:, b % 2, j, :, :].rearrange("p a (o d) -> p a o d", d=HD)[:, :, 0:3:2, :],
                                            v_raw[:, c % 4, :].rearrange("p (a o d) -> p a o d", o=2, d=HD),
                                            over(gate_k[:, c % 2, :].rearrange("p (a o) -> p a o", o=2), HD), ALU.mult)\
                        .then_inc(v_gated, 1)

                def gate_sums(i, b, half):
                    dve.wait_ge(pv_done, per_batch(i, 4 * (TC * b + 2 * half + 2), 4 * TC))
                    dve.wait_ge(gate_copied, per_batch(i, 2 * b + half + 1, 2))
                    if b >= 2:
                        dve.wait_ge(wo_ready, per_batch(i, TC * (b - 1), TC))
                    nc.vector.tensor_tensor(coll[:, b % 2, half, :], coll_ps[:, :], gate_q[:, half, :], ALU.mult)\
                        .then_inc(coll_done, 1)

                def residual(i, c):
                    dve.wait_ge(wo_ready, per_slot(i, c + 1))
                    dve.wait_ge(xb_ready, per_slot(i, c + 1))
                    nc.vector.tensor_tensor(y[:, c % 2, :], b0[:, 0:D], xr[:, c % 4, :], ALU.add).then_inc(y_step, 1)
                    dve.wait_ge(y_step, per_slot(i, 4 * c + 1, 4))
                    nc.vector.bn_stats(ybn[:, c % 2, :], y[:, c % 2, :]).then_inc(y_step, 1)
                    dve.wait_ge(y_step, per_slot(i, 4 * c + 2, 4))
                    hold_wait()
                    nc.vector.bn_aggr(ymv[:, c % 2, :], ybn[:, c % 2, :]).then_inc(y_step, 1)
                    dve.wait_ge(y_step, per_slot(i, 4 * c + 3, 4))
                    nc.vector.tensor_scalar(yvar[:, c % 2:c % 2 + 1], ymv[:, c % 2, 1:2], LN_EPS, None, ALU.add).then_inc(y_step, 1)

                def first_norm(i, c):
                    dve.wait_ge(yrstd_ready, per_slot(i, c + 1))
                    if c >= 2:
                        dve.wait_ge(x1_stored[c % 2], times(i, 16 * (c // 2), 16 * LOOP_SLOTS // 2))
                    rs = yrstd[:, c % 2:c % 2 + 1]
                    nc.vector.tensor_scalar(x1[:, c % 2, :], y[:, c % 2, :], ymv[:, c % 2, 0:1], rs, ALU.subtract, ALU.mult)\
                        .then_inc(x1_ready, 1)
                    nc.vector.tensor_scalar(v1[:, c % 2, 0:1], ymv[:, c % 2, 1:2], rs, rs, ALU.mult, ALU.mult).then_inc(x1_ready, 1)
                    dve.wait_ge(x1_ready, per_slot(i, 3 * c + 2, 3))
                    nc.vector.tensor_scalar(v1[:, c % 2, 1:2], v1[:, c % 2, 0:1], LN_EPS, None, ALU.add).then_inc(x1_ready, 1)

                def second_norm(i, c):
                    b, j = c // TC, c % TC
                    dve.wait_ge(r1_ready, per_slot(i, c + 1))
                    nc.vector.scalar_tensor_tensor(out=xg[:], in0=x1[:, c % 2, :], scalar=r1[:, c % 2:c % 2 + 1], in1=gamma_all[:],
                                                   op0=ALU.mult, op1=ALU.mult).then_inc(xn_step, 1)
                    dve.wait_ge(xn_step, per_slot(i, 4 * c + 1, 4))
                    if b >= 2 and j == 0:
                        dve.wait_ge(slot_ready, per_batch(i, b - 1))
                    nc.vector.tensor_tensor(xn[:, b % 2, j, :], xg[:], beta_all[:], ALU.add).then_inc(xn_step, 1)
                    dve.wait_ge(xn_step, per_slot(i, 4 * c + 2, 4))
                    nc.vector.tensor_tensor_reduce(xg[:], xn[:, b % 2, j, :], xn[:, b % 2, j, :], 1.0, 0.0, ALU.mult, ALU.add,
                                                   xss[:, c % 2, 0:1]).then_inc(xn_step, 1)
                    dve.wait_ge(xn_step, per_slot(i, 4 * c + 3, 4))
                    nc.vector.tensor_scalar(xss[:, c % 2, 1:2], xss[:, c % 2, 0:1], NORM_EPS * NORM_EPS, None, ALU.max)\
                        .then_inc(xn_step, 1)

                def scale_logits(i, c):
                    b, t = c // TC, c % TC
                    dve.wait_ge(log_ready, per_slot(i, c + 1))
                    dve.wait_ge(xrn_ready, per_slot(i, c + 1))
                    nc.vector.tensor_reduce(rmax[:, b % 2, t, 0:1], b0[:, 0:ES], AX_X, ALU.max).then_inc(log_step, 1)
                    if b >= 2 and t == 0:
                        dve.wait_ge(combT_ready, per_batch(i, 2 * (b - 1), 2))
                    nc.vector.tensor_scalar(logit[:, b % 2, t, :], b0[:, 0:ES], xrn[:, c % 2:c % 2 + 1], None, ALU.mult)\
                        .then_inc(log_step, 1)
                    dve.wait_ge(log_step, per_slot(i, 3 * c + 1, 3))
                    nc.vector.tensor_scalar(rmax[:, b % 2, t, 1:2], rmax[:, b % 2, t, 0:1], xrn[:, c % 2:c % 2 + 1], -1.0,
                                            ALU.mult, ALU.mult).then_inc(log_step, 1)

                def column_max(i, b):
                    dve.wait_ge(logT_copied, per_batch(i, TC * (b + 1), TC))
                    if b >= 1:
                        dve.wait_ge(soft_exp, per_batch(i, 6 * b, 6))
                    nc.vector.tensor_reduce(cmax[:], logitT[:, b % 2, :, :], AX_X, ALU.max).then_inc(soft_max, 1)
                    dve.wait_ge(soft_max, per_batch(i, 2 * b + 1, 2))
                    nc.vector.tensor_scalar(cmax[:], cmax[:], -1.0, None, ALU.mult).then_inc(soft_max, 1)

                def normalise_dispatch(i, b):
                    dve.wait_ge(soft_exp, per_batch(i, 6 * (b + 1), 6))
                    nc.vector.reciprocal(esum[:, b % 2, :], esum[:, b % 2, :]).then_inc(soft_post, 1)
                    dve.wait_ge(soft_post, per_batch(i, 4 * b + 1, 4))
                    for k in range(KC):
                        nc.vector.tensor_scalar(logitT[:, b % 2, k, :], logitT[:, b % 2, k, :], esum[:, b % 2, k:k + 1], None, ALU.mult)\
                            .then_inc(soft_post, 1)
                    nc.vector.reciprocal(crec[:, bass.ds(per_batch(i, TC * b, TC), TC)], csum[:, b % 2, :]).then_inc(soft_post, 1)

                def slot(i, s):
                    b, j = s // TC, s % TC
                    if s == -8:
                        setup()
                    if s == -5:
                        setup_mu()
                    if s == -4:
                        setup_mu_diag()
                    if chunk_ok(s + 8):
                        row_stats(i, s + 8)
                    if chunk_ok(s + 4):
                        copy_stacks(i, s + 4)
                    if chunk_ok(s - 5):
                        first_norm(i, s - 5)
                    if j == 3 and batch_ok(b - 2):
                        normalise_dispatch(i, b - 2)
                    if chunk_ok(s + 6):
                        sum_squares(i, s + 6)
                    if j == 2 and batch_ok(b):
                        gate_sums(i, b, 0)
                    if j == 0 and batch_ok(b - 1):
                        gate_sums(i, b - 1, 1)
                    if chunk_ok(s + 4):
                        gate_values(i, s + 4)
                    if chunk_ok(s + 5):
                        split_qk(i, s + 5)
                    if chunk_ok(s - 6):
                        scale_logits(i, s - 6)
                    if j == 2 and batch_ok(b - 2):
                        column_max(i, b - 2)
                    if chunk_ok(s + 8):
                        normalise(i, s + 8)
                    if chunk_ok(s - 5):
                        second_norm(i, s - 5)
                    if chunk_ok(s + 7):
                        add_qk_bias(i, s + 7)
                    if chunk_ok(s - 4):
                        residual(i, s - 4)

                slots(dve, slot, FIRST, LAST)


        M = B * S // P
        EP = E // 2
        b1_col = sb("b1_col", [P, EP])
        res_flat = res[:, :, :, :].rearrange("p a q t -> p (a q t)")
        b2_all = res_flat[:, 0:E * D].rearrange("p (e d) -> p e d", e=E)
        slot_out = res_flat[:, E * D:E * D + 4 * M * D].rearrange("p (r m d) -> p r m d", r=4, m=M)
        out_sb = res_flat[:, E * D + 4 * M * D:E * D + 4 * M * D + 2 * TC * D].rearrange("p (a t d) -> p a t d", a=2, t=TC)
        stack_flat = stack[:, :, :, :, :].rearrange("p a b c t -> p (a b c t)").bitcast(F32)
        hidden = stack_flat[:, 0:EP * B * S].rearrange("p (a n) -> p a n", a=EP)
        at = EP * B * S
        x1_sb = stack_flat[:, at:at + 2 * TC * D].rearrange("p (a t d) -> p a t d", a=2, t=TC)
        at += 2 * TC * D
        comb_sb = stack_flat[:, at:at + 2 * KC * T].rearrange("p (a k n) -> p a k n", a=2, k=KC)
        at += 2 * KC * T
        w1s = stack_flat[:, at:at + KC * E * HF].rearrange("p (k e h) -> p k e h", k=KC, e=E)
        w2s = vpad[:, :, :, :, :].rearrange("p a t c d -> p (a t c d)")[:, 0:EP * D].rearrange("p (a d) -> p a d", a=EP)
        so_sb = coll[:, :, :, :].rearrange("p a b t -> p (a b t)")[:, 0:2 * KC * D].rearrange("p (a k d) -> p a k d", a=2, k=KC)
        y2 = qk[:, :, :].rearrange("p a n -> p (a n)").rearrange("p (a t d) -> p a t d", a=2, t=TC)
        crec4 = sb("crec4", [P, 2, TC])
        obn = sb("obn", [P, 2, TC, 6])
        omv = sb("omv", [P, 2, TC, 2])
        ovar, orstd, oshift = sb("ovar", [P, 2, TC]), sb("orstd", [P, 2, TC]), sb("oshift", [P, 2, 2, TC])

        expert_loaded, b2_loaded = sem("expert_loaded"), sem("b2_loaded")
        h_ready, h_done, so_ready, so_done = sem("h_ready"), sem("h_done"), sem("so_ready"), sem("so_done")
        so_stored = [sem(f"so_stored{k}") for k in range(4)]
        xc_loaded = [sem(f"xc_loaded{k}") for k in range(2)]
        so_loaded = [sem(f"so_loaded{k}") for k in range(2)]
        comb_ready_ps, y2_step, oagg = sem("comb_ready_ps"), sem("y2_step"), sem("oagg")
        ostat_ready, out_ready = sem("ostat_ready"), sem("out_ready")
        crec_copied, obn_ready, omv_ready = sem("crec_copied"), sem("obn_ready"), sem("omv_ready")
        out_stored = [sem(f"out_stored{k}") for k in range(2)]

        def batches(eng, batch):
            batch(None, 0)
            batch(None, 1)
            with eng.Fori(0, B // 2 - 1) as i:
                batch(i, 2)
                batch(i, 3)

        h_ps = [f0, f1]
        so_ps = [score_ps[0][:, 0, :], score_ps[0][:, 1, :], score_ps[1][:, 0, :], score_ps[1][:, 1, :]]

        with nc.Block() as block:

            @block.sync
            def _(sp):
                for k in range(KC):
                    sp.dma_start(w1s[:, k, :, :], w1.rearrange("e (k p) h -> k p e h", p=P)[k]).then_inc(expert_loaded, 16)
                for i in range(2):
                    rows = slice(HF * i, HF * i + HF)
                    sp.dma_start(b1_col[rows, :], b1.rearrange("(a i) h -> i h a", i=2)[i],
                                 allow_slow_non_contiguous=True).then_inc(expert_loaded, 16)
                    sp.dma_start(w2s[rows, :, :], w2.rearrange("(a i) h d -> i h a d", i=2)[i]).then_inc(expert_loaded, 16)
                sp.dma_start(b2_all, b2.unsqueeze(0).broadcast_to([P, E, D])).then_inc(b2_loaded, 16)

                def load(i, b):
                    if b >= 2:
                        sp.wait_ge(y2_step, times(i, TC * (b - 1), 2 * TC))
                    sp.dma_start(x1_sb[:, b % 2, :, :], x1_dram[bass.ds(times(i, b * T, 2 * T), T), :]
                                 .rearrange("(t p) d -> p t d", p=P)).then_inc(xc_loaded[b % 2], 16)
                    sp.dma_start(comb_sb[:, b % 2, :, :], comb_dram[bass.ds(times(i, b, 2), 1), :, :, :]
                                 .rearrange("b p k n -> (b p) k n")).then_inc(xc_loaded[b % 2], 16)

                def load_slots(i, b):
                    if b >= 2:
                        sp.wait_ge(y2_step, times(i, TC * (b - 1), 2 * TC))
                    sp.dma_start(so_sb[:, b % 2, :, :], slot_dram[bass.ds(times(i, b, 2), 1), :, :]
                                 .rearrange("b (k p) d -> (b p) k d", p=P)).then_inc(so_loaded[b % 2], 16)

                load(None, 0)
                load(None, 1)
                for e in range(E):
                    sp.wait_ge(so_done, e + 1)
                    for m in range(M):
                        sp.dma_start(slot_dram[m * (P // S):(m + 1) * (P // S), e * S:(e + 1) * S, :],
                                     slot_out[:, e % 4, m, :]).then_inc(so_stored[e % 4], 16)
                for k in range(4):
                    sp.wait_ge(so_stored[k], 16 * M * E // 4)
                load_slots(None, 0)
                load_slots(None, 1)

                def store(i, b):
                    sp.wait_ge(out_ready, times(i, TC * (b + 1), 2 * TC))
                    sp.dma_start(out_rows[bass.ds(times(i, b * T, 2 * T), T), :].rearrange("(t p) d -> p t d", p=P),
                                 out_sb[:, b % 2, :, :]).then_inc(out_stored[b % 2], 16)

                with sp.Fori(0, B // 2 - 1) as i:
                    for b in (2, 3):
                        load(i, b)
                        load_slots(i, b)
                        store(i, b - 2)
                store(None, B - 2)
                store(None, B - 1)
                for k in range(2):
                    sp.wait_ge(out_stored[k], 16 * B // 2)

            @block.tensor
            def _(pe):
                def hidden_layer(a):
                    if a >= 2:
                        pe.wait_ge(h_done, a - 1)
                    for k in range(KC):
                        for i in range(2):
                            last = nc.tensor.matmul(h_ps[a % 2][HF * i:HF * i + HF, 0:B * S], w1s[:, k, 2 * a + i, :],
                                                    slotT[:, k, 2 * a + i, :, :].rearrange("p b s -> p (b s)"),
                                                    start=(k == 0), stop=(k == KC - 1), tile_position=(0, HF * i))
                    last.then_inc(h_ready, 1)

                def output_layer(a):
                    pe.wait_ge(h_done, a + 1)
                    for i in range(2):
                        e = 2 * a + i
                        rows = slice(HF * i, HF * i + HF)
                        if e >= 4:
                            pe.wait_ge(so_done, e - 3)
                        for m in range(M):
                            last = nc.tensor.matmul(so_ps[e % 4][:, m * D:(m + 1) * D], hidden[rows, a, m * P:(m + 1) * P],
                                                    w2s[rows, a, :], start=True, stop=True, tile_position=(HF * i, 0))
                        last.then_inc(so_ready, 1)

                pe.wait_ge(expert_loaded, 16 * (KC + 4))
                for a in range(EP):
                    hidden_layer(a)
                    if a >= 1:
                        output_layer(a - 1)
                output_layer(EP - 1)
                pe.wait_ge(so_done, E)

                def combine(i, b):
                    pe.wait_ge(xc_loaded[b % 2], times(i, 32 * (b // 2 + 1), 32))
                    pe.wait_ge(so_loaded[b % 2], times(i, 16 * (b // 2 + 1), 16))
                    for t in range(TC):
                        if b >= 1:
                            pe.wait_ge(y2_step, times(i, TC * (b - 1) + t + 1, 2 * TC))
                        for k in range(KC):
                            last = nc.tensor.matmul(so_ps[t][:, 0:D], comb_sb[:, b % 2, k, t * P:(t + 1) * P], so_sb[:, b % 2, k, :],
                                                    start=(k == 0), stop=(k == KC - 1))
                        last.then_inc(comb_ready_ps, 1)

                batches(pe, combine)

            @block.scalar
            def _(act):
                act.wait_ge(expert_loaded, 16 * (KC + 4))
                for a in range(EP):
                    act.wait_ge(h_ready, a + 1)
                    nc.scalar.activation(hidden[:, a, :], h_ps[a % 2][:, 0:B * S], ACT.Gelu, bias=b1_col[:, a:a + 1])\
                        .then_inc(h_done, 1)

                def normalise_out(i, b):
                    act.wait_ge(ostat_ready, times(i, 3 * (b + 1), 6))
                    if b >= 2:
                        act.wait_ge(out_stored[b % 2], times(i, 16 * (b // 2), 16))
                    for t in range(TC):
                        nc.scalar.activation(out_sb[:, b % 2, t, :], y2[:, b % 2, t, :], ACT.Identity,
                                             scale=orstd[:, b % 2, t:t + 1], bias=oshift[:, b % 2, 1, t:t + 1]).then_inc(out_ready, 1)

                batches(act, normalise_out)

            @block.gpsimd
            def _(pool):
                def out_stats(i, b):
                    pool.wait_ge(oagg, times(i, b + 1, 2))
                    if b >= 2:
                        pool.wait_ge(out_ready, times(i, TC * (b - 1), 2 * TC))
                    nc.gpsimd.tensor_tensor(orstd[:, b % 2, :], ovar[:, b % 2, :], minus_half[:, 0:TC], ALU.pow).then_inc(ostat_ready, 1)
                    nc.gpsimd.tensor_scalar(oshift[:, b % 2, 0, :], omv[:, b % 2, :, 0], -1.0, None, ALU.mult).then_inc(ostat_ready, 1)
                    pool.wait_ge(ostat_ready, times(i, 3 * b + 2, 6))
                    nc.gpsimd.tensor_tensor(oshift[:, b % 2, 1, :], oshift[:, b % 2, 0, :], orstd[:, b % 2, :], ALU.mult)\
                        .then_inc(ostat_ready, 1)

                batches(pool, out_stats)

            @block.vector
            def _(dve):
                dve.wait_ge(b2_loaded, 16)
                for e in range(E):
                    dve.wait_ge(so_ready, e + 1)
                    if e >= 4:
                        dve.wait_ge(so_stored[e % 4], 16 * M * (e // 4))
                    nc.vector.tensor_tensor(slot_out[:, e % 4, :, :], so_ps[e % 4].rearrange("p (m d) -> p m d", m=M),
                                            b2_all[:, e, :].unsqueeze(1).broadcast_to([P, M, D]), ALU.add).then_inc(so_done, 1)

                def residual_out(i, b):
                    if b >= 2:
                        dve.wait_ge(out_ready, times(i, TC * (b - 1), 2 * TC))
                    nc.vector.tensor_copy(crec4[:, b % 2, :], crec[:, bass.ds(times(i, TC * b, 2 * TC), TC)]).then_inc(crec_copied, 1)
                    dve.wait_ge(crec_copied, times(i, b + 1, 2))
                    dve.wait_ge(xc_loaded[b % 2], times(i, 32 * (b // 2 + 1), 32))
                    for t in range(TC):
                        dve.wait_ge(comb_ready_ps, times(i, TC * b + t + 1, 2 * TC))
                        nc.vector.scalar_tensor_tensor(out=y2[:, b % 2, t, :], in0=so_ps[t][:, 0:D], scalar=crec4[:, b % 2, t:t + 1],
                                                       in1=x1_sb[:, b % 2, t, :], op0=ALU.mult, op1=ALU.add).then_inc(y2_step, 1)
                    for t in range(TC):
                        dve.wait_ge(y2_step, times(i, TC * b + t + 1, 2 * TC))
                        nc.vector.bn_stats(obn[:, b % 2, t, :], y2[:, b % 2, t, :]).then_inc(obn_ready, 1)
                    dve.wait_ge(obn_ready, times(i, TC * (b + 1), 2 * TC))
                    hold_wait()
                    for t in range(TC):
                        nc.vector.bn_aggr(omv[:, b % 2, t, :], obn[:, b % 2, t, :]).then_inc(omv_ready, 1)
                    dve.wait_ge(omv_ready, times(i, TC * (b + 1), 2 * TC))
                    nc.vector.tensor_scalar(ovar[:, b % 2, :], omv[:, b % 2, :, 1], LN_EPS, None, ALU.add).then_inc(oagg, 1)

                batches(dve, residual_out)


_INS = ['L0_attn_x', 'L0_attn_Wq', 'L0_attn_Wk', 'L0_attn_Wv', 'L0_attn_gq', 'L0_attn_gk', 'L0_attn_Wo', 'L0_attn_bo',
        'L0_attn_ln_w', 'L0_attn_ln_b', 'L0_ffn_ln_gamma', 'L0_ffn_ln_beta', 'L0_ffn_mu', 'L0_ffn_scale',
        'L0_ffn_w1', 'L0_ffn_b1', 'L0_ffn_w2', 'L0_ffn_b2']


def kernel(**inputs):
    import numpy as np
    import concourse.bacc as bacc
    from concourse import mybir as mb
    from concourse.bass_utils import run_bass_kernel_spmd

    nc = bacc.Bacc("TRN2", target_bir_lowering=False, num_devices=1, dynamic_dma_scratch_size=1024)
    arrays, args = {}, []

    def give(name, a):
        arrays[f"in_{name}_dram"] = a
        args.append(nc.dram_tensor(f"in_{name}_dram", a.shape, mb.dt.from_np(a.dtype), kind="ExternalInput").ap())

    for name in _INS:
        give(name, np.ascontiguousarray(inputs[name]))
    row, head_rows, hd = np.arange(128), 64, 16
    low = (row % head_rows) // hd % 2
    block = (row[:, None] // head_rows) == (np.arange(2 * hd)[None, :] // hd)
    give("consts", np.concatenate([np.eye(128), (low == 0)[:, None], (low == 1)[:, None], block], axis=1).astype(np.float32))
    shape = inputs['L0_attn_x'].shape
    args.append(nc.dram_tensor("out_0_dram", shape, mb.dt.float32, kind="ExternalOutput").ap())
    seq_block_kernel(nc, *args)
    r = run_bass_kernel_spmd(nc, [arrays], core_ids=[0])
    return r.results[0]["out_0_dram"]
```

```python
from contextlib import ExitStack

import concourse.bass as bass
from concourse import mybir

F32 = mybir.dt.float32
F16 = mybir.dt.float16
ALU = mybir.AluOpType
ACT = mybir.ActivationFunctionType
AX_X = mybir.AxisListType.X

P = 128
THRESH = 0.29514
SHARP = 15.0
LN_EPS = 1e-5
NORM_EPS = 1e-12
GATE_SCALE = 16.0
W_SCALE = 1024.0

LOOP_FROM, LOOP_SLOTS, LOOP_TIMES = 16, 8, 4


def seq_block_kernel(nc, x, Wq, Wk, Wv, gq, gk, Wo, bo, ln_w, ln_b, gamma, beta, mu, scale,
                     w1, b1, w2, b2, consts, out):
    B, T, D = x.shape
    HD = gq.shape[0]
    H = D // HD
    E, S = mu.shape[1], mu.shape[2]
    ES = E * S
    HF = w1.shape[2]
    KC = D // P
    TC = T // P
    NCH = B * TC
    PAIRS = H // 2
    GROUPS = 4
    QUADS = 4
    assert (D, HD, E, S, HF, TC) == (256, 16, 16, 16, 64, 4)

    x_rows = x.rearrange("b t d -> (b t) d")
    out_rows = out.rearrange("b t d -> (b t) d")
    x1_dram = nc.dram_tensor("x1_scratch", (B * T, D), F32, kind="Internal").ap()
    comb_dram = nc.dram_tensor("combine_scratch", (B, P, KC, T), F32, kind="Internal").ap()
    slot_dram = nc.dram_tensor("slot_out_scratch", (B, ES, D), F32, kind="Internal").ap()

    with ExitStack() as ctx:
        def sb(name, shape, dt=F32):
            return ctx.enter_context(nc.sbuf_tensor(name, shape, dt))

        def ps(name, shape, dt=F32):
            return ctx.enter_context(nc.psum_tensor(name, shape, dt))

        def sem(name):
            return ctx.enter_context(nc.semaphore(name))

        ident = sb("ident", [P, P])
        ident16 = sb("ident16", [P, P], F16)
        masks = sb("masks", [P, 2 + 2 * HD])
        minus_half = sb("minus_half", [P, 2 * H])
        wqk_hi, wqk_lo = sb("wqk_hi", [P, KC, 2 * D], F16), sb("wqk_lo", [P, KC, 2 * D], F16)
        wv_hi, wv_lo = sb("wv_hi", [P, KC, D], F16), sb("wv_lo", [P, KC, D], F16)
        wo = sb("wo", [P, KC, D])
        mu_hi, mu_lo = sb("mu_hi", [P, KC, ES], F16), sb("mu_lo", [P, KC, ES], F16)
        wv_sum = sb("wv_sum", [P, D])
        lnw_scaled = sb("lnw_scaled", [P, KC])
        qk_bias = sb("qk_bias", [P, 2 * D])
        gk_all = sb("gk_all", [P, D])
        bo_all = sb("bo_all", [P, D])
        gamma_all = sb("gamma_all", [P, D])
        beta_all = sb("beta_all", [P, D])
        lnw_col = sb("lnw_col", [P, KC])
        lnb_col = sb("lnb_col", [P, KC])
        scale_col = sb("scale_col", [P, 1])
        gq_col = sb("gq_col", [P, 4])
        gq_hi16 = sb("gq_hi16", [P, 1], F16)
        gate_w = sb("gate_w", [P, 2 * HD], F16)
        wait_holder = sb("wait_holder", [P, 1])
        mu_norm = sb("mu_norm", [P, 2 * KC])

        xs = sb("xs", [P, 4, D])
        bn = sb("bn", [P, 2, 6])
        mv = sb("mv", [P, 4, 2])
        var_eps = sb("var_eps", [P, 4])
        rstd = sb("rstd", [P, 4])
        z = sb("z", [P, 2, D])
        zT_hi, zT_lo = sb("zT_hi", [P, 2, KC, P], F16), sb("zT_lo", [P, 2, KC, P], F16)
        sd_v = sb("sd_v", [P, 4])
        qk = sb("qk", [P, 4, 2 * D])
        v_raw = sb("v_raw", [P, 4, D])
        sqg = sb("sqg", [P, 3 * D])
        sums = sb("sums", [P, 2, 3 * H])
        rn = sb("rn", [P, 2, 2 * H])
        qn = sb("qn", [P, 2 * D])
        hl = sb("hl", [P, 2, 2 * H, 4, HD], F16)
        gate_k = sb("gate_k", [P, 2, H])
        stack = sb("stack", [P, 2, 2, PAIRS, T], F16)
        vpad = sb("vpad", [P, 2, TC, PAIRS, 3 * HD])
        res = sb("res", [P, 4, QUADS, T])
        ones = res[:, 0, 0, 0:P]
        lnb_cols = res[:, 0, 1, 0:KC * P].rearrange("p (k n) -> p k n", k=KC)
        wqk = res[:, 1, 0:2, :]
        wv = res[:, 2, 0, :].rearrange("p (k n) -> p k n", k=KC)
        mu_whole = res[:, 2, 1, :].rearrange("p (k n) -> p k n", k=KC)
        gate_q = sb("gate_q", [P, 2, T])
        coll = sb("coll", [P, 2, 2, T])
        xr = sb("xr", [P, 4, D])
        y = sb("y", [P, 2, D])
        ybn = sb("ybn", [P, 2, 6])
        ymv = sb("ymv", [P, 2, 2])
        yvar = sb("yvar", [P, 2])
        yrstd = sb("yrstd", [P, 2])
        v1 = sb("v1", [P, 2, 2])
        r1 = sb("r1", [P, 2])
        x1 = sb("x1", [P, 2, D])
        xg = sb("xg", [P, D])
        xn = sb("xn", [P, 2, TC, D])
        xss = sb("xss", [P, 2, 2])
        xrn = sb("xrn", [P, 2])
        xnT_hi, xnT_lo = sb("xnT_hi", [P, 2, KC, P], F16), sb("xnT_lo", [P, 2, KC, P], F16)
        logit = sb("logit", [P, 2, TC, ES])
        rmax = sb("rmax", [P, 2, TC, 2])
        csum = sb("csum", [P, 2, TC])
        logitT = sb("logitT", [P, 2, KC, T])
        cmax = sb("cmax", [P, KC])
        esum = sb("esum", [P, 2, KC])
        disp = sb("disp", [P, TC, ES])
        combT = sb("combT", [P, 2, 2 * ES])
        slotT = sb("slotT", [P, KC, E, B, S])
        crec = sb("crec", [P, NCH])

        score_ps = [ps(f"score{t}", [P, 2, T]) for t in range(2)]
        coll_ps = ps("coll_ps", [P, T])
        f0 = ps("f0", [P, 512])
        f1 = ps("f1", [P, 512])
        b0 = ps("b0", [P, 512])
        f0h, f1h = f0[:, :].bitcast(F16), f1[:, :].bitcast(F16)

        const_loaded, wqk_loaded, weight_loaded = sem("const_loaded"), sem("wqk_loaded"), sem("weight_loaded")
        zT_split, v_shifted, wqk_split, wv_split = sem("zT_split"), sem("v_shifted"), sem("wqk_split"), sem("wv_split")
        xnT_split, mu_split, squares_ready = sem("xnT_split"), sem("mu_split"), sem("squares_ready")
        lnw_ready, mu_squared, kg_ready, sd_ready = sem("lnw_ready"), sem("mu_squared"), sem("kg_ready"), sem("sd_ready")
        setup_v, setup_p, setup_t = sem("setup_v"), sem("setup_p"), sem("setup_t")
        x_loaded = [sem(f"x_loaded{k}") for k in range(4)]
        xr_loaded = [sem(f"xr_loaded{k}") for k in range(4)]
        x1_stored = [sem(f"x1_stored{k}") for k in range(2)]
        comb_stored = [sem(f"comb_stored{k}") for k in range(2)]
        stats, z_ready, rstd_ready = sem("stats"), sem("z_ready"), sem("rstd_ready")
        zT_ready, zT_copied = sem("zT_ready"), sem("zT_copied")
        qk_ready, qk_copied = sem("qk_ready"), sem("qk_copied")
        v_ready, v_copied = sem("v_ready"), sem("v_copied")
        sums_ready, rn_ready = sem("sums_ready"), sem("rn_ready")
        norm_step, hl_ready, v_gated = sem("norm_step"), sem("hl_ready"), sem("v_gated")
        stk_ready, stk_copied = sem("stk_ready"), sem("stk_copied")
        sc_ready, sig_done, pv_done = sem("sc_ready"), sem("sig_done"), sem("pv_done")
        gate_ready, gate_copied, coll_done = sem("gate_ready"), sem("gate_copied"), sem("coll_done")
        wo_ready, xb_ready = sem("wo_ready"), sem("xb_ready")
        y_step, yrstd_ready = sem("y_step"), sem("yrstd_ready")
        x1_ready, r1_ready = sem("x1_ready"), sem("r1_ready")
        xn_step, xrn_ready = sem("xn_step"), sem("xrn_ready")
        xnT_ready, xnT_copied = sem("xnT_ready"), sem("xnT_copied")
        log_ready, log_step = sem("log_ready"), sem("log_step")
        logT_ready, logT_copied = sem("logT_ready"), sem("logT_copied")
        soft_max, soft_exp, soft_post = sem("soft_max"), sem("soft_exp"), sem("soft_post")
        disp_ready, disp_copied = sem("disp_ready"), sem("disp_copied")
        slot_ready, slot_copied = sem("slot_ready"), sem("slot_copied")
        combT_ready, combT_copied = sem("combT_ready"), sem("combT_copied")

        gate_setup, hi_ready = sem("gate_setup"), sem("hi_ready")

        def times(i, base, per_body):
            return base if i is None else i * per_body + base

        def per_slot(i, base, n=1):
            return times(i, base, n * LOOP_SLOTS)

        def per_batch(i, base, n=1):
            return times(i, base, n * LOOP_SLOTS // TC)

        def slots(eng, slot, first, last):
            loop_end = LOOP_FROM + LOOP_SLOTS * LOOP_TIMES
            for s in range(first, LOOP_FROM):
                slot(None, s)
            with eng.Fori(0, LOOP_TIMES) as i:
                for s in range(LOOP_FROM, LOOP_FROM + LOOP_SLOTS):
                    slot(i, s)
            for s in range(loop_end, last + 1):
                slot(None, s)

        def chunk_ok(c):
            return 0 <= c < NCH

        def batch_ok(b):
            return 0 <= b < B

        FIRST, LAST = -10, NCH + 10

        def hold_wait():
            nc.vector.memset(wait_holder[:], 0.0)

        def heads(ap):
            return ap.rearrange("p (h d) -> p h d", d=HD)

        def over(ap, n):
            return ap.unsqueeze(len(ap.shape)).broadcast_to(list(ap.shape) + [n])

        WEIGHTS = 8 + P // HD
        with nc.Block() as block:

            @block.sync
            def _(sp):
                c_eye, c_masks = consts[:, 0:P], consts[:, P:P + 2 + 2 * HD]
                sp.dma_start(ident[:], c_eye).then_inc(const_loaded, 16)
                sp.dma_start(masks[:], c_masks).then_inc(const_loaded, 16)

                def load_x(i, c):
                    k = c % 4
                    if c >= 4:
                        sp.wait_ge(zT_ready, per_slot(i, c - 3))
                    sp.dma_start(xs[:, k, :], x_rows[bass.ds(per_slot(i, c * P, P), P), :]).then_inc(x_loaded[k], 16)

                load_x(None, 0)
                for dst, src in ((wqk[:, :, 0:D], Wq), (wqk[:, :, D:2 * D], Wk)):
                    sp.dma_start(dst, src.rearrange("(k p) n -> p k n", p=P)).then_inc(wqk_loaded, 16)
                for c in range(1, 4):
                    load_x(None, c)

                def slot(i, s):
                    j = s % TC
                    if chunk_ok(s + 10) and s + 10 >= 4:
                        load_x(i, s + 10)
                    c = s - 2
                    if chunk_ok(c):
                        if c >= 4:
                            sp.wait_ge(y_step, per_slot(i, 4 * (c - 4) + 1, 4))
                        sp.dma_start(xr[:, c % 4, :], x_rows[bass.ds(per_slot(i, c * P, P), P), :])\
                            .then_inc(xr_loaded[c % 4], 16)
                    c = s - 6
                    if chunk_ok(c):
                        sp.wait_ge(x1_ready, per_slot(i, 3 * c + 1, 3))
                        sp.dma_start(x1_dram[bass.ds(per_slot(i, c * P, P), P), :], x1[:, c % 2, :])\
                            .then_inc(x1_stored[c % 2], 16)
                    half, b = j - 1, s // TC - 3
                    if j in (1, 2) and batch_ok(b):
                        sp.wait_ge(combT_copied, per_batch(i, 2 * b + half + 1, 2))
                        dst = comb_dram[bass.ds(per_batch(i, b), 1), :, :, half * 2 * P:(half + 1) * 2 * P]
                        sp.dma_start(dst.rearrange("b p k n -> (b p) k n"),
                                     combT[:, half, :].rearrange("p (k n) -> p k n", k=KC))\
                            .then_inc(comb_stored[half], 16)

                slots(sp, slot, FIRST, LAST)
                for k in range(2):
                    sp.wait_ge(x1_stored[k], 16 * NCH // 2)
                for k in range(2):
                    sp.wait_ge(comb_stored[k], 16 * B)

            @block.gpsimd
            def _(pool):
                nc.gpsimd.memset(minus_half[:], -0.5).then_inc(setup_p, 1)
                nc.gpsimd.memset(vpad[:], 0.0).then_inc(setup_p, 1)
                pool.wait_ge(setup_p, 2)

                def power(dst, src, n):
                    return nc.gpsimd.tensor_tensor(dst, src, minus_half[:, 0:n], ALU.pow)

                def slot(i, s):
                    c = s - 5
                    if chunk_ok(c):
                        pool.wait_ge(y_step, per_slot(i, 4 * c + 4, 4))
                        power(yrstd[:, c % 2:c % 2 + 1], yvar[:, c % 2:c % 2 + 1], 1).then_inc(yrstd_ready, 1)
                    c = s + 8
                    if chunk_ok(c):
                        pool.wait_ge(stats, per_slot(i, 3 * c + 3, 3))
                        power(rstd[:, c % 4:c % 4 + 1], var_eps[:, c % 4:c % 4 + 1], 1).then_inc(rstd_ready, 1)
                    if s == -5:
                        pool.wait_ge(mu_squared, 2)
                        power(mu_norm[:, KC:2 * KC], mu_norm[:, 0:KC], KC).then_inc(setup_p, 1)
                    c = s + 6
                    if chunk_ok(c):
                        pool.wait_ge(qk_copied, per_slot(i, c + 1))
                        if c == 0:
                            pool.wait_ge(weight_loaded, 16 * WEIGHTS)
                        if c >= 1:
                            pool.wait_ge(sums_ready, per_slot(i, 2 * (c - 1) + 1, 2))
                        nc.gpsimd.tensor_tensor(sqg[:, 2 * D:3 * D], qk[:, c % 4, D:2 * D], gk_all[:], ALU.mult)\
                            .then_inc(kg_ready, 1)
                    c = s - 5
                    if chunk_ok(c):
                        pool.wait_ge(x1_ready, per_slot(i, 3 * c + 3, 3))
                        power(r1[:, c % 2:c % 2 + 1], v1[:, c % 2, 1:2], 1).then_inc(r1_ready, 1)
                    c = s + 6
                    if chunk_ok(c):
                        pool.wait_ge(sums_ready, per_slot(i, 2 * c + 2, 2))
                        if c >= 2:
                            pool.wait_ge(norm_step, per_slot(i, 2 * (c - 2) + 2, 2))
                        power(rn[:, c % 2, :], sums[:, c % 2, 0:2 * H], 2 * H).then_inc(rn_ready, 1)
                    c = s - 3
                    if chunk_ok(c):
                        pool.wait_ge(xr_loaded[c % 4], per_batch(i, 16 * (c // 4 + 1), 16))
                        nc.gpsimd.tensor_tensor(xr[:, c % 4, :], xr[:, c % 4, :], bo_all[:], ALU.add)\
                            .then_inc(xb_ready, 1)
                    c = s - 5
                    if chunk_ok(c):
                        pool.wait_ge(xn_step, per_slot(i, 4 * c + 4, 4))
                        if c >= 2:
                            pool.wait_ge(log_step, per_slot(i, 3 * (c - 2) + 3, 3))
                        power(xrn[:, c % 2:c % 2 + 1], xss[:, c % 2, 1:2], 1).then_inc(xrn_ready, 1)

                slots(pool, slot, FIRST, LAST)

            @block.scalar
            def _(act):
                for dst, src in ((lnw_col, ln_w), (lnb_col, ln_b)):
                    act.dma_start(dst[:], src.rearrange("(k p) -> p k", p=P), allow_slow_non_contiguous=True)\
                        .then_inc(wqk_loaded, 16)

                def weight(dst, src):
                    act.dma_start(dst, src, allow_slow_non_contiguous=True).then_inc(weight_loaded, 16)

                weight(wv, Wv.rearrange("(k p) n -> p k n", p=P))
                weight(gk_all[:, :].rearrange("p (h d) -> p h d", d=HD),
                       gk.unsqueeze(0).unsqueeze(0).broadcast_to([P, H, HD]))
                for n in range(P // HD):
                    weight(gq_col[n * HD:(n + 1) * HD, 0:1], gq.unsqueeze(1))
                weight(mu_whole, mu.rearrange("(k p) e s -> p k (e s)", p=P))
                weight(scale_col[:], scale.unsqueeze(0).broadcast_to([P, 1]))
                weight(wo[:], Wo.rearrange("(k p) n -> p k n", p=P))
                weight(bo_all[:], bo.unsqueeze(0).broadcast_to([P, D]))
                weight(gamma_all[:], gamma.unsqueeze(0).broadcast_to([P, D]))
                weight(beta_all[:], beta.unsqueeze(0).broadcast_to([P, D]))

                def sigmoid(i, s, k):
                    u = 4 * s + k
                    for t in range(2):
                        act.wait_ge(sc_ready, per_slot(i, 2 * u + t + 1, 8))
                        if t == 0 and u >= 4:
                            act.wait_ge(pv_done, per_slot(i, u - 3, 4))
                        nc.scalar.activation(res[:, k, 2 * t:2 * t + 2, :], score_ps[t][:, :, :], ACT.Sigmoid,
                                             bias=-THRESH * SHARP, scale=SHARP).then_inc(sig_done, 1)

                def slot(i, s):
                    j = s % TC
                    attn = chunk_ok(s)
                    if attn:
                        sigmoid(i, s, 0)
                    b = s // TC - 3
                    if j in (1, 2) and batch_ok(b):
                        half = j - 1
                        act.wait_ge(combT_ready, per_batch(i, 2 * b + half + 1, 2))
                        if b >= 1:
                            act.wait_ge(comb_stored[half], per_batch(i, 16 * b, 16))
                        nc.scalar.activation(combT[:, half, :], b0[:, :], ACT.Copy).then_inc(combT_copied, 1)
                    if j == 0 and batch_ok(b):
                        act.wait_ge(disp_ready, per_batch(i, 2 * b + 2, 2))
                        nc.scalar.activation(disp[:, 2:4, :], b0[:, :].rearrange("p (t n) -> p t n", t=2), ACT.Copy)\
                            .then_inc(disp_copied, 1)
                    if attn and j != 3:
                        sigmoid(i, s, 1)
                    c = s - 6
                    if chunk_ok(c):
                        act.wait_ge(xnT_ready, per_slot(i, c + 1))
                        if c >= 1:
                            act.wait_ge(logT_ready, per_slot(i, c))
                        if c >= 2:
                            act.wait_ge(log_ready, per_slot(i, c - 1))
                        nc.scalar.activation(xnT_hi[:, c % 2, :, :], b0[:, 0:KC * P].rearrange("p (k n) -> p k n", n=P), ACT.Copy)\
                            .then_inc(xnT_copied, 1)
                    c = s - 7
                    if chunk_ok(c):
                        b, t = c // TC, c % TC
                        act.wait_ge(logT_ready, per_slot(i, c + 1))
                        if b >= 2 and t == 0:
                            act.wait_ge(disp_ready, per_batch(i, 2 * (b - 1), 2))
                        nc.scalar.activation(logitT[:, b % 2, :, t * P:(t + 1) * P],
                                             b0[:, KC * P:2 * KC * P].rearrange("p (k n) -> p k n", n=P), ACT.Copy)\
                            .then_inc(logT_copied, 1)
                    if attn and j == 3:
                        sigmoid(i, s, 1)
                    c = s + 6
                    if chunk_ok(c):
                        act.wait_ge(qk_copied, per_slot(i, c + 1))
                        if c >= 1:
                            act.wait_ge(sums_ready, per_slot(i, 2 * (c - 1) + 1, 2))
                        nc.scalar.activation(sqg[:, 0:2 * D], qk[:, c % 4, :], ACT.Square).then_inc(squares_ready, 1)
                    if attn:
                        sigmoid(i, s, 2)
                    c = s + 7
                    if chunk_ok(c):
                        act.wait_ge(v_ready, per_slot(i, c + 1))
                        act.wait_ge(sd_ready, per_slot(i, c + 1))
                        if c >= 4:
                            act.wait_ge(v_gated, per_slot(i, c - 3))
                        nc.scalar.activation(v_raw[:, c % 4, :], f0[:, 0:D], ACT.Copy, scale=sd_v[:, c % 4:c % 4 + 1]).then_inc(v_copied, 1)
                    b = s // TC
                    if attn and j in (0, 2):
                        half = j // 2
                        act.wait_ge(gate_ready, per_batch(i, 2 * b + half + 1, 2))
                        if b >= 1:
                            act.wait_ge(coll_done, per_batch(i, 2 * (b - 1) + half + 1, 2))
                        nc.scalar.activation(gate_q[:, half, :], f1[:, :], ACT.Copy, scale=1.0 / GATE_SCALE)\
                            .then_inc(gate_copied, 1)
                    b = s // TC - 3
                    if batch_ok(b) and j == 1:
                        act.wait_ge(slot_ready, per_batch(i, b + 1))
                        nc.scalar.activation(slotT[:, :, :, bass.ds(per_batch(i, b), 1), :].rearrange("p k e b s -> p k e (b s)"),
                                             f1[:, :].rearrange("p (k e s) -> p k e s", k=KC, s=S), ACT.Copy)\
                            .then_inc(slot_copied, 1)
                    b = s // TC - 2
                    if batch_ok(b) and j == 3:
                        act.wait_ge(disp_ready, per_batch(i, 2 * b + 1, 2))
                        if b >= 1:
                            act.wait_ge(slot_ready, per_batch(i, b))
                        nc.scalar.activation(disp[:, 0:2, :], f1[:, :].rearrange("p (t n) -> p t n", t=2), ACT.Copy)\
                            .then_inc(disp_copied, 1)
                    if attn:
                        sigmoid(i, s, 3)
                    c = s + 8
                    if chunk_ok(c):
                        act.wait_ge(zT_ready, per_slot(i, c + 1))
                        if c >= 2:
                            act.wait_ge(qk_ready, per_slot(i, c - 1))
                        nc.scalar.activation(zT_hi[:, c % 2, :, :], f0[:, 0:KC * P].rearrange("p (k n) -> p k n", n=P), ACT.Copy)\
                            .then_inc(zT_copied, 1)
                    b = s // TC - 2
                    if batch_ok(b) and j == 2:
                        act.wait_ge(log_step, per_batch(i, 3 * TC * (b + 1), 3 * TC))
                        if b >= 2:
                            act.wait_ge(soft_post, per_batch(i, 4 * (b - 1), 4))
                        for t in range(TC):
                            nc.scalar.activation(logit[:, b % 2, t, :], logit[:, b % 2, t, :], ACT.Exp,
                                                 bias=rmax[:, b % 2, t, 1:2], accum_out=csum[:, b % 2, t:t + 1]).then_inc(soft_exp, 1)
                        act.wait_ge(soft_max, per_batch(i, 2 * b + 2, 2))
                        for k in range(KC):
                            nc.scalar.activation(logitT[:, b % 2, k, :], logitT[:, b % 2, k, :], ACT.Exp,
                                                 bias=cmax[:, k:k + 1], accum_out=esum[:, b % 2, k:k + 1]).then_inc(soft_exp, 1)
                slots(act, slot, FIRST, LAST)

            @block.tensor
            def _(pe):
                def setup():
                    pe.wait_ge(setup_v, 3)
                    for k in range(KC):
                        last = nc.tensor.matmul(f1[:, :], lnb_cols[:, k, :], wqk[:, k, :], start=(k == 0), stop=(k == KC - 1))
                    last.then_inc(setup_t, 1)
                    pe.wait_ge(weight_loaded, 16 * WEIGHTS)
                    for k in range(KC):
                        last = nc.tensor.matmul(b0[:, 0:D], ones, wv[:, k, :], start=(k == 0), stop=(k == KC - 1))
                    last.then_inc(setup_t, 1)

                def setup_mu():
                    pe.wait_ge(mu_squared, 1)
                    pe.wait_ge(wv_split, 3)
                    for m in range(KC):
                        for k in range(KC):
                            last = nc.tensor.matmul(b0[:, m:m + 1], logit[:, 0, k, m * P:(m + 1) * P], ones[:, 0:1],
                                                    start=(k == 0), stop=(k == KC - 1))
                    last.then_inc(setup_t, 1)

                def setup_mu_rows():
                    pe.wait_ge(mu_squared, 2 + KC)
                    for m in range(KC):
                        last = nc.tensor.matmul(b0[:, m * P:(m + 1) * P], ones, disp[:, m, 0:P], start=True, stop=True)
                    last.then_inc(setup_t, 1)

                def scores(i, s, k):
                    u = 4 * s + k
                    b, j = s // TC, s % TC
                    half, odd = j // 2, j % 2
                    rows = slice(64 * odd, 64 * odd + 64)
                    if j == 0 and k == 0:
                        pe.wait_ge(stk_copied, per_slot(i, 2 * TC * (b + 1), 2))
                    for t in range(2):
                        if 2 * u + t >= 2:
                            pe.wait_ge(sig_done, per_slot(i, 2 * u + t - 1, 8))
                        for q in (2 * t, 2 * t + 1):
                            pair = 4 * half + q
                            last = nc.tensor.matmul(score_ps[t][:, q % 2, :], stack[rows, b % 2, 1, pair, k * P:(k + 1) * P],
                                                    stack[rows, b % 2, 0, pair, :], start=True, stop=True,
                                                    tile_position=(64 * odd, 0))
                        last.then_inc(sc_ready, 1)

                def weighted_sum(i, s, k):
                    u = 4 * s + k
                    b, j = s // TC, s % TC
                    half, odd = j // 2, j % 2
                    if j == 0 and k == 0:
                        pe.wait_ge(v_gated, per_slot(i, TC * (b + 1)))
                    if odd == 0 and k == 0 and 2 * b + half >= 1:
                        pe.wait_ge(coll_done, per_batch(i, 2 * b + half, 2))
                    pe.wait_ge(sig_done, per_slot(i, 2 * u + 2, 8))
                    for q in range(QUADS):
                        pair = 4 * half + q
                        last = nc.tensor.matmul(coll_ps[32 * q:32 * q + 32, :],
                                                vpad[:, b % 2, k, pair, HD * odd:HD * odd + 2 * HD], res[:, k, q, :],
                                                start=(odd == 0 and k == 0), stop=(odd == 1 and k == TC - 1),
                                                tile_position=(0, 32 * q))
                    last.then_inc(pv_done, 1)

                def misc_emptied(i, s):
                    b, j = s // TC, s % TC
                    if chunk_ok(s) and j in (0, 2):
                        pe.wait_ge(gate_copied, per_batch(i, 2 * b + j // 2 + 1, 2))
                    if j == 1 and batch_ok(b - 3):
                        pe.wait_ge(slot_copied, per_batch(i, b - 3 + 1))
                    if j == 3 and batch_ok(b - 2):
                        pe.wait_ge(disp_copied, per_batch(i, 2 * (b - 2) + 1, 2))

                def misc_may_start(i, s):
                    if chunk_ok(s + 4):
                        pe.wait_ge(stk_copied, per_slot(i, 2 * (s + 4) + 2, 2))
                    else:
                        misc_emptied(i, s - 1)
                        misc_emptied(i, s - 2)

                def stacks(i, c):
                    pe.wait_ge(hl_ready, per_slot(i, 3 * c + 3, 3))
                    for side, bank in ((0, f0h), (1, f1h)):
                        if side == 0:
                            if c + 3 < NCH:
                                pe.wait_ge(zT_split, per_slot(i, c + 4))
                            elif c + 3 == NCH:
                                pe.wait_ge(v_copied, NCH)
                            else:
                                pe.wait_ge(stk_copied, per_slot(i, 2 * (c - 1) + 1, 2))
                        else:
                            if c + 2 < NCH:
                                pe.wait_ge(qk_copied, per_slot(i, c + 3))
                            else:
                                misc_emptied(i, c - 5)
                        for pair in range(PAIRS):
                            parts = hl[:, c % 2, side * H + 2 * pair:side * H + 2 * pair + 2, :, :].rearrange("p h a d -> p (h a d)")
                            last = nc.tensor.transpose(bank[:, pair * P:(pair + 1) * P], parts, ident16[:])
                        last.then_inc(stk_ready, 1)

                def transposes(i, c):
                    pe.wait_ge(z_ready, per_slot(i, c + 1))
                    if c == 0:
                        pe.wait_ge(const_loaded, 32)
                    if c >= 1:
                        pe.wait_ge(v_copied, per_slot(i, c))
                    for k in range(KC):
                        last = nc.tensor.transpose(f0[:, k * P:(k + 1) * P], z[:, c % 2, k * P:(k + 1) * P], ident[:])
                    last.then_inc(zT_ready, 1)

                def split_matmuls(dst, hi, lo, w_hi, w_lo):
                    for k in range(KC):
                        for n, (a, w) in enumerate(((hi, w_hi), (hi, w_lo), (lo, w_hi))):
                            last = nc.tensor.matmul(dst, a[:, k, :], w[:, k, :], start=(k == 0 and n == 0),
                                                    stop=(k == KC - 1 and n == 2))
                    return last

                def project_v(i, c):
                    pe.wait_ge(zT_split, per_slot(i, c + 1))
                    if c == 0:
                        pe.wait_ge(wv_split, 3)
                    if chunk_ok(c - 3):
                        pe.wait_ge(stk_copied, per_slot(i, 2 * (c - 3) + 1, 2))
                    split_matmuls(f0[:, 0:D], zT_hi[:, c % 2, :, :], zT_lo[:, c % 2, :, :], wv_hi, wv_lo).then_inc(v_ready, 1)

                def project_qk(i, s, c):
                    if c == 0:
                        pe.wait_ge(wqk_split, 4)
                        pe.wait_ge(setup_v, 4)
                    if chunk_ok(s + 4):
                        pe.wait_ge(stk_copied, per_slot(i, 2 * (s + 4) + 2, 2))
                    elif c >= 1:
                        pe.wait_ge(qk_copied, per_slot(i, c))
                    misc_emptied(i, s)
                    split_matmuls(f1[:, :], zT_hi[:, c % 2, :, :], zT_lo[:, c % 2, :, :], wqk_hi, wqk_lo).then_inc(qk_ready, 1)

                def gates(i, s):
                    b, half = s // TC, s % TC // 2
                    misc_may_start(i, s)
                    if half == 0:
                        pe.wait_ge(stk_copied, per_slot(i, 2 * TC * (b + 1), 2))
                    for q in range(QUADS):
                        last = nc.tensor.matmul(f1[32 * q:32 * q + 32, :], gate_w[:], stack[:, b % 2, 0, 4 * half + q, :],
                                                start=True, stop=True, tile_position=(0, 32 * q))
                    last.then_inc(gate_ready, 1)

                def output_projection(i, c):
                    b, j = c // TC, c % TC
                    if j == 0:
                        pe.wait_ge(coll_done, per_batch(i, 2 * b + 2, 2))
                    if chunk_ok(c - 2):
                        pe.wait_ge(log_step, per_slot(i, 3 * (c - 2) + 3, 3))
                    elif c == 0:
                        pe.wait_ge(mu_split, 3)
                    elif c == 1:
                        pe.wait_ge(y_step, 1)
                    for k in range(KC):
                        last = nc.tensor.matmul(b0[:, 0:D], coll[:, b % 2, k, j * P:(j + 1) * P], wo[:, k, :],
                                                start=(k == 0), stop=(k == KC - 1))
                    last.then_inc(wo_ready, 1)

                def b0_emptied(i, s):
                    b, j = s // TC - 3, s % TC
                    if chunk_ok(s - 5):
                        pe.wait_ge(y_step, per_slot(i, 4 * (s - 5) + 1, 4))
                    elif chunk_ok(s - 7):
                        pe.wait_ge(log_step, per_slot(i, 3 * (s - 7) + 3, 3))
                    elif chunk_ok(s - 8):
                        pe.wait_ge(logT_copied, per_slot(i, s - 7))
                    if j in (1, 2) and batch_ok(b):
                        pe.wait_ge(combT_copied, per_batch(i, 2 * b + j, 2))
                    if j == 0 and batch_ok(b):
                        pe.wait_ge(disp_copied, per_batch(i, 2 * b + 2, 2))

                def transpose_xn_and_logits(i, s):
                    b0_emptied(i, s)
                    c = s - 6
                    if chunk_ok(c):
                        pe.wait_ge(xn_step, per_slot(i, 4 * c + 2, 4))
                        for k in range(KC):
                            last = nc.tensor.transpose(b0[:, k * P:(k + 1) * P], xn[:, c // TC % 2, c % TC, k * P:(k + 1) * P], ident[:])
                        last.then_inc(xnT_ready, 1)
                    c = s - 7
                    if chunk_ok(c):
                        pe.wait_ge(log_step, per_slot(i, 3 * c + 3, 3))
                        for k in range(KC):
                            last = nc.tensor.transpose(b0[:, (KC + k) * P:(KC + k + 1) * P],
                                                       logit[:, c // TC % 2, c % TC, k * P:(k + 1) * P], ident[:])
                        last.then_inc(logT_ready, 1)

                def logits(i, c):
                    pe.wait_ge(xnT_split, per_slot(i, c + 1))
                    if c >= 1:
                        pe.wait_ge(logT_copied, per_slot(i, c))
                    last = split_matmuls(b0[:, 0:ES], xnT_hi[:, c % 2, :, :], xnT_lo[:, c % 2, :, :], mu_hi, mu_lo)
                    last.then_inc(log_ready, 1)

                def b0_emptied_first(i, s):
                    if chunk_ok(s - 5):
                        pe.wait_ge(y_step, per_slot(i, 4 * (s - 5) + 1, 4))
                    elif chunk_ok(s - 7):
                        pe.wait_ge(log_step, per_slot(i, 3 * (s - 7) + 3, 3))
                    elif chunk_ok(s - 8):
                        pe.wait_ge(logT_copied, per_slot(i, s - 7))
                    elif s % TC == 1:
                        pe.wait_ge(disp_copied, 2 * (s // TC - 3) + 2)
                    elif s % TC == 2:
                        pe.wait_ge(combT_copied, 2 * (s // TC - 3) + 1)

                def transpose_combine(i, s, b, half):
                    pe.wait_ge(soft_exp, per_batch(i, 6 * b + TC, 6))
                    b0_emptied_first(i, s)
                    for k in range(KC):
                        for t in range(2):
                            last = nc.tensor.transpose(b0[:, (2 * k + t) * P:(2 * k + t + 1) * P],
                                                       logit[:, b % 2, 2 * half + t, k * P:(k + 1) * P], ident[:])
                    last.then_inc(combT_ready, 1)

                def transpose_dispatch(i, s, b, half):
                    pe.wait_ge(soft_post, per_batch(i, 4 * b + 3, 4))
                    if half == 1:
                        bank = b0
                        b0_emptied_first(i, s)
                    else:
                        bank = f1
                        misc_may_start(i, s)
                    for t in range(2):
                        for k in range(KC):
                            n = 2 * half + t
                            last = nc.tensor.transpose(bank[:, (t * KC + k) * P:(t * KC + k + 1) * P],
                                                       logitT[:, b % 2, k, n * P:(n + 1) * P], ident[:])
                    last.then_inc(disp_ready, 1)

                def slot_inputs(i, s, b):
                    pe.wait_ge(disp_copied, per_batch(i, 2 * b + 2, 2))
                    misc_may_start(i, s)
                    for k in range(KC):
                        for t in range(TC):
                            last = nc.tensor.matmul(f1[:, k * ES:(k + 1) * ES], xn[:, b % 2, t, k * P:(k + 1) * P], disp[:, t, :],
                                                    start=(t == 0), stop=(t == TC - 1))
                    last.then_inc(slot_ready, 1)

                def slot(i, s):
                    b, j = s // TC, s % TC
                    attn = chunk_ok(s)
                    if s == -8:
                        setup()
                    if s == -6:
                        setup_mu()
                    if s == -3:
                        setup_mu_rows()
                    if attn:
                        scores(i, s, 0)
                    if j in (1, 2) and batch_ok(b - 3):
                        transpose_combine(i, s, b - 3, j - 1)
                    if j == 0 and batch_ok(b - 3):
                        transpose_dispatch(i, s, b - 3, 1)
                    if chunk_ok(s - 1):
                        weighted_sum(i, s - 1, 2)
                    if attn and j != 3:
                        scores(i, s, 1)
                    if chunk_ok(s - 1):
                        weighted_sum(i, s - 1, 3)
                    if chunk_ok(s - 6) or chunk_ok(s - 7):
                        transpose_xn_and_logits(i, s)
                    if chunk_ok(s + 4):
                        stacks(i, s + 4)
                    if attn and j == 3:
                        scores(i, s, 1)
                    if attn:
                        scores(i, s, 2)
                    if chunk_ok(s + 7):
                        project_v(i, s + 7)
                    if chunk_ok(s - 6):
                        logits(i, s - 6)
                    if attn and j in (0, 2):
                        gates(i, s)
                    if j == 1 and batch_ok(b - 3):
                        slot_inputs(i, s, b - 3)
                    if j == 3 and batch_ok(b - 2):
                        transpose_dispatch(i, s, b - 2, 0)
                    if attn:
                        weighted_sum(i, s, 0)
                    if attn:
                        scores(i, s, 3)
                    if chunk_ok(s + 8):
                        transposes(i, s + 8)
                    if chunk_ok(s + 7):
                        project_qk(i, s, s + 7)
                    if attn:
                        weighted_sum(i, s, 1)
                    if chunk_ok(s - 4):
                        output_projection(i, s - 4)

                slots(pe, slot, FIRST, LAST)

            @block.vector
            def _(dve):
                def setup():
                    nc.vector.memset(ones, 1.0).then_inc(setup_v, 1)
                    dve.wait_ge(const_loaded, 32)
                    nc.vector.tensor_copy(ident16[:], ident[:]).then_inc(setup_v, 1)
                    dve.wait_ge(wqk_loaded, 64)
                    nc.vector.tensor_copy(lnb_cols, over(lnb_col[:, :], P)).then_inc(setup_v, 1)
                    nc.vector.tensor_scalar(lnw_scaled[:], lnw_col[:], W_SCALE, None, ALU.mult).then_inc(lnw_ready, 1)
                    dve.wait_ge(lnw_ready, 1)
                    for k in range(KC):
                        nc.vector.tensor_scalar(wqk_hi[:, k, :], wqk[:, k, :], lnw_scaled[:, k:k + 1], None, ALU.mult)\
                            .then_inc(wqk_split, 1)
                    for k in range(KC):
                        dve.wait_ge(wqk_split, k + 1)
                        nc.vector.scalar_tensor_tensor(out=wqk_lo[:, k, :], in0=wqk[:, k, :], scalar=lnw_scaled[:, k:k + 1],
                                                       in1=wqk_hi[:, k, :], op0=ALU.mult, op1=ALU.subtract).then_inc(wqk_split, 1)
                    dve.wait_ge(setup_t, 1)
                    nc.vector.tensor_copy(qk_bias[:], f1[:, :]).then_inc(setup_v, 1)
                    dve.wait_ge(weight_loaded, 16 * WEIGHTS)
                    nc.vector.tensor_scalar(wv_hi[:], wv, W_SCALE, None, ALU.mult).then_inc(wv_split, 1)
                    dve.wait_ge(wv_split, 1)
                    nc.vector.scalar_tensor_tensor(out=wv_lo[:], in0=wv, scalar=W_SCALE, in1=wv_hi[:],
                                                   op0=ALU.mult, op1=ALU.subtract).then_inc(wv_split, 1)
                    dve.wait_ge(setup_t, 2)
                    nc.vector.tensor_copy(wv_sum[:], b0[:, 0:D]).then_inc(wv_split, 1)
                    nc.vector.tensor_tensor(logit[:, 0, 0:KC, :], mu_whole, mu_whole, ALU.mult).then_inc(mu_squared, 1)

                def setup_gate():
                    nc.vector.tensor_scalar(gq_col[:, 1:2], gq_col[:, 0:1], GATE_SCALE, None, ALU.mult).then_inc(gate_setup, 1)
                    dve.wait_ge(gate_setup, 1)
                    nc.vector.tensor_copy(gq_hi16[:], gq_col[:, 1:2]).then_inc(gate_setup, 1)
                    dve.wait_ge(gate_setup, 2)
                    nc.vector.tensor_tensor(gq_col[:, 2:3], gq_col[:, 1:2], gq_hi16[:], ALU.subtract).then_inc(gate_setup, 1)
                    nc.vector.tensor_tensor(gq_col[:, 3:4], gq_hi16[:], masks[:, 0:1], ALU.mult).then_inc(gate_setup, 1)
                    dve.wait_ge(gate_setup, 4)
                    nc.vector.scalar_tensor_tensor(out=gq_col[:, 0:1], in0=gq_col[:, 2:3], scalar=masks[:, 1:2],
                                                   in1=gq_col[:, 3:4], op0=ALU.mult, op1=ALU.add).then_inc(gate_setup, 1)
                    dve.wait_ge(gate_setup, 5)
                    nc.vector.tensor_scalar(gate_w[:], masks[:, 2:2 + 2 * HD], gq_col[:, 0:1], None, ALU.mult)\
                        .then_inc(gate_setup, 1)

                def setup_mu():
                    dve.wait_ge(setup_t, 3)
                    nc.vector.tensor_scalar(mu_norm[:, 0:KC], b0[:, 0:KC], NORM_EPS * NORM_EPS, None, ALU.max)\
                        .then_inc(mu_squared, 1)

                def setup_mu_diag():
                    dve.wait_ge(setup_p, 3)
                    for k in range(KC):
                        nc.vector.tensor_scalar(disp[:, k, 0:P], ident[:], mu_norm[:, KC + k:KC + k + 1], W_SCALE, ALU.mult, ALU.mult)\
                            .then_inc(mu_squared, 1)

                def split_mu():
                    dve.wait_ge(setup_t, 4)
                    nc.vector.scalar_tensor_tensor(out=mu_whole, in0=mu_whole, scalar=scale_col[:, 0:1],
                                                   in1=b0[:, 0:ES].unsqueeze(1).broadcast_to([P, KC, ES]),
                                                   op0=ALU.mult, op1=ALU.mult).then_inc(mu_split, 1)
                    dve.wait_ge(mu_split, 1)
                    nc.vector.tensor_copy(mu_hi[:], mu_whole).then_inc(mu_split, 1)
                    dve.wait_ge(mu_split, 2)
                    nc.vector.tensor_tensor(mu_lo[:], mu_whole, mu_hi[:], ALU.subtract).then_inc(mu_split, 1)

                def row_stats(i, c):
                    dve.wait_ge(x_loaded[c % 4], times(i, 16 * (c // 4 + 1), 32))
                    nc.vector.bn_stats(bn[:, c % 2, :], xs[:, c % 4, :]).then_inc(stats, 1)
                    dve.wait_ge(stats, per_slot(i, 3 * c + 1, 3))
                    hold_wait()
                    nc.vector.bn_aggr(mv[:, c % 4, :], bn[:, c % 2, :]).then_inc(stats, 1)
                    dve.wait_ge(stats, per_slot(i, 3 * c + 2, 3))
                    nc.vector.tensor_scalar(var_eps[:, c % 4:c % 4 + 1], mv[:, c % 4, 1:2], LN_EPS, None, ALU.add)\
                        .then_inc(stats, 1)

                def normalise(i, c):
                    dve.wait_ge(rstd_ready, per_slot(i, c + 1))
                    if c >= 2:
                        dve.wait_ge(zT_ready, per_slot(i, c - 1))
                    nc.vector.tensor_scalar(z[:, c % 2, :], xs[:, c % 4, :], mv[:, c % 4, 0:1], rstd[:, c % 4:c % 4 + 1],
                                            ALU.subtract, ALU.mult).then_inc(z_ready, 1)
                    if c >= 4:
                        dve.wait_ge(v_copied, per_slot(i, c - 3))
                    nc.vector.tensor_scalar(sd_v[:, c % 4:c % 4 + 1], var_eps[:, c % 4:c % 4 + 1], rstd[:, c % 4:c % 4 + 1],
                                            1.0 / W_SCALE, ALU.mult, ALU.mult).then_inc(sd_ready, 1)

                def split_zT(i, c):
                    dve.wait_ge(zT_copied, per_slot(i, c + 1))
                    nc.vector.tensor_tensor(zT_lo[:, c % 2, :, :], f0[:, 0:KC * P].rearrange("p (k n) -> p k n", n=P),
                                            zT_hi[:, c % 2, :, :], ALU.subtract).then_inc(zT_split, 1)

                def shift_values(i, c):
                    dve.wait_ge(v_copied, per_slot(i, c + 1))
                    nc.vector.scalar_tensor_tensor(out=v_raw[:, c % 4, :], in0=wv_sum[:], scalar=mv[:, c % 4, 0:1],
                                                   in1=v_raw[:, c % 4, :], op0=ALU.mult, op1=ALU.add).then_inc(v_shifted, 1)

                def copy_stacks(i, c):
                    b, j = c // TC, c % TC
                    if b >= 2 and j == 0:
                        dve.wait_ge(sc_ready, per_slot(i, 8 * TC * (b - 1), 8))
                        dve.wait_ge(gate_ready, per_batch(i, 2 * (b - 1), 2))
                    for side, bank in ((0, f0h), (1, f1h)):
                        dve.wait_ge(stk_ready, per_slot(i, 2 * c + side + 1, 2))
                        nc.vector.tensor_copy(stack[:, b % 2, side, :, j * P:(j + 1) * P],
                                              bank.rearrange("p (a n) -> p a n", n=P)).then_inc(stk_copied, 1)

                def add_qk_bias(i, c):
                    dve.wait_ge(qk_ready, per_slot(i, c + 1))
                    if c >= 4:
                        dve.wait_ge(squares_ready, per_slot(i, c - 3))
                        dve.wait_ge(kg_ready, per_slot(i, c - 3))
                    nc.vector.scalar_tensor_tensor(out=qk[:, c % 4, :], in0=f1[:, :], scalar=1.0 / W_SCALE, in1=qk_bias[:],
                                                   op0=ALU.mult, op1=ALU.add).then_inc(qk_copied, 1)

                def sum_squares(i, c):
                    dve.wait_ge(squares_ready, per_slot(i, c + 1))
                    dve.wait_ge(kg_ready, per_slot(i, c + 1))
                    if c >= 2:
                        dve.wait_ge(rn_ready, per_slot(i, c - 1))
                    nc.vector.tensor_reduce(sums[:, c % 2, :], heads(sqg[:, :]), AX_X, ALU.add).then_inc(sums_ready, 1)
                    dve.wait_ge(sums_ready, per_slot(i, 2 * c + 1, 2))
                    nc.vector.tensor_scalar(sums[:, c % 2, 0:2 * H], sums[:, c % 2, 0:2 * H], NORM_EPS * NORM_EPS, None, ALU.max)\
                        .then_inc(sums_ready, 1)

                def split_qk(i, c):
                    dve.wait_ge(rn_ready, per_slot(i, c + 1))
                    nc.vector.tensor_tensor(heads(qn[:, :]), heads(qk[:, c % 4, :]), over(rn[:, c % 2, :], HD), ALU.mult)\
                        .then_inc(norm_step, 1)
                    if c >= 2:
                        dve.wait_ge(v_gated, per_slot(i, c - 1))
                    nc.vector.tensor_tensor(gate_k[:, c % 2, :], sums[:, c % 2, 2 * H:3 * H], rn[:, c % 2, H:2 * H], ALU.mult)\
                        .then_inc(norm_step, 1)
                    if c >= 2:
                        dve.wait_ge(stk_ready, per_slot(i, 2 * (c - 2) + 2, 2))
                    dve.wait_ge(norm_step, per_slot(i, 2 * c + 2, 2))
                    nc.vector.tensor_copy(hl[:, c % 2, :, 0, :], heads(qn[:, :])).then_inc(hi_ready, 1)
                    dve.wait_ge(hi_ready, per_slot(i, 2 * c + 1, 2))
                    nc.vector.tensor_tensor(hl[:, c % 2, :, 3, :], heads(qn[:, :]), hl[:, c % 2, :, 0, :], ALU.subtract)\
                        .then_inc(hi_ready, 1)
                    dve.wait_ge(hi_ready, per_slot(i, 2 * c + 2, 2))
                    nc.vector.tensor_copy(hl[:, c % 2, 0:H, 1:3, :], hl[:, c % 2, 0:H, 0:4:3, :]).then_inc(hl_ready, 1)
                    nc.vector.tensor_copy(hl[:, c % 2, H:2 * H, 1, :], hl[:, c % 2, H:2 * H, 3, :]).then_inc(hl_ready, 1)
                    nc.vector.tensor_copy(hl[:, c % 2, H:2 * H, 2, :], hl[:, c % 2, H:2 * H, 0, :]).then_inc(hl_ready, 1)

                def gate_values(i, c):
                    b, j = c // TC, c % TC
                    dve.wait_ge(norm_step, per_slot(i, 2 * c + 2, 2))
                    dve.wait_ge(v_shifted, per_slot(i, c + 1))
                    if c == 0:
                        dve.wait_ge(setup_p, 2)
                    if b >= 2 and j == 0:
                        dve.wait_ge(pv_done, per_slot(i, 4 * TC * (b - 1), 4))
                    nc.vector.tensor_tensor(vpad[:, b % 2, j, :, :].rearrange("p a (o d) -> p a o d", d=HD)[:, :, 0:3:2, :],
                                            v_raw[:, c % 4, :].rearrange("p (a o d) -> p a o d", o=2, d=HD),
                                            over(gate_k[:, c % 2, :].rearrange("p (a o) -> p a o", o=2), HD), ALU.mult)\
                        .then_inc(v_gated, 1)

                def gate_sums(i, b, half):
                    dve.wait_ge(pv_done, per_batch(i, 4 * (TC * b + 2 * half + 2), 4 * TC))
                    dve.wait_ge(gate_copied, per_batch(i, 2 * b + half + 1, 2))
                    if b >= 2:
                        dve.wait_ge(wo_ready, per_batch(i, TC * (b - 1), TC))
                    nc.vector.tensor_tensor(coll[:, b % 2, half, :], coll_ps[:, :], gate_q[:, half, :], ALU.mult)\
                        .then_inc(coll_done, 1)

                def residual(i, c):
                    dve.wait_ge(wo_ready, per_slot(i, c + 1))
                    dve.wait_ge(xb_ready, per_slot(i, c + 1))
                    nc.vector.tensor_tensor(y[:, c % 2, :], b0[:, 0:D], xr[:, c % 4, :], ALU.add).then_inc(y_step, 1)
                    dve.wait_ge(y_step, per_slot(i, 4 * c + 1, 4))
                    nc.vector.bn_stats(ybn[:, c % 2, :], y[:, c % 2, :]).then_inc(y_step, 1)
                    dve.wait_ge(y_step, per_slot(i, 4 * c + 2, 4))
                    hold_wait()
                    nc.vector.bn_aggr(ymv[:, c % 2, :], ybn[:, c % 2, :]).then_inc(y_step, 1)
                    dve.wait_ge(y_step, per_slot(i, 4 * c + 3, 4))
                    nc.vector.tensor_scalar(yvar[:, c % 2:c % 2 + 1], ymv[:, c % 2, 1:2], LN_EPS, None, ALU.add).then_inc(y_step, 1)

                def first_norm(i, c):
                    dve.wait_ge(yrstd_ready, per_slot(i, c + 1))
                    if c >= 2:
                        dve.wait_ge(x1_stored[c % 2], times(i, 16 * (c // 2), 16 * LOOP_SLOTS // 2))
                    rs = yrstd[:, c % 2:c % 2 + 1]
                    nc.vector.tensor_scalar(x1[:, c % 2, :], y[:, c % 2, :], ymv[:, c % 2, 0:1], rs, ALU.subtract, ALU.mult)\
                        .then_inc(x1_ready, 1)
                    nc.vector.tensor_scalar(v1[:, c % 2, 0:1], ymv[:, c % 2, 1:2], rs, rs, ALU.mult, ALU.mult).then_inc(x1_ready, 1)
                    dve.wait_ge(x1_ready, per_slot(i, 3 * c + 2, 3))
                    nc.vector.tensor_scalar(v1[:, c % 2, 1:2], v1[:, c % 2, 0:1], LN_EPS, None, ALU.add).then_inc(x1_ready, 1)

                def second_norm(i, c):
                    b, j = c // TC, c % TC
                    dve.wait_ge(r1_ready, per_slot(i, c + 1))
                    nc.vector.scalar_tensor_tensor(out=xg[:], in0=x1[:, c % 2, :], scalar=r1[:, c % 2:c % 2 + 1], in1=gamma_all[:],
                                                   op0=ALU.mult, op1=ALU.mult).then_inc(xn_step, 1)
                    dve.wait_ge(xn_step, per_slot(i, 4 * c + 1, 4))
                    if b >= 2 and j == 0:
                        dve.wait_ge(slot_ready, per_batch(i, b - 1))
                    nc.vector.tensor_tensor(xn[:, b % 2, j, :], xg[:], beta_all[:], ALU.add).then_inc(xn_step, 1)
                    dve.wait_ge(xn_step, per_slot(i, 4 * c + 2, 4))
                    nc.vector.tensor_tensor_reduce(xg[:], xn[:, b % 2, j, :], xn[:, b % 2, j, :], 1.0, 0.0, ALU.mult, ALU.add,
                                                   xss[:, c % 2, 0:1]).then_inc(xn_step, 1)
                    dve.wait_ge(xn_step, per_slot(i, 4 * c + 3, 4))
                    nc.vector.tensor_scalar(xss[:, c % 2, 1:2], xss[:, c % 2, 0:1], NORM_EPS * NORM_EPS,
                                            W_SCALE * W_SCALE, ALU.max, ALU.mult)\
                        .then_inc(xn_step, 1)

                def split_xnT(i, c):
                    dve.wait_ge(xnT_copied, per_slot(i, c + 1))
                    if c >= 1:
                        dve.wait_ge(logT_copied, per_slot(i, c))
                    nc.vector.tensor_tensor(xnT_lo[:, c % 2, :, :], b0[:, 0:KC * P].rearrange("p (k n) -> p k n", n=P),
                                            xnT_hi[:, c % 2, :, :], ALU.subtract).then_inc(xnT_split, 1)

                def scale_logits(i, c):
                    b, t = c // TC, c % TC
                    dve.wait_ge(log_ready, per_slot(i, c + 1))
                    dve.wait_ge(xrn_ready, per_slot(i, c + 1))
                    nc.vector.tensor_reduce(rmax[:, b % 2, t, 0:1], b0[:, 0:ES], AX_X, ALU.max).then_inc(log_step, 1)
                    if b >= 2 and t == 0:
                        dve.wait_ge(combT_ready, per_batch(i, 2 * (b - 1), 2))
                    nc.vector.tensor_scalar(logit[:, b % 2, t, :], b0[:, 0:ES], xrn[:, c % 2:c % 2 + 1], None, ALU.mult)\
                        .then_inc(log_step, 1)
                    dve.wait_ge(log_step, per_slot(i, 3 * c + 1, 3))
                    nc.vector.tensor_scalar(rmax[:, b % 2, t, 1:2], rmax[:, b % 2, t, 0:1], xrn[:, c % 2:c % 2 + 1], -1.0,
                                            ALU.mult, ALU.mult).then_inc(log_step, 1)

                def column_max(i, b):
                    dve.wait_ge(logT_copied, per_batch(i, TC * (b + 1), TC))
                    if b >= 1:
                        dve.wait_ge(soft_exp, per_batch(i, 6 * b, 6))
                    nc.vector.tensor_reduce(cmax[:], logitT[:, b % 2, :, :], AX_X, ALU.max).then_inc(soft_max, 1)
                    dve.wait_ge(soft_max, per_batch(i, 2 * b + 1, 2))
                    nc.vector.tensor_scalar(cmax[:], cmax[:], -1.0, None, ALU.mult).then_inc(soft_max, 1)

                def normalise_dispatch(i, b):
                    dve.wait_ge(soft_exp, per_batch(i, 6 * (b + 1), 6))
                    nc.vector.reciprocal(esum[:, b % 2, :], esum[:, b % 2, :]).then_inc(soft_post, 1)
                    dve.wait_ge(soft_post, per_batch(i, 4 * b + 1, 4))
                    for k in range(KC):
                        nc.vector.tensor_scalar(logitT[:, b % 2, k, :], logitT[:, b % 2, k, :], esum[:, b % 2, k:k + 1], None, ALU.mult)\
                            .then_inc(soft_post, 1)
                    nc.vector.reciprocal(crec[:, bass.ds(per_batch(i, TC * b, TC), TC)], csum[:, b % 2, :]).then_inc(soft_post, 1)

                def slot(i, s):
                    b, j = s // TC, s % TC
                    if chunk_ok(s + 6):
                        add_qk_bias(i, s + 6)
                        shift_values(i, s + 6)
                    if chunk_ok(s + 8):
                        row_stats(i, s + 8)
                    if chunk_ok(s - 5):
                        first_norm(i, s - 5)
                    if chunk_ok(s + 7):
                        split_zT(i, s + 7)
                    if s == -8:
                        normalise(i, 0)
                        setup()
                    if s == -6:
                        setup_gate()
                        setup_mu()
                    if j == 2 and batch_ok(b):
                        gate_sums(i, b, 0)
                    if j == 0 and batch_ok(b - 1):
                        gate_sums(i, b - 1, 1)
                    if chunk_ok(s + 4):
                        copy_stacks(i, s + 4)
                    if chunk_ok(s - 6):
                        split_xnT(i, s - 6)
                    if j == 3 and batch_ok(b - 2):
                        normalise_dispatch(i, b - 2)
                    if chunk_ok(s + 6):
                        sum_squares(i, s + 6)
                    if chunk_ok(s + 4):
                        gate_values(i, s + 4)
                    if chunk_ok(s + 8) and s > -8:
                        normalise(i, s + 8)
                    if j == 2 and batch_ok(b - 2):
                        column_max(i, b - 2)
                    if chunk_ok(s + 5):
                        split_qk(i, s + 5)
                    if chunk_ok(s - 6):
                        scale_logits(i, s - 6)
                    if chunk_ok(s - 5):
                        second_norm(i, s - 5)
                    if chunk_ok(s - 4):
                        residual(i, s - 4)
                    if s == -4:
                        setup_mu_diag()
                    if s == -3:
                        split_mu()

                slots(dve, slot, FIRST, LAST)


        M = B * S // P
        EP = E // 2
        b1_col = sb("b1_col", [P, EP])
        res_flat = res[:, :, :, :].rearrange("p a q t -> p (a q t)")
        b2_all = res_flat[:, 0:E * D].rearrange("p (e d) -> p e d", e=E)
        slot_out = res_flat[:, E * D:E * D + 4 * M * D].rearrange("p (r m d) -> p r m d", r=4, m=M)
        out_sb = res_flat[:, E * D + 4 * M * D:E * D + 4 * M * D + 2 * TC * D].rearrange("p (a t d) -> p a t d", a=2, t=TC)
        stack_flat = stack[:, :, :, :, :].rearrange("p a b c t -> p (a b c t)").bitcast(F32)
        hidden = stack_flat[:, 0:EP * B * S].rearrange("p (a n) -> p a n", a=EP)
        at = EP * B * S
        x1_sb = stack_flat[:, at:at + 2 * TC * D].rearrange("p (a t d) -> p a t d", a=2, t=TC)
        at += 2 * TC * D
        comb_sb = stack_flat[:, at:at + 2 * KC * T].rearrange("p (a k n) -> p a k n", a=2, k=KC)
        at += 2 * KC * T
        w1s = stack_flat[:, at:at + KC * E * HF].rearrange("p (k e h) -> p k e h", k=KC, e=E)
        w2s = vpad[:, :, :, :, :].rearrange("p a t c d -> p (a t c d)")[:, 0:EP * D].rearrange("p (a d) -> p a d", a=EP)
        so_sb = coll[:, :, :, :].rearrange("p a b t -> p (a b t)")[:, 0:2 * KC * D].rearrange("p (a k d) -> p a k d", a=2, k=KC)
        y2 = qk[:, :, :].rearrange("p a n -> p (a n)").rearrange("p (a t d) -> p a t d", a=2, t=TC)
        crec4 = sb("crec4", [P, 2, TC])
        obn = sb("obn", [P, 2, TC, 6])
        omv = sb("omv", [P, 2, TC, 2])
        ovar, orstd, oshift = sb("ovar", [P, 2, TC]), sb("orstd", [P, 2, TC]), sb("oshift", [P, 2, 2, TC])

        expert_loaded, b2_loaded = sem("expert_loaded"), sem("b2_loaded")
        h_ready, h_done, so_ready, so_done = sem("h_ready"), sem("h_done"), sem("so_ready"), sem("so_done")
        so_stored = [sem(f"so_stored{k}") for k in range(4)]
        xc_loaded = [sem(f"xc_loaded{k}") for k in range(2)]
        so_loaded = [sem(f"so_loaded{k}") for k in range(2)]
        comb_ready_ps, y2_step, oagg = sem("comb_ready_ps"), sem("y2_step"), sem("oagg")
        ostat_ready, out_ready = sem("ostat_ready"), sem("out_ready")
        crec_copied, obn_ready, omv_ready = sem("crec_copied"), sem("obn_ready"), sem("omv_ready")
        out_stored = [sem(f"out_stored{k}") for k in range(2)]

        def batches(eng, batch):
            batch(None, 0)
            batch(None, 1)
            with eng.Fori(0, B // 2 - 1) as i:
                batch(i, 2)
                batch(i, 3)

        h_ps = [f0, f1]
        out_ps = [[score_ps[0][:, 0, :], score_ps[0][:, 1, :], score_ps[1][:, 0, :], score_ps[1][:, 1, :]],
                  [coll_ps[:, :], f0[:, :], f1[:, :], b0[:, :]]]
        so_ps = [score_ps[0][:, 0, :], score_ps[0][:, 1, :], score_ps[1][:, 0, :], score_ps[1][:, 1, :]]

        with nc.Block() as block:

            @block.sync
            def _(sp):
                for k in range(KC):
                    sp.dma_start(w1s[:, k, :, :], w1.rearrange("e (k p) h -> k p e h", p=P)[k]).then_inc(expert_loaded, 16)
                for i in range(2):
                    rows = slice(HF * i, HF * i + HF)
                    sp.dma_start(b1_col[rows, :], b1.rearrange("(a i) h -> i h a", i=2)[i],
                                 allow_slow_non_contiguous=True).then_inc(expert_loaded, 16)
                    sp.dma_start(w2s[rows, :, :], w2.rearrange("(a i) h d -> i h a d", i=2)[i]).then_inc(expert_loaded, 16)
                sp.dma_start(b2_all, b2.unsqueeze(0).broadcast_to([P, E, D])).then_inc(b2_loaded, 16)

                def load(i, b):
                    if b >= 2:
                        sp.wait_ge(y2_step, times(i, TC * (b - 1), 2 * TC))
                    sp.dma_start(x1_sb[:, b % 2, :, :], x1_dram[bass.ds(times(i, b * T, 2 * T), T), :]
                                 .rearrange("(t p) d -> p t d", p=P)).then_inc(xc_loaded[b % 2], 16)
                    sp.dma_start(comb_sb[:, b % 2, :, :], comb_dram[bass.ds(times(i, b, 2), 1), :, :, :]
                                 .rearrange("b p k n -> (b p) k n")).then_inc(xc_loaded[b % 2], 16)

                def load_slots(i, b):
                    if b >= 2:
                        sp.wait_ge(y2_step, times(i, TC * (b - 1), 2 * TC))
                    sp.dma_start(so_sb[:, b % 2, :, :], slot_dram[bass.ds(times(i, b, 2), 1), :, :]
                                 .rearrange("b (k p) d -> (b p) k d", p=P)).then_inc(so_loaded[b % 2], 16)

                load(None, 0)
                load(None, 1)
                for e in range(E):
                    sp.wait_ge(so_done, e + 1)
                    for m in range(M):
                        sp.dma_start(slot_dram[m * (P // S):(m + 1) * (P // S), e * S:(e + 1) * S, :],
                                     slot_out[:, e % 4, m, :]).then_inc(so_stored[e % 4], 16)
                for k in range(4):
                    sp.wait_ge(so_stored[k], 16 * M * E // 4)
                load_slots(None, 0)
                load_slots(None, 1)

                def store(i, b):
                    sp.wait_ge(out_ready, times(i, TC * (b + 1), 2 * TC))
                    sp.dma_start(out_rows[bass.ds(times(i, b * T, 2 * T), T), :].rearrange("(t p) d -> p t d", p=P),
                                 out_sb[:, b % 2, :, :]).then_inc(out_stored[b % 2], 16)

                with sp.Fori(0, B // 2 - 1) as i:
                    for b in (2, 3):
                        load(i, b)
                        load_slots(i, b)
                        store(i, b - 2)
                store(None, B - 2)
                store(None, B - 1)
                for k in range(2):
                    sp.wait_ge(out_stored[k], 16 * B // 2)

            @block.tensor
            def _(pe):
                def hidden_layer(a):
                    if a >= 2:
                        pe.wait_ge(h_done, a - 1)
                    for k in range(KC):
                        for i in range(2):
                            last = nc.tensor.matmul(h_ps[a % 2][HF * i:HF * i + HF, 0:B * S], w1s[:, k, 2 * a + i, :],
                                                    slotT[:, k, 2 * a + i, :, :].rearrange("p b s -> p (b s)"),
                                                    start=(k == 0), stop=(k == KC - 1), tile_position=(0, HF * i))
                    last.then_inc(h_ready, 1)

                def output_layer(a):
                    pe.wait_ge(h_done, a + 1)
                    for i in range(2):
                        e = 2 * a + i
                        rows = slice(HF * i, HF * i + HF)
                        if e >= 4:
                            pe.wait_ge(so_done, e - 3)
                        for m in range(M):
                            last = nc.tensor.matmul(so_ps[e % 4][:, m * D:(m + 1) * D], hidden[rows, a, m * P:(m + 1) * P],
                                                    w2s[rows, a, :], start=True, stop=True, tile_position=(HF * i, 0))
                        last.then_inc(so_ready, 1)

                pe.wait_ge(expert_loaded, 16 * (KC + 4))
                for a in range(EP):
                    hidden_layer(a)
                    if a >= 1:
                        output_layer(a - 1)
                output_layer(EP - 1)
                pe.wait_ge(so_done, E)

                def combine(i, b):
                    pe.wait_ge(xc_loaded[b % 2], times(i, 32 * (b // 2 + 1), 32))
                    pe.wait_ge(so_loaded[b % 2], times(i, 16 * (b // 2 + 1), 16))
                    for t in range(TC):
                        if b >= 2:
                            pe.wait_ge(y2_step, times(i, TC * (b - 2) + t + 1, 2 * TC))
                        for k in range(KC):
                            last = nc.tensor.matmul(out_ps[b % 2][t][:, 0:D], comb_sb[:, b % 2, k, t * P:(t + 1) * P], so_sb[:, b % 2, k, :],
                                                    start=(k == 0), stop=(k == KC - 1))
                        last.then_inc(comb_ready_ps, 1)

                batches(pe, combine)

            @block.scalar
            def _(act):
                act.wait_ge(expert_loaded, 16 * (KC + 4))
                for a in range(EP):
                    act.wait_ge(h_ready, a + 1)
                    nc.scalar.activation(hidden[:, a, :], h_ps[a % 2][:, 0:B * S], ACT.Gelu, bias=b1_col[:, a:a + 1])\
                        .then_inc(h_done, 1)

                def normalise_out(i, b):
                    act.wait_ge(ostat_ready, times(i, 3 * (b + 1), 6))
                    if b >= 2:
                        act.wait_ge(out_stored[b % 2], times(i, 16 * (b // 2), 16))
                    for t in range(TC):
                        nc.scalar.activation(out_sb[:, b % 2, t, :], y2[:, b % 2, t, :], ACT.Identity,
                                             scale=orstd[:, b % 2, t:t + 1], bias=oshift[:, b % 2, 1, t:t + 1]).then_inc(out_ready, 1)

                batches(act, normalise_out)

            @block.gpsimd
            def _(pool):
                def out_stats(i, b):
                    pool.wait_ge(oagg, times(i, b + 1, 2))
                    if b >= 2:
                        pool.wait_ge(out_ready, times(i, TC * (b - 1), 2 * TC))
                    nc.gpsimd.tensor_tensor(orstd[:, b % 2, :], ovar[:, b % 2, :], minus_half[:, 0:TC], ALU.pow).then_inc(ostat_ready, 1)
                    nc.gpsimd.tensor_scalar(oshift[:, b % 2, 0, :], omv[:, b % 2, :, 0], -1.0, None, ALU.mult).then_inc(ostat_ready, 1)
                    pool.wait_ge(ostat_ready, times(i, 3 * b + 2, 6))
                    nc.gpsimd.tensor_tensor(oshift[:, b % 2, 1, :], oshift[:, b % 2, 0, :], orstd[:, b % 2, :], ALU.mult)\
                        .then_inc(ostat_ready, 1)

                batches(pool, out_stats)

            @block.vector
            def _(dve):
                dve.wait_ge(b2_loaded, 16)
                for e in range(E):
                    dve.wait_ge(so_ready, e + 1)
                    if e >= 4:
                        dve.wait_ge(so_stored[e % 4], 16 * M * (e // 4))
                    nc.vector.tensor_tensor(slot_out[:, e % 4, :, :], so_ps[e % 4].rearrange("p (m d) -> p m d", m=M),
                                            b2_all[:, e, :].unsqueeze(1).broadcast_to([P, M, D]), ALU.add).then_inc(so_done, 1)

                def residual_out(i, b):
                    if b >= 2:
                        dve.wait_ge(out_ready, times(i, TC * (b - 1), 2 * TC))
                    nc.vector.tensor_copy(crec4[:, b % 2, :], crec[:, bass.ds(times(i, TC * b, 2 * TC), TC)]).then_inc(crec_copied, 1)
                    dve.wait_ge(crec_copied, times(i, b + 1, 2))
                    dve.wait_ge(xc_loaded[b % 2], times(i, 32 * (b // 2 + 1), 32))
                    for t in range(TC):
                        dve.wait_ge(comb_ready_ps, times(i, TC * b + t + 1, 2 * TC))
                        nc.vector.scalar_tensor_tensor(out=y2[:, b % 2, t, :], in0=out_ps[b % 2][t][:, 0:D], scalar=crec4[:, b % 2, t:t + 1],
                                                       in1=x1_sb[:, b % 2, t, :], op0=ALU.mult, op1=ALU.add).then_inc(y2_step, 1)
                    for t in range(TC):
                        dve.wait_ge(y2_step, times(i, TC * b + t + 1, 2 * TC))
                        nc.vector.bn_stats(obn[:, b % 2, t, :], y2[:, b % 2, t, :]).then_inc(obn_ready, 1)
                    dve.wait_ge(obn_ready, times(i, TC * (b + 1), 2 * TC))
                    hold_wait()
                    for t in range(TC):
                        nc.vector.bn_aggr(omv[:, b % 2, t, :], obn[:, b % 2, t, :]).then_inc(omv_ready, 1)
                    dve.wait_ge(omv_ready, times(i, TC * (b + 1), 2 * TC))
                    nc.vector.tensor_scalar(ovar[:, b % 2, :], omv[:, b % 2, :, 1], LN_EPS, None, ALU.add).then_inc(oagg, 1)

                batches(dve, residual_out)


_INS = ['L0_attn_x', 'L0_attn_Wq', 'L0_attn_Wk', 'L0_attn_Wv', 'L0_attn_gq', 'L0_attn_gk', 'L0_attn_Wo', 'L0_attn_bo',
        'L0_attn_ln_w', 'L0_attn_ln_b', 'L0_ffn_ln_gamma', 'L0_ffn_ln_beta', 'L0_ffn_mu', 'L0_ffn_scale',
        'L0_ffn_w1', 'L0_ffn_b1', 'L0_ffn_w2', 'L0_ffn_b2']


def kernel(**inputs):
    import numpy as np
    import concourse.bacc as bacc
    from concourse import mybir as mb
    from concourse.bass_utils import run_bass_kernel_spmd

    nc = bacc.Bacc("TRN2", target_bir_lowering=False, num_devices=1, dynamic_dma_scratch_size=1024)
    arrays, args = {}, []

    def give(name, a):
        arrays[f"in_{name}_dram"] = a
        args.append(nc.dram_tensor(f"in_{name}_dram", a.shape, mb.dt.from_np(a.dtype), kind="ExternalInput").ap())

    for name in _INS:
        give(name, np.ascontiguousarray(inputs[name]))
    row, head_rows, hd = np.arange(128), 64, 16
    low = (row % head_rows) // hd % 2
    block = (row[:, None] // head_rows) == (np.arange(2 * hd)[None, :] // hd)
    give("consts", np.concatenate([np.eye(128), (low == 0)[:, None], (low == 1)[:, None], block], axis=1).astype(np.float32))
    shape = inputs['L0_attn_x'].shape
    args.append(nc.dram_tensor("out_0_dram", shape, mb.dt.float32, kind="ExternalOutput").ap())
    seq_block_kernel(nc, *args)
    r = run_bass_kernel_spmd(nc, [arrays], core_ids=[0])
    return r.results[0]["out_0_dram"]
```

```python
from contextlib import ExitStack

import concourse.bass as bass
from concourse import mybir

F32 = mybir.dt.float32
F16 = mybir.dt.float16
ALU = mybir.AluOpType
ACT = mybir.ActivationFunctionType
AX_X = mybir.AxisListType.X

P = 128
THRESH = 0.29514
SHARP = 15.0
LN_EPS = 1e-5
NORM_EPS = 1e-12
GATE_SCALE = 16.0
W_SCALE = 1024.0

LOOP_FROM, LOOP_SLOTS, LOOP_TIMES = 16, 8, 4


def seq_block_kernel(nc, x, Wq, Wk, Wv, gq, gk, Wo, bo, ln_w, ln_b, gamma, beta, mu, scale,
                     w1, b1, w2, b2, consts, out):
    B, T, D = x.shape
    HD = gq.shape[0]
    H = D // HD
    E, S = mu.shape[1], mu.shape[2]
    ES = E * S
    HF = w1.shape[2]
    KC = D // P
    TC = T // P
    NCH = B * TC
    PAIRS = H // 2
    GROUPS = 4
    QUADS = 4
    assert (D, HD, E, S, HF, TC) == (256, 16, 16, 16, 64, 4)

    x_rows = x.rearrange("b t d -> (b t) d")
    out_rows = out.rearrange("b t d -> (b t) d")
    x1_dram = nc.dram_tensor("x1_scratch", (B * T, D), F32, kind="Internal").ap()
    comb_dram = nc.dram_tensor("combine_scratch", (B, P, KC, T), F32, kind="Internal").ap()
    slot_dram = nc.dram_tensor("slot_out_scratch", (B, ES, D), F32, kind="Internal").ap()

    with ExitStack() as ctx:
        def sb(name, shape, dt=F32):
            return ctx.enter_context(nc.sbuf_tensor(name, shape, dt))

        def ps(name, shape, dt=F32):
            return ctx.enter_context(nc.psum_tensor(name, shape, dt))

        def sem(name):
            return ctx.enter_context(nc.semaphore(name))

        ident = sb("ident", [P, P])
        ident16 = sb("ident16", [P, P], F16)
        masks = sb("masks", [P, 2 + 2 * HD])
        minus_half = sb("minus_half", [P, 2 * H])
        wqk_hi, wqk_lo = sb("wqk_hi", [P, KC, 2 * D], F16), sb("wqk_lo", [P, KC, 2 * D], F16)
        wv_hi, wv_lo = sb("wv_hi", [P, KC, D], F16), sb("wv_lo", [P, KC, D], F16)
        wo = sb("wo", [P, KC, D])
        mu_hi, mu_lo = sb("mu_hi", [P, KC, ES], F16), sb("mu_lo", [P, KC, ES], F16)
        wv_sum = sb("wv_sum", [P, D])
        lnw_scaled = sb("lnw_scaled", [P, KC])
        qk_bias = sb("qk_bias", [P, 2 * D])
        gk_all = sb("gk_all", [P, D])
        bo_all = sb("bo_all", [P, D])
        gamma_all = sb("gamma_all", [P, D])
        beta_all = sb("beta_all", [P, D])
        lnw_col = sb("lnw_col", [P, KC])
        lnb_col = sb("lnb_col", [P, KC])
        scale_col = sb("scale_col", [P, 1])
        gq_col = sb("gq_col", [P, 4])
        gq_hi16 = sb("gq_hi16", [P, 1], F16)
        gate_w = sb("gate_w", [P, 2 * HD], F16)
        wait_holder = sb("wait_holder", [P, 1])
        mu_norm = sb("mu_norm", [P, 2 * KC])

        xs = sb("xs", [P, 4, D])
        bn = sb("bn", [P, 2, 6])
        mv = sb("mv", [P, 4, 2])
        var_eps = sb("var_eps", [P, 4])
        rstd = sb("rstd", [P, 4])
        z = sb("z", [P, 2, D])
        zT_hi, zT_lo = sb("zT_hi", [P, 2, KC, P], F16), sb("zT_lo", [P, 2, KC, P], F16)
        sd_v = sb("sd_v", [P, 4])
        qk = sb("qk", [P, 4, 2 * D])
        v_raw = sb("v_raw", [P, 4, D])
        sqg = sb("sqg", [P, 3 * D])
        sums = sb("sums", [P, 2, 3 * H])
        rn = sb("rn", [P, 2, 2 * H])
        qn = sb("qn", [P, 2 * D])
        hl = sb("hl", [P, 2, 2 * H, 4, HD], F16)
        gate_k = sb("gate_k", [P, 2, H])
        stack = sb("stack", [P, 2, 2, PAIRS, T], F16)
        vpad = sb("vpad", [P, 2, TC, PAIRS, 3 * HD])
        res = sb("res", [P, 4, QUADS, T])
        ones = res[:, 0, 0, 0:P]
        lnb_cols = res[:, 0, 1, 0:KC * P].rearrange("p (k n) -> p k n", k=KC)
        wqk = res[:, 1, 0:2, :]
        wv = res[:, 2, 0, :].rearrange("p (k n) -> p k n", k=KC)
        mu_whole = res[:, 2, 1, :].rearrange("p (k n) -> p k n", k=KC)
        gate_q = sb("gate_q", [P, 2, T])
        coll = sb("coll", [P, 2, 2, T])
        xr = sb("xr", [P, 4, D])
        y = sb("y", [P, 2, D])
        ybn = sb("ybn", [P, 2, 6])
        ymv = sb("ymv", [P, 2, 2])
        yvar = sb("yvar", [P, 2])
        yrstd = sb("yrstd", [P, 2])
        v1 = sb("v1", [P, 2, 2])
        r1 = sb("r1", [P, 2])
        x1 = sb("x1", [P, 2, D])
        xg = sb("xg", [P, D])
        xn = sb("xn", [P, D])
        xn_parts = sb("xn_parts", [P, 2, 2, TC, D], F16)
        xss = sb("xss", [P, 2, 2])
        xrn = sb("xrn", [P, 2])
        xnT = sb("xnT", [P, 2, 2, KC, P], F16)
        logit = sb("logit", [P, 2, TC, ES])
        rmax = sb("rmax", [P, 2, TC, 2])
        csum = sb("csum", [P, 2, TC])
        logitT = sb("logitT", [P, 2, KC, T])
        cmax = sb("cmax", [P, KC])
        esum = sb("esum", [P, 2, KC])
        disp = sb("disp", [P, 2, TC, ES], F16)
        disp_f32 = disp[:, :, :, :].rearrange("p a t n -> p (a t n)").bitcast(F32)
        combT = sb("combT", [P, 2, 2 * ES])
        slotT = sb("slotT", [P, KC, E, B, S])
        crec = sb("crec", [P, NCH])

        score_ps = [ps(f"score{t}", [P, 2, T]) for t in range(2)]
        coll_ps = ps("coll_ps", [P, T])
        f0 = ps("f0", [P, 512])
        f1 = ps("f1", [P, 512])
        b0 = ps("b0", [P, 512])
        f0h, f1h = f0[:, :].bitcast(F16), f1[:, :].bitcast(F16)

        TAIL = NCH
        LOGITS_TAIL, WO_TAIL, XN_TAIL, LOGT_TAIL = TAIL - 6, TAIL - 4, TAIL + 1 - 6, TAIL + 1 - 7

        def wo_bank(c):
            return score_ps[c % 2][:, 0, 0:D] if c >= WO_TAIL else b0[:, 0:D]

        def logits_bank(c):
            return coll_ps[:, 0:ES] if c >= LOGITS_TAIL else b0[:, 0:ES]

        def xnT_bank(c):
            bank = score_ps[0][:, 1, 0:KC * P] if c >= XN_TAIL else b0[:, 0:KC * P]
            return bank.bitcast(F16)

        def logT_bank(c):
            return score_ps[1][:, 1, 0:KC * P] if c >= LOGT_TAIL else b0[:, KC * P:2 * KC * P]

        const_loaded, wqk_loaded, weight_loaded = sem("const_loaded"), sem("wqk_loaded"), sem("weight_loaded")
        zT_split, v_shifted, wqk_split, wv_split = sem("zT_split"), sem("v_shifted"), sem("wqk_split"), sem("wv_split")
        xn_split, mu_split, squares_ready = sem("xn_split"), sem("mu_split"), sem("squares_ready")
        disp_split = sem("disp_split")
        wv_loaded = sem("wv_loaded")
        lnw_ready, mu_squared, kg_ready, sd_ready = sem("lnw_ready"), sem("mu_squared"), sem("kg_ready"), sem("sd_ready")
        setup_v, setup_p, setup_t = sem("setup_v"), sem("setup_p"), sem("setup_t")
        x_loaded = [sem(f"x_loaded{k}") for k in range(4)]
        xr_loaded = [sem(f"xr_loaded{k}") for k in range(4)]
        x1_stored = [sem(f"x1_stored{k}") for k in range(2)]
        comb_stored = [sem(f"comb_stored{k}") for k in range(2)]
        stats, z_ready, rstd_ready = sem("stats"), sem("z_ready"), sem("rstd_ready")
        zT_ready, zT_copied = sem("zT_ready"), sem("zT_copied")
        qk_ready, qk_copied = sem("qk_ready"), sem("qk_copied")
        v_ready, v_copied = sem("v_ready"), sem("v_copied")
        sums_ready, rn_ready = sem("sums_ready"), sem("rn_ready")
        norm_step, hl_ready, v_gated = sem("norm_step"), sem("hl_ready"), sem("v_gated")
        stk_ready, stk_copied = sem("stk_ready"), sem("stk_copied")
        sc_ready, sig_done, pv_done = sem("sc_ready"), sem("sig_done"), sem("pv_done")
        gate_ready, gate_copied, coll_done = sem("gate_ready"), sem("gate_copied"), sem("coll_done")
        wo_ready, xb_ready = sem("wo_ready"), sem("xb_ready")
        y_step, yrstd_ready = sem("y_step"), sem("yrstd_ready")
        x1_ready, r1_ready = sem("x1_ready"), sem("r1_ready")
        xn_step, xrn_ready = sem("xn_step"), sem("xrn_ready")
        xnT_ready, xnT_copied = sem("xnT_ready"), sem("xnT_copied")
        log_ready, log_step = sem("log_ready"), sem("log_step")
        logT_ready, logT_copied = sem("logT_ready"), sem("logT_copied")
        soft_max, soft_exp, soft_post = sem("soft_max"), sem("soft_exp"), sem("soft_post")
        disp_ready, disp_copied = sem("disp_ready"), sem("disp_copied")
        slot_ready, slot_copied = sem("slot_ready"), sem("slot_copied")
        combT_ready, combT_copied = sem("combT_ready"), sem("combT_copied")

        gate_setup, hi_ready = sem("gate_setup"), sem("hi_ready")

        def times(i, base, per_body):
            return base if i is None else i * per_body + base

        def per_slot(i, base, n=1):
            return times(i, base, n * LOOP_SLOTS)

        def per_batch(i, base, n=1):
            return times(i, base, n * LOOP_SLOTS // TC)

        def slots(eng, slot, first, last):
            loop_end = LOOP_FROM + LOOP_SLOTS * LOOP_TIMES
            for s in range(first, LOOP_FROM):
                slot(None, s)
            with eng.Fori(0, LOOP_TIMES) as i:
                for s in range(LOOP_FROM, LOOP_FROM + LOOP_SLOTS):
                    slot(i, s)
            for s in range(loop_end, last + 1):
                slot(None, s)

        def chunk_ok(c):
            return 0 <= c < NCH

        def batch_ok(b):
            return 0 <= b < B

        FIRST, LAST = -10, NCH + 11
        VECTOR_KG = 8

        def hold_wait():
            nc.vector.memset(wait_holder[:], 0.0)

        def heads(ap):
            return ap.rearrange("p (h d) -> p h d", d=HD)

        def over(ap, n):
            return ap.unsqueeze(len(ap.shape)).broadcast_to(list(ap.shape) + [n])

        M = B * S // P
        EP = E // 2
        b1_col = sb("b1_col", [P, EP])
        res_flat = res[:, :, :, :].rearrange("p a q t -> p (a q t)")
        b2_all = res_flat[:, 0:E * D].rearrange("p (e d) -> p e d", e=E)
        slot_out = res_flat[:, E * D:E * D + 4 * M * D].rearrange("p (r m d) -> p r m d", r=4, m=M)
        out_sb = res_flat[:, E * D + 4 * M * D:E * D + 4 * M * D + 2 * TC * D].rearrange("p (a t d) -> p a t d", a=2, t=TC)
        stack_flat = stack[:, :, :, :, :].rearrange("p a b c t -> p (a b c t)").bitcast(F32)
        hidden = stack_flat[:, 0:EP * B * S].rearrange("p (a n) -> p a n", a=EP)
        at = EP * B * S
        x1_stack = stack_flat[:, at:at + 2 * TC * D].rearrange("p (a t d) -> p a t d", a=2, t=TC)
        at += 2 * TC * D
        comb_stack = stack_flat[:, at:at + 2 * KC * T].rearrange("p (a k n) -> p a k n", a=2, k=KC)
        at += 2 * KC * T
        w1s = stack_flat[:, at:at + KC * E * HF].rearrange("p (k e h) -> p k e h", k=KC, e=E)
        w2s = vpad[:, :, :, :, :].rearrange("p a t c d -> p (a t c d)")[:, 0:EP * D].rearrange("p (a d) -> p a d", a=EP)
        RING = 4

        def as_rows(ap):
            return ap.rearrange("p (t d) -> p t d", d=D)

        def as_comb(ap):
            return ap.rearrange("p (k n) -> p k n", k=KC)

        xn_places = [as_rows(xn_parts[:, k, :, :, :].rearrange("p a t d -> p (a t d)").bitcast(F32)) for k in range(2)]
        x1_places = [x1_stack[:, 0], x1_stack[:, 1], xn_places[0], xn_places[1],
                     logit[:, 0], logit[:, 1], as_rows(gate_q[:, :, :].rearrange("p a n -> p (a n)")), as_rows(disp_f32)]
        comb_places = [comb_stack[:, 0], comb_stack[:, 1], logitT[:, 0], logitT[:, 1]] + \
            [as_comb(a[:, :, :].rearrange("p a n -> p (a n)")) for a in (combT, xr, v_raw, xs)]
        so_sb = coll[:, :, :, :].rearrange("p a b t -> p (a b t)").rearrange("p (a k d) -> p a k d", a=RING, k=KC)

        def place(b):
            return b if b < RING else RING + b % RING

        def x1_in(b):
            return x1_places[place(b)]

        def comb_in(b):
            return comb_places[place(b)]

        y2 = qk[:, :, :].rearrange("p a n -> p (a n)").rearrange("p (a t d) -> p a t d", a=2, t=TC)
        crec4 = sb("crec4", [P, 2, TC])
        obn = sb("obn", [P, 2, TC, 6])
        omv = sb("omv", [P, 2, TC, 2])
        ovar, orstd, oshift = sb("ovar", [P, 2, TC]), sb("orstd", [P, 2, TC]), sb("oshift", [P, 2, 2, TC])

        expert_loaded, b2_loaded = sem("expert_loaded"), sem("b2_loaded")
        h_ready, h_done, so_ready, so_done = sem("h_ready"), sem("h_done"), sem("so_ready"), sem("so_done")
        so_stored = [sem(f"so_stored{k}") for k in range(4)]
        xc_loaded = [sem(f"xc_loaded{k}") for k in range(2 * RING)]
        so_loaded = [sem(f"so_loaded{k}") for k in range(RING)]
        comb_ready_ps, y2_step, oagg = sem("comb_ready_ps"), sem("y2_step"), sem("oagg")
        ostat_ready, out_ready = sem("ostat_ready"), sem("out_ready")
        crec_copied, obn_ready, omv_ready = sem("crec_copied"), sem("obn_ready"), sem("omv_ready")
        out_stored = [sem(f"out_stored{k}") for k in range(2)]

        def per_ring(i, base, n=1):
            return times(i, base, n * RING)

        def load_batch(sp, i, b):
            if b >= 2 * RING:
                sp.wait_ge(y2_step, per_ring(i, TC * (b - RING + 1), TC))
            sp.dma_start(x1_in(b), x1_dram[bass.ds(per_ring(i, b * T, T), T), :]
                         .rearrange("(t p) d -> p t d", p=P)).then_inc(xc_loaded[place(b)], 16)
            sp.dma_start(comb_in(b), comb_dram[bass.ds(per_ring(i, b), 1), :, :, :]
                         .rearrange("b p k n -> (b p) k n")).then_inc(xc_loaded[place(b)], 16)

        def batch_loaded(eng, i, b):
            eng.wait_ge(xc_loaded[place(b)], times(i, 32 * max(b // RING, 1), 32))

        WEIGHTS = 7 + P // HD
        with nc.Block() as block:

            @block.sync
            def _(sp):
                c_eye, c_masks = consts[:, 0:P], consts[:, P:P + 2 + 2 * HD]
                sp.dma_start(ident[:], c_eye).then_inc(const_loaded, 16)
                sp.dma_start(masks[:], c_masks).then_inc(const_loaded, 16)

                def load_x(i, c):
                    k = c % 4
                    if c >= 4:
                        sp.wait_ge(zT_ready, per_slot(i, c - 3))
                    sp.dma_start(xs[:, k, :], x_rows[bass.ds(per_slot(i, c * P, P), P), :]).then_inc(x_loaded[k], 16)

                load_x(None, 0)
                for dst, src in ((wqk[:, :, 0:D], Wq), (wqk[:, :, D:2 * D], Wk)):
                    sp.dma_start(dst, src.rearrange("(k p) n -> p k n", p=P)).then_inc(wqk_loaded, 16)
                for c in range(1, 4):
                    load_x(None, c)

                def load_experts():
                    sp.wait_ge(pv_done, 4 * NCH)
                    sp.wait_ge(gate_ready, 2 * B)
                    for k in range(KC):
                        sp.dma_start(w1s[:, k, :, :], w1.rearrange("e (k p) h -> k p e h", p=P)[k]).then_inc(expert_loaded, 16)
                    for i in range(2):
                        rows = slice(HF * i, HF * i + HF)
                        sp.dma_start(b1_col[rows, :], b1.rearrange("(a i) h -> i h a", i=2)[i],
                                     allow_slow_non_contiguous=True).then_inc(expert_loaded, 16)
                        sp.dma_start(w2s[rows, :, :], w2.rearrange("(a i) h d -> i h a d", i=2)[i]).then_inc(expert_loaded, 16)
                    sp.dma_start(b2_all, b2.unsqueeze(0).broadcast_to([P, E, D])).then_inc(b2_loaded, 16)
                    for k in range(2):
                        sp.wait_ge(x1_stored[k], 16 * TC)
                        sp.wait_ge(comb_stored[k], 16 * 2)
                    load_batch(sp, None, 0)
                    load_batch(sp, None, 1)

                def slot(i, s):
                    j = s % TC
                    if s == NCH + 2:
                        load_experts()
                    if chunk_ok(s + 10) and s + 10 >= 4:
                        load_x(i, s + 10)
                    c = s - 2
                    if chunk_ok(c):
                        if c >= 4:
                            sp.wait_ge(y_step, per_slot(i, 4 * (c - 4) + 1, 4))
                        sp.dma_start(xr[:, c % 4, :], x_rows[bass.ds(per_slot(i, c * P, P), P), :])\
                            .then_inc(xr_loaded[c % 4], 16)
                    c = s - 6
                    if chunk_ok(c):
                        sp.wait_ge(x1_ready, per_slot(i, 3 * c + 1, 3))
                        sp.dma_start(x1_dram[bass.ds(per_slot(i, c * P, P), P), :], x1[:, c % 2, :])\
                            .then_inc(x1_stored[c % 2], 16)
                    half, b = j // 2, s // TC - 3
                    if j in (1, 3) and batch_ok(b):
                        sp.wait_ge(combT_copied, per_batch(i, 2 * b + half + 1, 2))
                        dst = comb_dram[bass.ds(per_batch(i, b), 1), :, :, half * 2 * P:(half + 1) * 2 * P]
                        sp.dma_start(dst.rearrange("b p k n -> (b p) k n"),
                                     combT[:, half, :].rearrange("p (k n) -> p k n", k=KC))\
                            .then_inc(comb_stored[half], 16)

                slots(sp, slot, FIRST, LAST)

            @block.gpsimd
            def _(pool):
                nc.gpsimd.memset(minus_half[:], -0.5).then_inc(setup_p, 1)
                nc.gpsimd.memset(vpad[:], 0.0).then_inc(setup_p, 1)
                pool.wait_ge(setup_p, 2)

                def power(dst, src, n):
                    return nc.gpsimd.tensor_tensor(dst, src, minus_half[:, 0:n], ALU.pow)

                def slot(i, s):
                    c = s - 5
                    if chunk_ok(c):
                        pool.wait_ge(y_step, per_slot(i, 4 * c + 4, 4))
                        power(yrstd[:, c % 2:c % 2 + 1], yvar[:, c % 2:c % 2 + 1], 1).then_inc(yrstd_ready, 1)
                    c = s + 8
                    if chunk_ok(c):
                        pool.wait_ge(stats, per_slot(i, 3 * c + 3, 3))
                        power(rstd[:, c % 4:c % 4 + 1], var_eps[:, c % 4:c % 4 + 1], 1).then_inc(rstd_ready, 1)
                    if s == -5:
                        pool.wait_ge(mu_squared, 2)
                        power(mu_norm[:, KC:2 * KC], mu_norm[:, 0:KC], KC).then_inc(setup_p, 1)
                    c = s + 6
                    if chunk_ok(c) and c >= VECTOR_KG:
                        pool.wait_ge(qk_copied, per_slot(i, c + 1))
                        if c >= 1:
                            pool.wait_ge(sums_ready, per_slot(i, 2 * (c - 1) + 1, 2))
                        nc.gpsimd.tensor_tensor(sqg[:, 2 * D:3 * D], qk[:, c % 4, D:2 * D], gk_all[:], ALU.mult)\
                            .then_inc(kg_ready, 1)
                    c = s - 5
                    if chunk_ok(c):
                        pool.wait_ge(x1_ready, per_slot(i, 3 * c + 3, 3))
                        power(r1[:, c % 2:c % 2 + 1], v1[:, c % 2, 1:2], 1).then_inc(r1_ready, 1)
                    c = s + 6
                    if chunk_ok(c):
                        pool.wait_ge(sums_ready, per_slot(i, 2 * c + 2, 2))
                        if c >= 2:
                            pool.wait_ge(norm_step, per_slot(i, 2 * (c - 2) + 2, 2))
                        power(rn[:, c % 2, :], sums[:, c % 2, 0:2 * H], 2 * H).then_inc(rn_ready, 1)
                    c = s - 3
                    if chunk_ok(c):
                        if c == 0:
                            pool.wait_ge(weight_loaded, 16 * WEIGHTS)
                        pool.wait_ge(xr_loaded[c % 4], per_batch(i, 16 * (c // 4 + 1), 16))
                        nc.gpsimd.tensor_tensor(xr[:, c % 4, :], xr[:, c % 4, :], bo_all[:], ALU.add)\
                            .then_inc(xb_ready, 1)
                    c = s - 5
                    if chunk_ok(c):
                        pool.wait_ge(xn_step, per_slot(i, 4 * c + 4, 4))
                        if c >= 2:
                            pool.wait_ge(log_step, per_slot(i, 3 * (c - 2) + 3, 3))
                        power(xrn[:, c % 2:c % 2 + 1], xss[:, c % 2, 1:2], 1).then_inc(xrn_ready, 1)

                slots(pool, slot, FIRST, LAST)

            @block.scalar
            def _(act):
                for dst, src in ((lnw_col, ln_w), (lnb_col, ln_b)):
                    act.dma_start(dst[:], src.rearrange("(k p) -> p k", p=P), allow_slow_non_contiguous=True)\
                        .then_inc(wqk_loaded, 16)

                def weight(dst, src):
                    act.dma_start(dst, src, allow_slow_non_contiguous=True).then_inc(weight_loaded, 16)

                act.dma_start(wv, Wv.rearrange("(k p) n -> p k n", p=P)).then_inc(wv_loaded, 16)
                weight(gk_all[:, :].rearrange("p (h d) -> p h d", d=HD),
                       gk.unsqueeze(0).unsqueeze(0).broadcast_to([P, H, HD]))
                for n in range(P // HD):
                    weight(gq_col[n * HD:(n + 1) * HD, 0:1], gq.unsqueeze(1))
                weight(mu_whole, mu.rearrange("(k p) e s -> p k (e s)", p=P))
                weight(scale_col[:], scale.unsqueeze(0).broadcast_to([P, 1]))
                weight(wo[:], Wo.rearrange("(k p) n -> p k n", p=P))
                weight(bo_all[:], bo.unsqueeze(0).broadcast_to([P, D]))
                weight(gamma_all[:], gamma.unsqueeze(0).broadcast_to([P, D]))
                weight(beta_all[:], beta.unsqueeze(0).broadcast_to([P, D]))

                def sigmoid(i, s, k):
                    u = 4 * s + k
                    for t in range(2):
                        act.wait_ge(sc_ready, per_slot(i, 2 * u + t + 1, 8))
                        if t == 0 and u >= 4:
                            act.wait_ge(pv_done, per_slot(i, u - 3, 4))
                        nc.scalar.activation(res[:, k, 2 * t:2 * t + 2, :], score_ps[t][:, :, :], ACT.Sigmoid,
                                             bias=-THRESH * SHARP, scale=SHARP).then_inc(sig_done, 1)

                def slot(i, s):
                    j = s % TC
                    attn = chunk_ok(s)
                    if attn:
                        sigmoid(i, s, 0)
                    b = s // TC - 3
                    if j == 1 and batch_ok(b):
                        act.wait_ge(combT_ready, per_batch(i, 2 * b + 1, 2))
                        if b >= 1:
                            act.wait_ge(comb_stored[0], per_batch(i, 16 * b, 16))
                        nc.scalar.activation(combT[:, 0, :], b0[:, :], ACT.Copy).then_inc(combT_copied, 1)
                    if j == 0 and batch_ok(b):
                        act.wait_ge(disp_ready, per_batch(i, 2 * b + 2, 2))
                        nc.scalar.activation(disp[:, 0, 2:4, :], b0[:, :].rearrange("p (t n) -> p t n", t=2), ACT.Copy)\
                            .then_inc(disp_copied, 1)
                    if attn and j != 3:
                        sigmoid(i, s, 1)
                    c = s - 6
                    if chunk_ok(c):
                        act.wait_ge(xnT_ready, per_slot(i, c + 1))
                        if c >= 1:
                            act.wait_ge(logT_ready, per_slot(i, c))
                        if c >= 2:
                            act.wait_ge(log_ready, per_slot(i, c - 1))
                        nc.scalar.activation(xnT[:, c % 2, :, :, :].rearrange("p a k n -> p (a k n)"), xnT_bank(c), ACT.Copy)\
                            .then_inc(xnT_copied, 1)
                    c = s - 7
                    if chunk_ok(c):
                        b, t = c // TC, c % TC
                        act.wait_ge(logT_ready, per_slot(i, c + 1))
                        if b >= 2 and t == 0:
                            act.wait_ge(disp_ready, per_batch(i, 2 * (b - 1), 2))
                        nc.scalar.activation(logitT[:, b % 2, :, t * P:(t + 1) * P],
                                             logT_bank(c).rearrange("p (k n) -> p k n", n=P), ACT.Copy)\
                            .then_inc(logT_copied, 1)
                    if attn and j == 3:
                        sigmoid(i, s, 1)
                    c = s + 6
                    if chunk_ok(c):
                        act.wait_ge(qk_copied, per_slot(i, c + 1))
                        if c >= 1:
                            act.wait_ge(sums_ready, per_slot(i, 2 * (c - 1) + 1, 2))
                        nc.scalar.activation(sqg[:, 0:2 * D], qk[:, c % 4, :], ACT.Square).then_inc(squares_ready, 1)
                    if attn:
                        sigmoid(i, s, 2)
                    c = s + 7
                    if chunk_ok(c):
                        act.wait_ge(v_ready, per_slot(i, c + 1))
                        act.wait_ge(sd_ready, per_slot(i, c + 1))
                        if c >= 4:
                            act.wait_ge(v_gated, per_slot(i, c - 3))
                        nc.scalar.activation(v_raw[:, c % 4, :], f0[:, 0:D], ACT.Copy, scale=sd_v[:, c % 4:c % 4 + 1])\
                            .then_inc(v_copied, 1)
                    b = s // TC
                    if attn and j in (0, 2):
                        half = j // 2
                        act.wait_ge(gate_ready, per_batch(i, 2 * b + half + 1, 2))
                        if b >= 1:
                            act.wait_ge(coll_done, per_batch(i, 2 * (b - 1) + half + 1, 2))
                        nc.scalar.activation(gate_q[:, half, :], f1[:, :], ACT.Copy, scale=1.0 / GATE_SCALE)\
                            .then_inc(gate_copied, 1)
                    b = s // TC - 3
                    if batch_ok(b) and j == 1:
                        act.wait_ge(slot_ready, per_batch(i, b + 1))
                        nc.scalar.activation(slotT[:, :, :, bass.ds(per_batch(i, b), 1), :].rearrange("p k e b s -> p k e (b s)"),
                                             f1[:, :].rearrange("p (k e s) -> p k e s", k=KC, s=S), ACT.Copy, scale=1.0 / W_SCALE)\
                            .then_inc(slot_copied, 1)
                    b = s // TC - 2
                    if batch_ok(b) and j == 3:
                        act.wait_ge(disp_ready, per_batch(i, 2 * b + 1, 2))
                        if b >= 1:
                            act.wait_ge(slot_ready, per_batch(i, b))
                        nc.scalar.activation(disp[:, 0, 0:2, :], f1[:, :].rearrange("p (t n) -> p t n", t=2), ACT.Copy)\
                            .then_inc(disp_copied, 1)
                    if attn:
                        sigmoid(i, s, 3)
                    c = s + 8
                    if chunk_ok(c):
                        act.wait_ge(zT_ready, per_slot(i, c + 1))
                        if c >= 2:
                            act.wait_ge(qk_ready, per_slot(i, c - 1))
                        nc.scalar.activation(zT_hi[:, c % 2, :, :], f0[:, 0:KC * P].rearrange("p (k n) -> p k n", n=P), ACT.Copy)\
                            .then_inc(zT_copied, 1)
                    b = s // TC - 2
                    if batch_ok(b) and j == 2:
                        act.wait_ge(log_step, per_batch(i, 3 * TC * (b + 1), 3 * TC))
                        if b >= 2:
                            act.wait_ge(soft_post, per_batch(i, 4 * (b - 1), 4))
                        for t in range(TC):
                            nc.scalar.activation(logit[:, b % 2, t, :], logit[:, b % 2, t, :], ACT.Exp,
                                                 bias=rmax[:, b % 2, t, 1:2], accum_out=csum[:, b % 2, t:t + 1]).then_inc(soft_exp, 1)
                        act.wait_ge(soft_max, per_batch(i, 2 * b + 2, 2))
                        for k in range(KC):
                            nc.scalar.activation(logitT[:, b % 2, k, :], logitT[:, b % 2, k, :], ACT.Exp,
                                                 bias=cmax[:, k:k + 1], accum_out=esum[:, b % 2, k:k + 1]).then_inc(soft_exp, 1)
                slots(act, slot, FIRST, LAST)

            @block.tensor
            def _(pe):
                def setup():
                    pe.wait_ge(setup_v, 3)
                    for k in range(KC):
                        last = nc.tensor.matmul(f1[:, :], lnb_cols[:, k, :], wqk[:, k, :], start=(k == 0), stop=(k == KC - 1))
                    last.then_inc(setup_t, 1)
                    pe.wait_ge(wv_loaded, 16)
                    for k in range(KC):
                        last = nc.tensor.matmul(b0[:, 0:D], ones, wv[:, k, :], start=(k == 0), stop=(k == KC - 1))
                    last.then_inc(setup_t, 1)

                def setup_mu():
                    pe.wait_ge(mu_squared, 1)
                    pe.wait_ge(wv_split, 3)
                    for m in range(KC):
                        for k in range(KC):
                            last = nc.tensor.matmul(b0[:, m:m + 1], logit[:, 0, k, m * P:(m + 1) * P], ones[:, 0:1],
                                                    start=(k == 0), stop=(k == KC - 1))
                    last.then_inc(setup_t, 1)

                def setup_mu_rows():
                    pe.wait_ge(mu_squared, 2 + KC)
                    for m in range(KC):
                        last = nc.tensor.matmul(b0[:, m * P:(m + 1) * P], ones, disp_f32[:, m * P:(m + 1) * P], start=True, stop=True)
                    last.then_inc(setup_t, 1)

                def scores(i, s, k):
                    u = 4 * s + k
                    b, j = s // TC, s % TC
                    half, odd = j // 2, j % 2
                    rows = slice(64 * odd, 64 * odd + 64)
                    if j == 0 and k == 0:
                        pe.wait_ge(stk_copied, per_slot(i, 2 * TC * (b + 1), 2))
                    for t in range(2):
                        if 2 * u + t >= 2:
                            pe.wait_ge(sig_done, per_slot(i, 2 * u + t - 1, 8))
                        for q in (2 * t, 2 * t + 1):
                            pair = 4 * half + q
                            last = nc.tensor.matmul(score_ps[t][:, q % 2, :], stack[rows, b % 2, 1, pair, k * P:(k + 1) * P],
                                                    stack[rows, b % 2, 0, pair, :], start=True, stop=True,
                                                    tile_position=(64 * odd, 0))
                        last.then_inc(sc_ready, 1)

                def weighted_sum(i, s, k):
                    u = 4 * s + k
                    b, j = s // TC, s % TC
                    half, odd = j // 2, j % 2
                    if j == 0 and k == 0:
                        pe.wait_ge(v_gated, per_slot(i, TC * (b + 1)))
                    if odd == 0 and k == 0 and 2 * b + half >= 1:
                        pe.wait_ge(coll_done, per_batch(i, 2 * b + half, 2))
                    pe.wait_ge(sig_done, per_slot(i, 2 * u + 2, 8))
                    for q in range(QUADS):
                        pair = 4 * half + q
                        last = nc.tensor.matmul(coll_ps[32 * q:32 * q + 32, :],
                                                vpad[:, b % 2, k, pair, HD * odd:HD * odd + 2 * HD], res[:, k, q, :],
                                                start=(odd == 0 and k == 0), stop=(odd == 1 and k == TC - 1),
                                                tile_position=(0, 32 * q))
                    last.then_inc(pv_done, 1)

                def misc_emptied(i, s):
                    b, j = s // TC, s % TC
                    if chunk_ok(s) and j in (0, 2):
                        pe.wait_ge(gate_copied, per_batch(i, 2 * b + j // 2 + 1, 2))
                    if j == 1 and batch_ok(b - 3):
                        pe.wait_ge(slot_copied, per_batch(i, b - 3 + 1))
                    if j == 3 and batch_ok(b - 2):
                        pe.wait_ge(disp_split, per_batch(i, 2 * (b - 2) + 1, 2))

                def misc_may_start(i, s):
                    if chunk_ok(s + 4):
                        pe.wait_ge(stk_copied, per_slot(i, 2 * (s + 4) + 2, 2))
                    else:
                        misc_emptied(i, s - 1)
                        misc_emptied(i, s - 2)

                def stacks(i, c):
                    pe.wait_ge(hl_ready, per_slot(i, 3 * c + 3, 3))
                    for side, bank in ((0, f0h), (1, f1h)):
                        if side == 0:
                            if c + 3 < NCH:
                                pe.wait_ge(zT_split, per_slot(i, c + 4))
                            elif c + 3 == NCH:
                                pe.wait_ge(v_copied, NCH)
                            else:
                                pe.wait_ge(stk_copied, per_slot(i, 2 * (c - 1) + 1, 2))
                        else:
                            if c + 2 < NCH:
                                pe.wait_ge(qk_copied, per_slot(i, c + 3))
                            else:
                                misc_emptied(i, c - 5)
                        for pair in range(PAIRS):
                            parts = hl[:, c % 2, side * H + 2 * pair:side * H + 2 * pair + 2, :, :].rearrange("p h a d -> p (h a d)")
                            last = nc.tensor.transpose(bank[:, pair * P:(pair + 1) * P], parts, ident16[:])
                        last.then_inc(stk_ready, 1)

                def transposes(i, c):
                    pe.wait_ge(z_ready, per_slot(i, c + 1))
                    if c == 0:
                        pe.wait_ge(const_loaded, 32)
                    if c >= 1:
                        pe.wait_ge(v_copied, per_slot(i, c))
                    for k in range(KC):
                        last = nc.tensor.transpose(f0[:, k * P:(k + 1) * P], z[:, c % 2, k * P:(k + 1) * P], ident[:])
                    last.then_inc(zT_ready, 1)

                def split_matmuls(dst, hi, lo, w_hi, w_lo):
                    for k in range(KC):
                        for n, (a, w) in enumerate(((hi, w_hi), (hi, w_lo), (lo, w_hi))):
                            last = nc.tensor.matmul(dst, a[:, k, :], w[:, k, :], start=(k == 0 and n == 0),
                                                    stop=(k == KC - 1 and n == 2))
                    return last

                def project_v(i, c):
                    pe.wait_ge(zT_split, per_slot(i, c + 1))
                    if c == 0:
                        pe.wait_ge(wv_split, 3)
                    if chunk_ok(c - 3):
                        pe.wait_ge(stk_copied, per_slot(i, 2 * (c - 3) + 1, 2))
                    split_matmuls(f0[:, 0:D], zT_hi[:, c % 2, :, :], zT_lo[:, c % 2, :, :], wv_hi, wv_lo).then_inc(v_ready, 1)

                def project_qk(i, s, c):
                    if c == 0:
                        pe.wait_ge(wqk_split, 4)
                        pe.wait_ge(setup_v, 4)
                    if chunk_ok(s + 4):
                        pe.wait_ge(stk_copied, per_slot(i, 2 * (s + 4) + 2, 2))
                    elif c >= 1:
                        pe.wait_ge(qk_copied, per_slot(i, c))
                    misc_emptied(i, s)
                    split_matmuls(f1[:, :], zT_hi[:, c % 2, :, :], zT_lo[:, c % 2, :, :], wqk_hi, wqk_lo).then_inc(qk_ready, 1)

                def gates(i, s):
                    b, half = s // TC, s % TC // 2
                    misc_may_start(i, s)
                    if half == 0:
                        pe.wait_ge(stk_copied, per_slot(i, 2 * TC * (b + 1), 2))
                    for q in range(QUADS):
                        last = nc.tensor.matmul(f1[32 * q:32 * q + 32, :], gate_w[:], stack[:, b % 2, 0, 4 * half + q, :],
                                                start=True, stop=True, tile_position=(0, 32 * q))
                    last.then_inc(gate_ready, 1)

                def output_projection(i, c):
                    b, j = c // TC, c % TC
                    if j == 0:
                        pe.wait_ge(coll_done, per_batch(i, 2 * b + 2, 2))
                    if c >= WO_TAIL:
                        if c >= WO_TAIL + 2:
                            pe.wait_ge(y_step, 4 * (c - 2) + 1)
                    elif chunk_ok(c - 2):
                        pe.wait_ge(log_step, per_slot(i, 3 * (c - 2) + 3, 3))
                    elif c == 0:
                        pe.wait_ge(mu_split, 3)
                    elif c == 1:
                        pe.wait_ge(y_step, 1)
                    for k in range(KC):
                        last = nc.tensor.matmul(wo_bank(c), coll[:, b % 2, k, j * P:(j + 1) * P], wo[:, k, :],
                                                start=(k == 0), stop=(k == KC - 1))
                    last.then_inc(wo_ready, 1)

                def b0_emptied(i, s):
                    b, j = s // TC - 3, s % TC
                    if chunk_ok(s - 5):
                        pe.wait_ge(y_step, per_slot(i, 4 * (s - 5) + 1, 4))
                    elif chunk_ok(s - 7):
                        pe.wait_ge(log_step, per_slot(i, 3 * (s - 7) + 3, 3))
                    elif chunk_ok(s - 8):
                        pe.wait_ge(logT_copied, per_slot(i, s - 7))
                    if j in (1, 3) and batch_ok(b):
                        pe.wait_ge(combT_copied, per_batch(i, 2 * b + j // 2 + 1, 2))
                    if j == 0 and batch_ok(b):
                        pe.wait_ge(disp_split, per_batch(i, 2 * b + 2, 2))

                def transpose_xn_and_logits(i, s):
                    if s <= TAIL:
                        b0_emptied(i, s)
                    c = s - 6
                    if chunk_ok(c):
                        pe.wait_ge(xn_split, per_slot(i, 2 * c + 2, 2))
                        if c > XN_TAIL:
                            pe.wait_ge(xnT_copied, c)
                        for part in range(2):
                            for k in range(KC):
                                at = part * KC + k
                                last = nc.tensor.transpose(xnT_bank(c)[:, at * P:(at + 1) * P],
                                                           xn_parts[:, c // TC % 2, part, c % TC, k * P:(k + 1) * P], ident16[:])
                        last.then_inc(xnT_ready, 1)
                    c = s - 7
                    if chunk_ok(c):
                        pe.wait_ge(log_step, per_slot(i, 3 * c + 3, 3))
                        if c > LOGT_TAIL:
                            pe.wait_ge(logT_copied, c)
                        for k in range(KC):
                            last = nc.tensor.transpose(logT_bank(c)[:, k * P:(k + 1) * P],
                                                       logit[:, c // TC % 2, c % TC, k * P:(k + 1) * P], ident[:])
                        last.then_inc(logT_ready, 1)

                def logits(i, c):
                    pe.wait_ge(xnT_copied, per_slot(i, c + 1))
                    if c > LOGITS_TAIL:
                        pe.wait_ge(log_step, 3 * c)
                    elif c == LOGITS_TAIL:
                        pe.wait_ge(coll_done, 2 * B)
                    elif c >= 1:
                        pe.wait_ge(logT_copied, per_slot(i, c))
                    last = split_matmuls(logits_bank(c), xnT[:, c % 2, 0, :, :], xnT[:, c % 2, 1, :, :], mu_hi, mu_lo)
                    last.then_inc(log_ready, 1)

                def b0_emptied_first(i, s):
                    if s <= TAIL:
                        pe.wait_ge(y_step, per_slot(i, 4 * (s - 5) + 1, 4))
                    if s == TAIL + 1:
                        pe.wait_ge(xnT_copied, XN_TAIL)
                        pe.wait_ge(logT_copied, LOGT_TAIL)
                    if s > TAIL:
                        if s % TC == 0:
                            pe.wait_ge(combT_copied, 2 * (s // TC - 4) + 2)
                        elif s % TC == 1:
                            pe.wait_ge(disp_split, 2 * (s // TC - 3) + 2)
                        elif s % TC == 3:
                            pe.wait_ge(combT_copied, 2 * (s // TC - 3) + 1)

                def transpose_combine(i, s, b, half):
                    pe.wait_ge(soft_exp, per_batch(i, 6 * b + TC, 6))
                    b0_emptied_first(i, s)
                    for k in range(KC):
                        for t in range(2):
                            last = nc.tensor.transpose(b0[:, (2 * k + t) * P:(2 * k + t + 1) * P],
                                                       logit[:, b % 2, 2 * half + t, k * P:(k + 1) * P], ident[:])
                    last.then_inc(combT_ready, 1)

                def transpose_dispatch(i, s, b, half):
                    pe.wait_ge(soft_post, per_batch(i, 4 * b + 3, 4))
                    if half == 1:
                        bank = b0
                        b0_emptied_first(i, s)
                    else:
                        bank = f1
                        misc_may_start(i, s)
                    for t in range(2):
                        for k in range(KC):
                            n = 2 * half + t
                            last = nc.tensor.transpose(bank[:, (t * KC + k) * P:(t * KC + k + 1) * P],
                                                       logitT[:, b % 2, k, n * P:(n + 1) * P], ident[:])
                    last.then_inc(disp_ready, 1)

                def slot_inputs(i, s, b):
                    pe.wait_ge(disp_split, per_batch(i, 2 * b + 2, 2))
                    misc_may_start(i, s)
                    for k in range(KC):
                        for t in range(TC):
                            for n, (x_part, w_part) in enumerate(((0, 0), (0, 1), (1, 0))):
                                last = nc.tensor.matmul(f1[:, k * ES:(k + 1) * ES], xn_parts[:, b % 2, x_part, t, k * P:(k + 1) * P],
                                                        disp[:, w_part, t, :], start=(t == 0 and n == 0),
                                                        stop=(t == TC - 1 and n == 2))
                    last.then_inc(slot_ready, 1)

                def slot(i, s):
                    b, j = s // TC, s % TC
                    attn = chunk_ok(s)
                    if s == -7:
                        setup()
                    if s == -6:
                        setup_mu()
                    if s == -3:
                        setup_mu_rows()
                    if attn:
                        scores(i, s, 0)
                    if j in (1, 3) and batch_ok(b - 3):
                        transpose_combine(i, s, b - 3, j // 2)
                    if j == 0 and batch_ok(b - 3):
                        transpose_dispatch(i, s, b - 3, 1)
                    if chunk_ok(s - 1):
                        weighted_sum(i, s - 1, 2)
                    if attn and j != 3:
                        scores(i, s, 1)
                    if chunk_ok(s - 1):
                        weighted_sum(i, s - 1, 3)
                    if chunk_ok(s + 4) and j == 0:
                        stacks(i, s + 4)
                    if chunk_ok(s - 6) or chunk_ok(s - 7):
                        transpose_xn_and_logits(i, s)
                    if chunk_ok(s + 4) and j != 0:
                        stacks(i, s + 4)
                    if attn and j != 3:
                        scores(i, s, 2)
                    if attn and j == 3:
                        scores(i, s, 1)
                    if chunk_ok(s + 7):
                        project_v(i, s + 7)
                    if chunk_ok(s - 6):
                        logits(i, s - 6)
                    if attn and j == 3:
                        scores(i, s, 2)
                    if attn and j in (0, 2):
                        gates(i, s)
                    if j == 1 and batch_ok(b - 3):
                        slot_inputs(i, s, b - 3)
                    if j == 3 and batch_ok(b - 2):
                        transpose_dispatch(i, s, b - 2, 0)
                    if attn:
                        weighted_sum(i, s, 0)
                    if attn:
                        scores(i, s, 3)
                    if chunk_ok(s + 8):
                        transposes(i, s + 8)
                    if chunk_ok(s + 7) and j != 3:
                        project_qk(i, s, s + 7)
                    if attn:
                        weighted_sum(i, s, 1)
                    if chunk_ok(s + 7) and j == 3:
                        project_qk(i, s, s + 7)
                    if chunk_ok(s - 4):
                        output_projection(i, s - 4)

                slots(pe, slot, FIRST, LAST)

            @block.vector
            def _(dve):
                def setup():
                    nc.vector.memset(ones, 1.0).then_inc(setup_v, 1)
                    dve.wait_ge(const_loaded, 32)
                    nc.vector.tensor_copy(ident16[:], ident[:]).then_inc(setup_v, 1)
                    dve.wait_ge(wqk_loaded, 64)
                    nc.vector.tensor_copy(lnb_cols, over(lnb_col[:, :], P)).then_inc(setup_v, 1)
                    nc.vector.tensor_scalar(lnw_scaled[:], lnw_col[:], W_SCALE, None, ALU.mult).then_inc(lnw_ready, 1)
                    dve.wait_ge(lnw_ready, 1)
                    for k in range(KC):
                        nc.vector.tensor_scalar(wqk_hi[:, k, :], wqk[:, k, :], lnw_scaled[:, k:k + 1], None, ALU.mult)\
                            .then_inc(wqk_split, 1)
                    for k in range(KC):
                        dve.wait_ge(wqk_split, k + 1)
                        nc.vector.scalar_tensor_tensor(out=wqk_lo[:, k, :], in0=wqk[:, k, :], scalar=lnw_scaled[:, k:k + 1],
                                                       in1=wqk_hi[:, k, :], op0=ALU.mult, op1=ALU.subtract).then_inc(wqk_split, 1)
                    dve.wait_ge(wv_loaded, 16)
                    nc.vector.tensor_scalar(wv_hi[:], wv, W_SCALE, None, ALU.mult).then_inc(wv_split, 1)
                    dve.wait_ge(wv_split, 1)
                    nc.vector.scalar_tensor_tensor(out=wv_lo[:], in0=wv, scalar=W_SCALE, in1=wv_hi[:],
                                                   op0=ALU.mult, op1=ALU.subtract).then_inc(wv_split, 1)
                    dve.wait_ge(setup_t, 1)
                    nc.vector.tensor_copy(qk_bias[:], f1[:, :]).then_inc(setup_v, 1)
                    dve.wait_ge(setup_t, 2)
                    nc.vector.tensor_copy(wv_sum[:], b0[:, 0:D]).then_inc(wv_split, 1)

                def square_mu():
                    dve.wait_ge(weight_loaded, 16 * WEIGHTS)
                    nc.vector.tensor_tensor(logit[:, 0, 0:KC, :], mu_whole, mu_whole, ALU.mult).then_inc(mu_squared, 1)

                def setup_gate():
                    nc.vector.tensor_scalar(gq_col[:, 1:2], gq_col[:, 0:1], GATE_SCALE, None, ALU.mult).then_inc(gate_setup, 1)
                    dve.wait_ge(gate_setup, 1)
                    nc.vector.tensor_copy(gq_hi16[:], gq_col[:, 1:2]).then_inc(gate_setup, 1)
                    dve.wait_ge(gate_setup, 2)
                    nc.vector.tensor_tensor(gq_col[:, 2:3], gq_col[:, 1:2], gq_hi16[:], ALU.subtract).then_inc(gate_setup, 1)
                    nc.vector.tensor_tensor(gq_col[:, 3:4], gq_hi16[:], masks[:, 0:1], ALU.mult).then_inc(gate_setup, 1)
                    dve.wait_ge(gate_setup, 4)
                    nc.vector.scalar_tensor_tensor(out=gq_col[:, 0:1], in0=gq_col[:, 2:3], scalar=masks[:, 1:2],
                                                   in1=gq_col[:, 3:4], op0=ALU.mult, op1=ALU.add).then_inc(gate_setup, 1)
                    dve.wait_ge(gate_setup, 5)
                    nc.vector.tensor_scalar(gate_w[:], masks[:, 2:2 + 2 * HD], gq_col[:, 0:1], None, ALU.mult)\
                        .then_inc(gate_setup, 1)

                def setup_mu():
                    dve.wait_ge(setup_t, 3)
                    nc.vector.tensor_scalar(mu_norm[:, 0:KC], b0[:, 0:KC], NORM_EPS * NORM_EPS, None, ALU.max)\
                        .then_inc(mu_squared, 1)

                def setup_mu_diag():
                    dve.wait_ge(setup_p, 3)
                    for k in range(KC):
                        nc.vector.tensor_scalar(disp_f32[:, k * P:(k + 1) * P], ident[:], mu_norm[:, KC + k:KC + k + 1],
                                                W_SCALE, ALU.mult, ALU.mult)\
                            .then_inc(mu_squared, 1)

                def split_mu():
                    dve.wait_ge(setup_t, 4)
                    nc.vector.scalar_tensor_tensor(out=mu_whole, in0=mu_whole, scalar=scale_col[:, 0:1],
                                                   in1=b0[:, 0:ES].unsqueeze(1).broadcast_to([P, KC, ES]),
                                                   op0=ALU.mult, op1=ALU.mult).then_inc(mu_split, 1)
                    dve.wait_ge(mu_split, 1)
                    nc.vector.tensor_copy(mu_hi[:], mu_whole).then_inc(mu_split, 1)
                    dve.wait_ge(mu_split, 2)
                    nc.vector.tensor_tensor(mu_lo[:], mu_whole, mu_hi[:], ALU.subtract).then_inc(mu_split, 1)


                def row_stats(i, c):
                    dve.wait_ge(x_loaded[c % 4], times(i, 16 * (c // 4 + 1), 32))
                    nc.vector.bn_stats(bn[:, c % 2, :], xs[:, c % 4, :]).then_inc(stats, 1)

                def row_moments(i, c):
                    dve.wait_ge(stats, per_slot(i, 3 * c + 1, 3))
                    hold_wait()
                    nc.vector.bn_aggr(mv[:, c % 4, :], bn[:, c % 2, :]).then_inc(stats, 1)

                def row_variance(i, c):
                    dve.wait_ge(stats, per_slot(i, 3 * c + 2, 3))
                    nc.vector.tensor_scalar(var_eps[:, c % 4:c % 4 + 1], mv[:, c % 4, 1:2], LN_EPS, None, ALU.add)\
                        .then_inc(stats, 1)

                def normalise(i, c):
                    dve.wait_ge(rstd_ready, per_slot(i, c + 1))
                    if c >= 2:
                        dve.wait_ge(zT_ready, per_slot(i, c - 1))
                    nc.vector.tensor_scalar(z[:, c % 2, :], xs[:, c % 4, :], mv[:, c % 4, 0:1], rstd[:, c % 4:c % 4 + 1],
                                            ALU.subtract, ALU.mult).then_inc(z_ready, 1)
                    if c >= 4:
                        dve.wait_ge(v_copied, per_slot(i, c - 3))
                    nc.vector.tensor_scalar(sd_v[:, c % 4:c % 4 + 1], var_eps[:, c % 4:c % 4 + 1], rstd[:, c % 4:c % 4 + 1],
                                            1.0 / W_SCALE, ALU.mult, ALU.mult).then_inc(sd_ready, 1)

                def split_zT(i, c):
                    dve.wait_ge(zT_copied, per_slot(i, c + 1))
                    nc.vector.tensor_tensor(zT_lo[:, c % 2, :, :], f0[:, 0:KC * P].rearrange("p (k n) -> p k n", n=P),
                                            zT_hi[:, c % 2, :, :], ALU.subtract).then_inc(zT_split, 1)

                def shift_values(i, c):
                    dve.wait_ge(v_copied, per_slot(i, c + 1))
                    nc.vector.scalar_tensor_tensor(out=v_raw[:, c % 4, :], in0=wv_sum[:], scalar=mv[:, c % 4, 0:1],
                                                   in1=v_raw[:, c % 4, :], op0=ALU.mult, op1=ALU.add).then_inc(v_shifted, 1)

                def copy_stacks(i, c):
                    b, j = c // TC, c % TC
                    if b >= 2 and j == 0:
                        dve.wait_ge(sc_ready, per_slot(i, 8 * TC * (b - 1), 8))
                        dve.wait_ge(gate_ready, per_batch(i, 2 * (b - 1), 2))
                    for side, bank in ((0, f0h), (1, f1h)):
                        dve.wait_ge(stk_ready, per_slot(i, 2 * c + side + 1, 2))
                        nc.vector.tensor_copy(stack[:, b % 2, side, :, j * P:(j + 1) * P],
                                              bank.rearrange("p (a n) -> p a n", n=P)).then_inc(stk_copied, 1)

                def add_qk_bias(i, c):
                    dve.wait_ge(qk_ready, per_slot(i, c + 1))
                    if c >= 4:
                        dve.wait_ge(squares_ready, per_slot(i, c - 3))
                        dve.wait_ge(kg_ready, per_slot(i, c - 3))
                    nc.vector.scalar_tensor_tensor(out=qk[:, c % 4, :], in0=f1[:, :], scalar=1.0 / W_SCALE, in1=qk_bias[:],
                                                   op0=ALU.mult, op1=ALU.add).then_inc(qk_copied, 1)

                def gate_products(i, c):
                    dve.wait_ge(qk_copied, c + 1)
                    if c >= 1:
                        dve.wait_ge(sums_ready, 2 * (c - 1) + 1)
                    nc.vector.tensor_tensor(sqg[:, 2 * D:3 * D], qk[:, c % 4, D:2 * D], gk_all[:], ALU.mult).then_inc(kg_ready, 1)

                def sum_squares(i, c):
                    dve.wait_ge(squares_ready, per_slot(i, c + 1))
                    dve.wait_ge(kg_ready, per_slot(i, c + 1))
                    if c >= 2:
                        dve.wait_ge(rn_ready, per_slot(i, c - 1))
                    nc.vector.tensor_reduce(sums[:, c % 2, :], heads(sqg[:, :]), AX_X, ALU.add).then_inc(sums_ready, 1)

                def clamp_squares(i, c):
                    dve.wait_ge(sums_ready, per_slot(i, 2 * c + 1, 2))
                    nc.vector.tensor_scalar(sums[:, c % 2, 0:2 * H], sums[:, c % 2, 0:2 * H], NORM_EPS * NORM_EPS, None, ALU.max)\
                        .then_inc(sums_ready, 1)

                def normalise_qk(i, c):
                    dve.wait_ge(rn_ready, per_slot(i, c + 1))
                    nc.vector.tensor_tensor(heads(qn[:, :]), heads(qk[:, c % 4, :]), over(rn[:, c % 2, :], HD), ALU.mult)\
                        .then_inc(norm_step, 1)
                    if c >= 2:
                        dve.wait_ge(v_gated, per_slot(i, c - 1))
                    nc.vector.tensor_tensor(gate_k[:, c % 2, :], sums[:, c % 2, 2 * H:3 * H], rn[:, c % 2, H:2 * H], ALU.mult)\
                        .then_inc(norm_step, 1)

                def split_qk(i, c):
                    if c >= 2:
                        dve.wait_ge(stk_ready, per_slot(i, 2 * (c - 2) + 2, 2))
                    dve.wait_ge(norm_step, per_slot(i, 2 * c + 2, 2))
                    nc.vector.tensor_copy(hl[:, c % 2, :, 0, :], heads(qn[:, :])).then_inc(hi_ready, 1)
                    dve.wait_ge(hi_ready, per_slot(i, 2 * c + 1, 2))
                    nc.vector.tensor_tensor(hl[:, c % 2, :, 3, :], heads(qn[:, :]), hl[:, c % 2, :, 0, :], ALU.subtract)\
                        .then_inc(hi_ready, 1)
                    dve.wait_ge(hi_ready, per_slot(i, 2 * c + 2, 2))
                    nc.vector.tensor_copy(hl[:, c % 2, 0:H, 1:3, :], hl[:, c % 2, 0:H, 0:4:3, :]).then_inc(hl_ready, 1)
                    nc.vector.tensor_copy(hl[:, c % 2, H:2 * H, 1, :], hl[:, c % 2, H:2 * H, 3, :]).then_inc(hl_ready, 1)
                    nc.vector.tensor_copy(hl[:, c % 2, H:2 * H, 2, :], hl[:, c % 2, H:2 * H, 0, :]).then_inc(hl_ready, 1)

                def gate_values(i, c):
                    b, j = c // TC, c % TC
                    dve.wait_ge(norm_step, per_slot(i, 2 * c + 2, 2))
                    dve.wait_ge(v_shifted, per_slot(i, c + 1))
                    if c == 0:
                        dve.wait_ge(setup_p, 2)
                    if b >= 2 and j == 0:
                        dve.wait_ge(pv_done, per_slot(i, 4 * TC * (b - 1), 4))
                    nc.vector.tensor_tensor(vpad[:, b % 2, j, :, :].rearrange("p a (o d) -> p a o d", d=HD)[:, :, 0:3:2, :],
                                            v_raw[:, c % 4, :].rearrange("p (a o d) -> p a o d", o=2, d=HD),
                                            over(gate_k[:, c % 2, :].rearrange("p (a o) -> p a o", o=2), HD), ALU.mult)\
                        .then_inc(v_gated, 1)

                def gate_sums(i, b, half):
                    dve.wait_ge(pv_done, per_batch(i, 4 * (TC * b + 2 * half + 2), 4 * TC))
                    dve.wait_ge(gate_copied, per_batch(i, 2 * b + half + 1, 2))
                    if b >= 2:
                        dve.wait_ge(wo_ready, per_batch(i, TC * (b - 1), TC))
                    nc.vector.tensor_tensor(coll[:, b % 2, half, :], coll_ps[:, :], gate_q[:, half, :], ALU.mult)\
                        .then_inc(coll_done, 1)

                def residual(i, c, step):
                    if step == 0:
                        dve.wait_ge(wo_ready, per_slot(i, c + 1))
                        dve.wait_ge(xb_ready, per_slot(i, c + 1))
                        nc.vector.tensor_tensor(y[:, c % 2, :], wo_bank(c), xr[:, c % 4, :], ALU.add).then_inc(y_step, 1)
                    if step == 1:
                        dve.wait_ge(y_step, per_slot(i, 4 * c + 1, 4))
                        nc.vector.bn_stats(ybn[:, c % 2, :], y[:, c % 2, :]).then_inc(y_step, 1)
                    if step == 2:
                        dve.wait_ge(y_step, per_slot(i, 4 * c + 2, 4))
                        hold_wait()
                        nc.vector.bn_aggr(ymv[:, c % 2, :], ybn[:, c % 2, :]).then_inc(y_step, 1)
                    if step == 3:
                        dve.wait_ge(y_step, per_slot(i, 4 * c + 3, 4))
                        nc.vector.tensor_scalar(yvar[:, c % 2:c % 2 + 1], ymv[:, c % 2, 1:2], LN_EPS, None, ALU.add)\
                            .then_inc(y_step, 1)

                def first_norm(i, c):
                    dve.wait_ge(yrstd_ready, per_slot(i, c + 1))
                    if c >= 2:
                        dve.wait_ge(x1_stored[c % 2], times(i, 16 * (c // 2), 16 * LOOP_SLOTS // 2))
                    rs = yrstd[:, c % 2:c % 2 + 1]
                    nc.vector.tensor_scalar(x1[:, c % 2, :], y[:, c % 2, :], ymv[:, c % 2, 0:1], rs, ALU.subtract, ALU.mult)\
                        .then_inc(x1_ready, 1)
                    nc.vector.tensor_scalar(v1[:, c % 2, 0:1], ymv[:, c % 2, 1:2], rs, rs, ALU.mult, ALU.mult).then_inc(x1_ready, 1)

                def x1_variance(i, c):
                    dve.wait_ge(x1_ready, per_slot(i, 3 * c + 2, 3))
                    nc.vector.tensor_scalar(v1[:, c % 2, 1:2], v1[:, c % 2, 0:1], LN_EPS, None, ALU.add).then_inc(x1_ready, 1)

                def second_norm(i, c, step):
                    b, j = c // TC, c % TC
                    if step == 0:
                        dve.wait_ge(r1_ready, per_slot(i, c + 1))
                        nc.vector.scalar_tensor_tensor(out=xg[:], in0=x1[:, c % 2, :], scalar=r1[:, c % 2:c % 2 + 1],
                                                       in1=gamma_all[:], op0=ALU.mult, op1=ALU.mult).then_inc(xn_step, 1)
                    if step == 1:
                        dve.wait_ge(xn_step, per_slot(i, 4 * c + 1, 4))
                        nc.vector.tensor_tensor(xn[:], xg[:], beta_all[:], ALU.add).then_inc(xn_step, 1)
                    if step == 2:
                        dve.wait_ge(xn_step, per_slot(i, 4 * c + 2, 4))
                        nc.vector.tensor_tensor_reduce(xg[:], xn[:], xn[:], 1.0, 0.0, ALU.mult, ALU.add,
                                                       xss[:, c % 2, 0:1]).then_inc(xn_step, 1)
                    if step == 3:
                        dve.wait_ge(xn_step, per_slot(i, 4 * c + 3, 4))
                        nc.vector.tensor_scalar(xss[:, c % 2, 1:2], xss[:, c % 2, 0:1], NORM_EPS * NORM_EPS,
                                                W_SCALE * W_SCALE, ALU.max, ALU.mult).then_inc(xn_step, 1)

                def split_xn(i, c, part):
                    b, j = c // TC, c % TC
                    if part == 0:
                        dve.wait_ge(xn_step, per_slot(i, 4 * c + 2, 4))
                        if b >= 2 and j == 0:
                            dve.wait_ge(slot_ready, per_batch(i, b - 1))
                        nc.vector.tensor_copy(xn_parts[:, b % 2, 0, j, :], xn[:]).then_inc(xn_split, 1)
                    else:
                        dve.wait_ge(xn_split, per_slot(i, 2 * c + 1, 2))
                        nc.vector.tensor_tensor(xn_parts[:, b % 2, 1, j, :], xn[:], xn_parts[:, b % 2, 0, j, :], ALU.subtract)\
                            .then_inc(xn_split, 1)

                def split_dispatch(i, b, half):
                    bank = b0 if half == 1 else f1
                    dve.wait_ge(disp_copied, per_batch(i, 2 * b + half + 1, 2))
                    hi, lo = disp[:, 0, 2 * half:2 * half + 2, :], disp[:, 1, 2 * half:2 * half + 2, :]
                    nc.vector.tensor_tensor(lo, bank[:, :].rearrange("p (t n) -> p t n", t=2), hi, ALU.subtract).then_inc(disp_split, 1)

                def scale_logits(i, c):
                    b, t = c // TC, c % TC
                    dve.wait_ge(log_ready, per_slot(i, c + 1))
                    dve.wait_ge(xrn_ready, per_slot(i, c + 1))
                    nc.vector.tensor_reduce(rmax[:, b % 2, t, 0:1], logits_bank(c), AX_X, ALU.max).then_inc(log_step, 1)
                    if b >= 2 and t in (0, 2):
                        dve.wait_ge(combT_ready, per_batch(i, 2 * (b - 2) + t // 2 + 1, 2))
                    nc.vector.tensor_scalar(logit[:, b % 2, t, :], logits_bank(c), xrn[:, c % 2:c % 2 + 1], None, ALU.mult)\
                        .then_inc(log_step, 1)
                    dve.wait_ge(log_step, per_slot(i, 3 * c + 1, 3))
                    nc.vector.tensor_scalar(rmax[:, b % 2, t, 1:2], rmax[:, b % 2, t, 0:1], xrn[:, c % 2:c % 2 + 1], -1.0,
                                            ALU.mult, ALU.mult).then_inc(log_step, 1)

                def copy_combine(i, b):
                    dve.wait_ge(combT_ready, per_batch(i, 2 * b + 2, 2))
                    if b >= 1:
                        dve.wait_ge(comb_stored[1], per_batch(i, 16 * b, 16))
                    nc.vector.tensor_copy(combT[:, 1, :], b0[:, :]).then_inc(combT_copied, 1)

                def column_max(i, b):
                    dve.wait_ge(logT_copied, per_batch(i, TC * (b + 1), TC))
                    if b >= 1:
                        dve.wait_ge(soft_exp, per_batch(i, 6 * b, 6))
                    nc.vector.tensor_reduce(cmax[:], logitT[:, b % 2, :, :], AX_X, ALU.max).then_inc(soft_max, 1)
                    dve.wait_ge(soft_max, per_batch(i, 2 * b + 1, 2))
                    nc.vector.tensor_scalar(cmax[:], cmax[:], -1.0, None, ALU.mult).then_inc(soft_max, 1)

                def normalise_dispatch(i, b):
                    dve.wait_ge(soft_exp, per_batch(i, 6 * (b + 1), 6))
                    nc.vector.reciprocal(esum[:, b % 2, :], esum[:, b % 2, :]).then_inc(soft_post, 1)
                    dve.wait_ge(soft_post, per_batch(i, 4 * b + 1, 4))
                    for k in range(KC):
                        nc.vector.tensor_scalar(logitT[:, b % 2, k, :], logitT[:, b % 2, k, :], esum[:, b % 2, k:k + 1],
                                                W_SCALE, ALU.mult, ALU.mult).then_inc(soft_post, 1)
                    nc.vector.reciprocal(crec[:, bass.ds(per_batch(i, TC * b, TC), TC)], csum[:, b % 2, :]).then_inc(soft_post, 1)

                def slot(i, s):
                    b, j = s // TC, s % TC
                    if j == 3 and batch_ok(b - 3):
                        copy_combine(i, b - 3)
                    if chunk_ok(s + 7):
                        split_zT(i, s + 7)
                    if chunk_ok(s + 8):
                        row_stats(i, s + 8)
                    if chunk_ok(s + 6):
                        add_qk_bias(i, s + 6)
                    if j == 0 and batch_ok(b - 3):
                        split_dispatch(i, b - 3, 1)
                    if chunk_ok(s + 8):
                        row_moments(i, s + 8)
                    if chunk_ok(s + 6):
                        shift_values(i, s + 6)
                    if 0 <= s + 6 < VECTOR_KG:
                        gate_products(i, s + 6)
                    if chunk_ok(s + 8):
                        row_variance(i, s + 8)
                    if chunk_ok(s - 5):
                        first_norm(i, s - 5)
                    if chunk_ok(s - 5):
                        x1_variance(i, s - 5)
                    if s == -8:
                        normalise(i, 0)
                        setup()
                    if s == -6:
                        setup_gate()
                        setup_mu()
                    if chunk_ok(s + 4):
                        copy_stacks(i, s + 4)
                    if j == 2 and batch_ok(b):
                        gate_sums(i, b, 0)
                    if j == 0 and batch_ok(b - 1):
                        gate_sums(i, b - 1, 1)
                    if j == 3 and batch_ok(b - 2):
                        normalise_dispatch(i, b - 2)
                    if chunk_ok(s + 4):
                        gate_values(i, s + 4)
                    if chunk_ok(s + 8) and s > -8:
                        normalise(i, s + 8)
                    if chunk_ok(s + 6):
                        sum_squares(i, s + 6)
                    if chunk_ok(s - 6):
                        scale_logits(i, s - 6)
                    if chunk_ok(s + 6):
                        clamp_squares(i, s + 6)
                    if j == 3 and batch_ok(b - 2):
                        split_dispatch(i, b - 2, 0)
                    if j == 2 and batch_ok(b - 2):
                        column_max(i, b - 2)
                    if chunk_ok(s + 5):
                        normalise_qk(i, s + 5)
                    if chunk_ok(s - 5):
                        second_norm(i, s - 5, 0)
                    if chunk_ok(s + 5):
                        split_qk(i, s + 5)
                    for step in range(1, 4):
                        if chunk_ok(s - 4):
                            residual(i, s - 4, step - 1)
                        if chunk_ok(s - 5):
                            second_norm(i, s - 5, step)
                    if chunk_ok(s - 5):
                        split_xn(i, s - 5, 0)
                    if chunk_ok(s - 4):
                        residual(i, s - 4, 3)
                    if chunk_ok(s - 5):
                        split_xn(i, s - 5, 1)
                    if s == -7:
                        square_mu()
                    if s == -4:
                        setup_mu_diag()
                    if s == -3:
                        split_mu()

                slots(dve, slot, FIRST, LAST)


        def batches(eng, batch):
            for b in range(2 * RING):
                batch(None, b)
            with eng.Fori(0, B // RING - 2) as i:
                for b in range(2 * RING, 3 * RING):
                    batch(i, b)

        h_ps = [f0, f1]
        out_ps = [[score_ps[0][:, 0, :], score_ps[0][:, 1, :], score_ps[1][:, 0, :], score_ps[1][:, 1, :]],
                  [coll_ps[:, :], f0[:, :], f1[:, :], b0[:, :]]]
        so_ps = [score_ps[0][:, 0, :], score_ps[0][:, 1, :], score_ps[1][:, 0, :], score_ps[1][:, 1, :]]

        with nc.Block() as block:

            @block.sync
            def _(sp):
                for k in range(2):
                    sp.wait_ge(x1_stored[k], 16 * NCH // 2)
                    sp.wait_ge(comb_stored[k], 16 * B)

                def load_slots(i, b):
                    if b >= RING:
                        sp.wait_ge(y2_step, per_ring(i, TC * (b - RING + 1), TC))
                    sp.dma_start(so_sb[:, b % RING, :, :], slot_dram[bass.ds(per_ring(i, b), 1), :, :]
                                 .rearrange("b (k p) d -> (b p) k d", p=P)).then_inc(so_loaded[b % RING], 16)

                load_batch(sp, None, 2)
                load_batch(sp, None, 3)
                for e in range(E):
                    sp.wait_ge(so_done, e + 1)
                    for m in range(M):
                        sp.dma_start(slot_dram[m * (P // S):(m + 1) * (P // S), e * S:(e + 1) * S, :],
                                     slot_out[:, e % 4, m, :]).then_inc(so_stored[e % 4], 16)
                    if e == RING:
                        load_batch(sp, None, RING)
                for k in range(4):
                    sp.wait_ge(so_stored[k], 16 * M * E // 4)
                load_slots(None, 0)
                for b in range(1, RING):
                    load_slots(None, b)
                    load_batch(sp, None, RING + b)

                for b in range(RING, 2 * RING):
                    load_slots(None, b)
                with sp.Fori(0, B // RING - 2) as i:
                    for b in range(2 * RING, 3 * RING):
                        load_batch(sp, i, b)
                        load_slots(i, b)

            @block.tensor
            def _(pe):
                def hidden_layer(a):
                    if a >= 2:
                        pe.wait_ge(h_done, a - 1)
                    for k in range(KC):
                        for i in range(2):
                            last = nc.tensor.matmul(h_ps[a % 2][HF * i:HF * i + HF, 0:B * S], w1s[:, k, 2 * a + i, :],
                                                    slotT[:, k, 2 * a + i, :, :].rearrange("p b s -> p (b s)"),
                                                    start=(k == 0), stop=(k == KC - 1), tile_position=(0, HF * i))
                    last.then_inc(h_ready, 1)

                def output_layer(a):
                    pe.wait_ge(h_done, a + 1)
                    for i in range(2):
                        e = 2 * a + i
                        rows = slice(HF * i, HF * i + HF)
                        if e >= 4:
                            pe.wait_ge(so_done, e - 3)
                        for m in range(M):
                            last = nc.tensor.matmul(so_ps[e % 4][:, m * D:(m + 1) * D], hidden[rows, a, m * P:(m + 1) * P],
                                                    w2s[rows, a, :], start=True, stop=True, tile_position=(HF * i, 0))
                        last.then_inc(so_ready, 1)

                pe.wait_ge(expert_loaded, 16 * (KC + 4))
                for a in range(EP):
                    hidden_layer(a)
                    if a >= 1:
                        output_layer(a - 1)
                output_layer(EP - 1)
                pe.wait_ge(so_done, E)

                def combine(i, b):
                    batch_loaded(pe, i, b)
                    pe.wait_ge(so_loaded[b % RING], times(i, 16 * (b // RING + 1), 16))
                    for t in range(TC):
                        if b >= 2:
                            pe.wait_ge(y2_step, per_ring(i, TC * (b - 2) + t + 1, TC))
                        for k in range(KC):
                            last = nc.tensor.matmul(out_ps[b % 2][t][:, 0:D], comb_in(b)[:, k, t * P:(t + 1) * P],
                                                    so_sb[:, b % RING, k, :],
                                                    start=(k == 0), stop=(k == KC - 1))
                        last.then_inc(comb_ready_ps, 1)

                batches(pe, combine)

            @block.scalar
            def _(act):
                act.wait_ge(expert_loaded, 16 * (KC + 4))
                for a in range(EP):
                    act.wait_ge(h_ready, a + 1)
                    nc.scalar.activation(hidden[:, a, :], h_ps[a % 2][:, 0:B * S], ACT.Gelu, bias=b1_col[:, a:a + 1])\
                        .then_inc(h_done, 1)

                def normalise_out(i, b):
                    act.wait_ge(ostat_ready, per_ring(i, 3 * (b + 1), 3))
                    if b >= 2:
                        act.wait_ge(out_stored[b % 2], times(i, 16 * (b // 2), 16 * RING // 2))
                    for t in range(TC):
                        nc.scalar.activation(out_sb[:, b % 2, t, :], y2[:, b % 2, t, :], ACT.Identity,
                                             scale=orstd[:, b % 2, t:t + 1], bias=oshift[:, b % 2, 1, t:t + 1]).then_inc(out_ready, 1)
                    act.wait_ge(out_ready, per_ring(i, TC * (b + 1), TC))
                    act.dma_start(out_rows[bass.ds(per_ring(i, b * T, T), T), :].rearrange("(t p) d -> p t d", p=P),
                                  out_sb[:, b % 2, :, :]).then_inc(out_stored[b % 2], 16)

                batches(act, normalise_out)
                for k in range(2):
                    act.wait_ge(out_stored[k], 16 * B // 2)

            @block.gpsimd
            def _(pool):
                def out_stats(i, b):
                    pool.wait_ge(oagg, per_ring(i, b + 1))
                    if b >= 2:
                        pool.wait_ge(out_ready, per_ring(i, TC * (b - 1), TC))
                    nc.gpsimd.tensor_tensor(orstd[:, b % 2, :], ovar[:, b % 2, :], minus_half[:, 0:TC], ALU.pow).then_inc(ostat_ready, 1)
                    nc.gpsimd.tensor_scalar(oshift[:, b % 2, 0, :], omv[:, b % 2, :, 0], -1.0, None, ALU.mult).then_inc(ostat_ready, 1)
                    pool.wait_ge(ostat_ready, per_ring(i, 3 * b + 2, 3))
                    nc.gpsimd.tensor_tensor(oshift[:, b % 2, 1, :], oshift[:, b % 2, 0, :], orstd[:, b % 2, :], ALU.mult)\
                        .then_inc(ostat_ready, 1)

                batches(pool, out_stats)

            @block.vector
            def _(dve):
                dve.wait_ge(b2_loaded, 16)
                for e in range(E):
                    dve.wait_ge(so_ready, e + 1)
                    if e >= 4:
                        dve.wait_ge(so_stored[e % 4], 16 * M * (e // 4))
                    nc.vector.tensor_tensor(slot_out[:, e % 4, :, :], so_ps[e % 4].rearrange("p (m d) -> p m d", m=M),
                                            b2_all[:, e, :].unsqueeze(1).broadcast_to([P, M, D]), ALU.add).then_inc(so_done, 1)

                def residual_out(i, b):
                    if b >= 2:
                        dve.wait_ge(out_ready, per_ring(i, TC * (b - 1), TC))
                    nc.vector.tensor_copy(crec4[:, b % 2, :], crec[:, bass.ds(per_ring(i, TC * b, TC), TC)]).then_inc(crec_copied, 1)
                    dve.wait_ge(crec_copied, per_ring(i, b + 1))
                    batch_loaded(dve, i, b)
                    for t in range(TC):
                        dve.wait_ge(comb_ready_ps, per_ring(i, TC * b + t + 1, TC))
                        nc.vector.scalar_tensor_tensor(out=y2[:, b % 2, t, :], in0=out_ps[b % 2][t][:, 0:D], scalar=crec4[:, b % 2, t:t + 1],
                                                       in1=x1_in(b)[:, t, :], op0=ALU.mult, op1=ALU.add).then_inc(y2_step, 1)
                    for t in range(TC):
                        dve.wait_ge(y2_step, per_ring(i, TC * b + t + 1, TC))
                        nc.vector.bn_stats(obn[:, b % 2, t, :], y2[:, b % 2, t, :]).then_inc(obn_ready, 1)
                    dve.wait_ge(obn_ready, per_ring(i, TC * (b + 1), TC))
                    hold_wait()
                    for t in range(TC):
                        nc.vector.bn_aggr(omv[:, b % 2, t, :], obn[:, b % 2, t, :]).then_inc(omv_ready, 1)
                    dve.wait_ge(omv_ready, per_ring(i, TC * (b + 1), TC))
                    nc.vector.tensor_scalar(ovar[:, b % 2, :], omv[:, b % 2, :, 1], LN_EPS, None, ALU.add).then_inc(oagg, 1)

                batches(dve, residual_out)


_INS = ['L0_attn_x', 'L0_attn_Wq', 'L0_attn_Wk', 'L0_attn_Wv', 'L0_attn_gq', 'L0_attn_gk', 'L0_attn_Wo', 'L0_attn_bo',
        'L0_attn_ln_w', 'L0_attn_ln_b', 'L0_ffn_ln_gamma', 'L0_ffn_ln_beta', 'L0_ffn_mu', 'L0_ffn_scale',
        'L0_ffn_w1', 'L0_ffn_b1', 'L0_ffn_w2', 'L0_ffn_b2']


def kernel(**inputs):
    import numpy as np
    import concourse.bacc as bacc
    from concourse import mybir as mb
    from concourse.bass_utils import run_bass_kernel_spmd

    nc = bacc.Bacc("TRN2", target_bir_lowering=False, num_devices=1, dynamic_dma_scratch_size=1024)
    arrays, args = {}, []

    def give(name, a):
        arrays[f"in_{name}_dram"] = a
        args.append(nc.dram_tensor(f"in_{name}_dram", a.shape, mb.dt.from_np(a.dtype), kind="ExternalInput").ap())

    for name in _INS:
        give(name, np.ascontiguousarray(inputs[name]))
    row, head_rows, hd = np.arange(128), 64, 16
    low = (row % head_rows) // hd % 2
    block = (row[:, None] // head_rows) == (np.arange(2 * hd)[None, :] // hd)
    give("consts", np.concatenate([np.eye(128), (low == 0)[:, None], (low == 1)[:, None], block], axis=1).astype(np.float32))
    shape = inputs['L0_attn_x'].shape
    args.append(nc.dram_tensor("out_0_dram", shape, mb.dt.float32, kind="ExternalOutput").ap())
    seq_block_kernel(nc, *args)
    r = run_bass_kernel_spmd(nc, [arrays], core_ids=[0])
    return r.results[0]["out_0_dram"]
```
